# Optimizing a Trainium2 kernel written in Bass

```python
import numpy as np
import jax
import jax.numpy as jnp

def _softmax(x, axis=-1):
    return jax.nn.softmax(x, axis=axis)

def _gelu(x):
    return jax.nn.gelu(x, approximate=True)

def _silu(x):
    return jax.nn.silu(x)

def _sigmoid(x):
    return jax.nn.sigmoid(x)

def _layernorm(x, axis=-1, eps=1e-05):
    m = jnp.mean(x, axis=axis, keepdims=True)
    v = jnp.var(x, axis=axis, keepdims=True)
    return (x - m) / jnp.sqrt(v + eps)

def _scatter_add(tgt, idx, src, axis=0):
    return tgt.at[idx].add(src)

def _segment_sum(src, seg, n):
    return jax.ops.segment_sum(src, seg, n)
kernel_name = 'mk_xattn_ffn_d4_seqx_r4_7f59fb'

def setup_inputs(seed: int=0):
    np.random.seed(seed)
    _w = jnp.asarray

    def _rec_inputs():
        import jax
        import jax.numpy as jnp
        _rk = jax.random.key(seed)
        x = 4.136e-05 + 0.9999 * jax.random.normal(jax.random.fold_in(_rk, 1), (4, 512, 512), jnp.float32)
        _lenS = 512 - jax.random.randint(jax.random.fold_in(_rk, 7), (4,), 0, max(1, 512 // 4) + 1, jnp.int32)
        _lenS2 = 512 - jax.random.randint(jax.random.fold_in(_rk, 8), (4,), 0, max(1, 512 // 4) + 1, jnp.int32)
        _ctx_1024P = jax.random.normal(jax.random.fold_in(_rk, 11), (4, 16, 256), jnp.float32)
        _ctx_1024c = jax.random.dirichlet(jax.random.fold_in(_rk, 511), 0.3 * jnp.ones((16,), jnp.float32), (4, 512))
        _ctx_1024t = jnp.einsum('bsk,bkd->bsd', _ctx_1024c, _ctx_1024P)
        _ctx_1024t = _ctx_1024t * jax.lax.rsqrt(jnp.mean(jnp.square(_ctx_1024t)) + 1e-12) * 0.953939
        ctx_1024 = -0.000292821 + 1.00034 * (_ctx_1024t + 0.3 * jax.random.normal(jax.random.fold_in(_rk, 611), (4, 512, 256), jnp.float32))
        fside_BxSx2_0 = jax.random.uniform(jax.random.fold_in(_rk, 12), (4, 512, 2), jnp.float32, 0.0, 0.999707)
        return (x, ctx_1024, fside_BxSx2_0)
    x, ctx_1024, fside_BxSx2_0 = _rec_inputs()

    def _L0_xattn_setup():
        import jax, jax.numpy as jnp
        import numpy as np
        import math
        B, L, DM = (2, 512, 256)
        DS, DC, EXP = (16, 4, 2)
        DI = EXP * DM
        DR = math.ceil(DM / 16)
        DT_MIN, DT_MAX, DT_FLOOR = (0.001, 0.1, 0.0001)

        def _ssm_forward(hidden_states, z, in_proj_w, conv_w, conv_b, x_proj_w, dt_proj_w, dt_proj_b, A_log, D):
            b = hidden_states.shape[0]
            x = jnp.einsum('ed,bld->bel', in_proj_w, hidden_states)
            xp = jnp.pad(x, ((0, 0), (0, 0), (DC - 1, 0)))
            xc = jax.lax.conv_general_dilated(xp, conv_w[:, None, :], window_strides=(1,), padding='VALID', dimension_numbers=('NCH', 'OIH', 'NCH'), feature_group_count=DI)
            u = jax.nn.silu(xc + conv_b[None, :, None])
            x_dbl = jnp.einsum('ke,bel->bkl', x_proj_w, u)
            dt_lo = x_dbl[:, :DR]
            Bm = x_dbl[:, DR:DR + DS]
            Cm = x_dbl[:, DR + DS:]
            delta = jax.nn.softplus(jnp.einsum('er,brl->bel', dt_proj_w, dt_lo) + dt_proj_b[None, :, None])
            A = -jnp.exp(A_log)

            def step(state, xs):
                d_t, B_t, C_t, u_t = xs
                dA = jnp.exp(d_t[..., None] * A)
                state = state * dA + (d_t * u_t)[..., None] * B_t[:, None, :]
                y_t = jnp.einsum('ben,bn->be', state, C_t)
                return (state, y_t)
            xs = (jnp.moveaxis(delta, -1, 0), jnp.moveaxis(Bm, -1, 0), jnp.moveaxis(Cm, -1, 0), jnp.moveaxis(u, -1, 0))
            state0 = jnp.zeros((b, DI, DS), delta.dtype)
            _, ys = jax.lax.scan(step, state0, xs)
            y = jnp.moveaxis(ys, 0, -1)
            y = y + D[None, :, None] * u
            y = y * jax.nn.silu(z)
            return jnp.swapaxes(y, 1, 2)
        key = jax.random.key(seed)
        ks = jax.random.split(key, 8)
        hidden_states = jax.random.normal(ks[0], (B, L, DM), jnp.float32)
        z = jax.random.normal(ks[1], (B, DI, L), jnp.float32)
        in_proj_w = jax.random.normal(ks[2], (DI, DM), jnp.float32) * DM ** (-0.5)
        conv_w = jax.random.normal(ks[3], (DI, DC), jnp.float32) * DC ** (-0.5)
        conv_b = jnp.zeros((DI,), jnp.float32)
        x_proj_w = jax.random.normal(ks[4], (DR + 2 * DS, DI), jnp.float32) * DI ** (-0.5)
        dt_std = DR ** (-0.5)
        dt_proj_w = jax.random.uniform(ks[5], (DI, DR), jnp.float32, -dt_std, dt_std)
        dt = jnp.exp(jax.random.uniform(ks[6], (DI,), jnp.float32) * (math.log(DT_MAX) - math.log(DT_MIN)) + math.log(DT_MIN))
        dt = jnp.clip(dt, DT_FLOOR)
        dt_proj_b = dt + jnp.log(-jnp.expm1(-dt))
        A_log = jnp.log(jnp.broadcast_to(jnp.arange(1, DS + 1, dtype=jnp.float32), (DI, DS)))
        D = jnp.ones((DI,), jnp.float32)
        return dict(hidden_states=hidden_states, z=z, in_proj_w=in_proj_w, conv_w=conv_w, conv_b=conv_b, x_proj_w=x_proj_w, dt_proj_w=dt_proj_w, dt_proj_b=dt_proj_b, A_log=A_log, D=D)
    _L0_xattn_all = _L0_xattn_setup()
    _L0_xattn_in = {k: v for k, v in _L0_xattn_all.items() if k in ('in_proj_w', 'conv_w', 'conv_b', 'x_proj_w', 'dt_proj_w', 'dt_proj_b', 'A_log', 'D')}
    del _L0_xattn_all

    def _L0_ffn_setup():
        import jax, jax.numpy as jnp
        import numpy as np
        BLOCK_SIZE = 32
        HIDDEN_SIZE = 512
        MLP_DIM = 4096
        NVFP4_LUT = jnp.array([0.0, 0.5, 1.0, 1.5, 2.0, 3.0, 4.0, 6.0, 0.0, -0.5, -1.0, -1.5, -2.0, -3.0, -4.0, -6.0], dtype=jnp.float32)

        def dequant_nvfp4(W_packed, scales, block=BLOCK_SIZE):
            N = W_packed.shape[0]
            low = W_packed & 15
            high = W_packed >> 4 & 15
            idx = jnp.stack([low, high], axis=-1).reshape(N, -1)
            vals = NVFP4_LUT[idx]
            K = vals.shape[1]
            vals = vals.reshape(N, K // block, block) * scales[:, :, None]
            return vals.reshape(N, K)
        key = jax.random.key(seed)
        ks = jax.random.split(key, 7)
        x = jax.random.normal(ks[0], (4, 32, HIDDEN_SIZE), dtype=jnp.float32)
        gate_W_packed = jax.random.randint(ks[1], (MLP_DIM, HIDDEN_SIZE // 2), 0, 64, dtype=jnp.int32)
        gate_scales = jax.random.uniform(ks[2], (MLP_DIM, HIDDEN_SIZE // BLOCK_SIZE), dtype=jnp.float32) * 0.1 + 0.001
        up_W_packed = jax.random.randint(ks[3], (MLP_DIM, HIDDEN_SIZE // 2), 0, 64, dtype=jnp.int32)
        up_scales = jax.random.uniform(ks[4], (MLP_DIM, HIDDEN_SIZE // BLOCK_SIZE), dtype=jnp.float32) * 0.1 + 0.001
        down_W_packed = jax.random.randint(ks[5], (HIDDEN_SIZE, MLP_DIM // 2), 0, 64, dtype=jnp.int32)
        down_scales = jax.random.uniform(ks[6], (HIDDEN_SIZE, MLP_DIM // BLOCK_SIZE), dtype=jnp.float32) * 0.1 + 0.001
        return {'x': x, 'gate_W_packed': gate_W_packed, 'gate_scales': gate_scales, 'up_W_packed': up_W_packed, 'up_scales': up_scales, 'down_W_packed': down_W_packed, 'down_scales': down_scales}
    _L0_ffn_all = _L0_ffn_setup()
    _L0_ffn_in = {k: v for k, v in _L0_ffn_all.items() if k in ('gate_W_packed', 'gate_scales', 'up_W_packed', 'up_scales', 'down_W_packed', 'down_scales')}
    del _L0_ffn_all

    def _L1_xattn_setup():
        import jax, jax.numpy as jnp
        import numpy as np
        DIM = 512
        CTX_DIM = 256
        N_HEADS = 32
        HEAD_DIM = DIM // N_HEADS
        POS_DIM = 2
        B, N, CTXN = (2, 512, 512)
        ROPE_BASE = 10000.0

        def apply_axial_rope(x, pos):
            b, n, h, d = x.shape
            p = pos.shape[-1]
            dpa = d // p
            half = dpa // 2
            freqs = ROPE_BASE ** (-jnp.arange(half, dtype=x.dtype) / half)
            ang = pos[..., :, None] * freqs
            cos = jnp.cos(ang)[:, :, None, :, :]
            sin = jnp.sin(ang)[:, :, None, :, :]
            xr = x.reshape(b, n, h, p, half, 2)
            x1, x2 = (xr[..., 0], xr[..., 1])
            out = jnp.stack([x1 * cos - x2 * sin, x1 * sin + x2 * cos], axis=-1)
            return out.reshape(b, n, h, d)
        key = jax.random.key(seed)
        ks = jax.random.split(key, 8)
        x = jax.random.normal(ks[0], (B, N, DIM), jnp.float32)
        ctx = jax.random.normal(ks[1], (B, CTXN, CTX_DIM), jnp.float32)
        pos_map = jax.random.uniform(ks[2], (B, N, POS_DIM), jnp.float32)
        ctx_pos_map = jax.random.uniform(ks[3], (B, CTXN, POS_DIM), jnp.float32)
        Wq = jax.random.normal(ks[4], (DIM, DIM), jnp.float32) / np.sqrt(DIM)
        Wkv = jax.random.normal(ks[5], (CTX_DIM, 2 * DIM), jnp.float32) / np.sqrt(CTX_DIM)
        Wout = jax.random.normal(ks[6], (DIM, DIM), jnp.float32) / np.sqrt(DIM)
        bout = jnp.zeros((DIM,), jnp.float32)
        return {'x': x, 'ctx': ctx, 'pos_map': pos_map, 'ctx_pos_map': ctx_pos_map, 'Wq': Wq, 'Wkv': Wkv, 'Wout': Wout, 'bout': bout}
    _L1_xattn_all = _L1_xattn_setup()
    _L1_xattn_in = {k: v for k, v in _L1_xattn_all.items() if k in ('Wq', 'Wkv', 'Wout', 'bout')}
    del _L1_xattn_all

    def _L1_ffn_setup():
        import jax, jax.numpy as jnp
        import numpy as np
        EPS = 1e-05

        def _quant_weight(w):
            scale = jnp.mean(jnp.abs(w)) + EPS
            wq = jnp.clip(jnp.round(w / scale), -1.0, 1.0) * scale
            return w + jax.lax.stop_gradient(wq - w)

        def _quant_act(x):
            scale = jnp.maximum(jnp.max(jnp.abs(x), axis=-1, keepdims=True), EPS) / 127.0
            xq = jnp.clip(jnp.round(x / scale), -128.0, 127.0) * scale
            return x + jax.lax.stop_gradient(xq - x)

        def bitlinear(x, w):
            return jnp.einsum('bsi,oi->bso', _quant_act(x), _quant_weight(w))
        key = jax.random.key(seed)
        k1, k2, k3, k4 = jax.random.split(key, 4)
        d_model, d_ff = (512, 2048)
        B, S = (4, 512)
        x = jax.random.normal(k1, (B, S, d_model), dtype=jnp.float32)
        w_gate = jax.random.normal(k2, (d_ff, d_model), dtype=jnp.float32) * 0.02
        w_up = jax.random.normal(k3, (d_ff, d_model), dtype=jnp.float32) * 0.02
        w_down = jax.random.normal(k4, (d_model, d_ff), dtype=jnp.float32) * 0.02
        return {'x': x, 'w_gate': w_gate, 'w_up': w_up, 'w_down': w_down}
    _L1_ffn_all = _L1_ffn_setup()
    _L1_ffn_in = {k: v for k, v in _L1_ffn_all.items() if k in ('w_gate', 'w_up', 'w_down')}
    del _L1_ffn_all

    def _L2_xattn_setup():
        import jax, jax.numpy as jnp
        import numpy as np
        key = jax.random.key(seed)
        ks = jax.random.split(key, 6)
        B, L, N, C, D = (8, 128, 512, 256, 128)
        return {'teacher_logits': jax.random.normal(ks[0], (B, L, N), dtype=jnp.float32), 'teacher_features': jax.random.normal(ks[1], (B, N, C), dtype=jnp.float32), 'Wq': jax.random.normal(ks[2], (D, C), dtype=jnp.float32) * (1.0 / np.sqrt(C)), 'bq': jnp.zeros((D,), dtype=jnp.float32), 'Wk': jax.random.normal(ks[3], (D, C), dtype=jnp.float32) * (1.0 / np.sqrt(C)), 'bk': jnp.zeros((D,), dtype=jnp.float32)}
    _L2_xattn_all = _L2_xattn_setup()
    _L2_xattn_in = {k: v for k, v in _L2_xattn_all.items() if k in ('Wq', 'bq', 'Wk', 'bk')}
    del _L2_xattn_all

    def _L2_ffn_setup():
        import jax, jax.numpy as jnp
        import numpy as np
        EPS = 1e-08

        def _rmsnorm(x, g):
            return g * (x * jax.lax.rsqrt(jnp.mean(x * x, axis=-1, keepdims=True) + EPS))

        def _act_quant(x):
            scale = 127.0 / jnp.clip(jnp.max(jnp.abs(x), axis=-1, keepdims=True), 0.0001, None)
            y = jnp.clip(jnp.round(x * scale), -128, 127) / scale
            return x + jax.lax.stop_gradient(y - x)

        def _ternary_quant(w):
            s = jnp.mean(jnp.abs(w))
            wq = jnp.round(jnp.tanh(w / (s + EPS))) * jnp.arctanh(s)
            return w + jax.lax.stop_gradient(wq - w)

        def _linear_bit(x, w, g):
            xq = _act_quant(_rmsnorm(x, g))
            wq = _ternary_quant(w)
            return jnp.einsum('bsd,od->bso', xq, wq)
        key = jax.random.key(seed)
        k = jax.random.split(key, 4)
        B, S, D, H = (4, 512, 512, 2048)
        std_up = float(np.sqrt(2.0 / (D + H)))
        std_dn = float(np.sqrt(2.0 / (H + D)))
        return {'x': jax.random.normal(k[0], (B, S, D), dtype=jnp.float32), 'w1': jax.random.normal(k[1], (H, D), dtype=jnp.float32) * std_up, 'g1': jnp.ones((D,), dtype=jnp.float32), 'w2': jax.random.normal(k[2], (H, D), dtype=jnp.float32) * std_up, 'g2': jnp.ones((D,), dtype=jnp.float32), 'w3': jax.random.normal(k[3], (D, H), dtype=jnp.float32) * std_dn, 'g3': jnp.ones((H,), dtype=jnp.float32)}
    _L2_ffn_all = _L2_ffn_setup()
    _L2_ffn_in = {k: v for k, v in _L2_ffn_all.items() if k in ('w1', 'g1', 'w2', 'g2', 'w3', 'g3')}
    del _L2_ffn_all

    def _L3_xattn_setup():
        import jax, jax.numpy as jnp
        import numpy as np
        B_, L_, D_MODEL = (4, 512, 256)
        D_STATE, D_CONV, EXPAND = (16, 4, 2)
        D_INNER = EXPAND * D_MODEL
        DT_RANK = (D_MODEL + 15) // 16

        def silu(x):
            return x * jax.nn.sigmoid(x)
        key = jax.random.key(seed)
        ks = jax.random.split(key, 10)
        f32 = jnp.float32
        hidden_states = jax.random.normal(ks[0], (B_, L_, D_MODEL), dtype=f32)
        z = jax.random.normal(ks[1], (B_, D_INNER, L_), dtype=f32)
        in_proj_w = jax.random.normal(ks[2], (D_INNER, D_MODEL), dtype=f32) * 0.02
        conv_w = jax.random.normal(ks[3], (D_INNER, 1, D_CONV), dtype=f32) * 0.1
        conv_b = jax.random.normal(ks[4], (D_INNER,), dtype=f32) * 0.02
        x_proj_w = jax.random.normal(ks[5], (DT_RANK + 2 * D_STATE, D_INNER), dtype=f32) * 0.02
        dt_proj_w = jax.random.uniform(ks[6], (D_INNER, DT_RANK), dtype=f32, minval=-DT_RANK ** (-0.5), maxval=DT_RANK ** (-0.5))
        dt = jnp.exp(jax.random.uniform(ks[7], (D_INNER,), dtype=f32, minval=np.log(0.001), maxval=np.log(0.1)))
        dt_proj_b = jnp.log(jnp.expm1(dt))
        A_log = jnp.log(jnp.broadcast_to(jnp.arange(1, D_STATE + 1, dtype=f32), (D_INNER, D_STATE)))
        D = jnp.ones((D_INNER,), f32)
        return {'hidden_states': hidden_states, 'z': z, 'in_proj_w': in_proj_w, 'conv_w': conv_w, 'conv_b': conv_b, 'x_proj_w': x_proj_w, 'dt_proj_w': dt_proj_w, 'dt_proj_b': dt_proj_b, 'A_log': A_log, 'D': D}
    _L3_xattn_all = _L3_xattn_setup()
    _L3_xattn_in = {k: v for k, v in _L3_xattn_all.items() if k in ('in_proj_w', 'conv_w', 'conv_b', 'x_proj_w', 'dt_proj_w', 'dt_proj_b', 'A_log', 'D')}
    del _L3_xattn_all

    def _L3_ffn_setup():
        import jax, jax.numpy as jnp
        import numpy as np
        import math
        N_EMBD = 512
        N_HEAD = 16
        HEAD_DIM = N_EMBD // N_HEAD
        B, T = (2, 512)
        key = jax.random.key(seed)
        k1, k2, k3 = jax.random.split(key, 3)
        x = jax.random.normal(k1, (B, T, N_EMBD), dtype=jnp.float32)
        W_gate = jax.random.normal(k2, (N_HEAD, N_EMBD), dtype=jnp.float32) * 0.02
        W_qkv = jax.random.normal(k3, (3 * N_EMBD, N_EMBD), dtype=jnp.float32) * 0.02
        return {'x': x, 'W_gate': W_gate, 'W_qkv': W_qkv}
    _L3_ffn_all = _L3_ffn_setup()
    _L3_ffn_in = {k: v for k, v in _L3_ffn_all.items() if k in ('W_gate', 'W_qkv')}
    del _L3_ffn_all
    return {'x': x, 'ctx_1024': ctx_1024, 'fside_BxSx2_0': fside_BxSx2_0, 'L0_xattn_in_proj_w': _L0_xattn_in['in_proj_w'], 'L0_xattn_conv_w': _L0_xattn_in['conv_w'], 'L0_xattn_conv_b': _L0_xattn_in['conv_b'], 'L0_xattn_x_proj_w': _L0_xattn_in['x_proj_w'], 'L0_xattn_dt_proj_w': _L0_xattn_in['dt_proj_w'], 'L0_xattn_dt_proj_b': _L0_xattn_in['dt_proj_b'], 'L0_xattn_A_log': _L0_xattn_in['A_log'], 'L0_xattn_D': _L0_xattn_in['D'], 'L0_ffn_gate_W_packed': _L0_ffn_in['gate_W_packed'], 'L0_ffn_gate_scales': _L0_ffn_in['gate_scales'], 'L0_ffn_up_W_packed': _L0_ffn_in['up_W_packed'], 'L0_ffn_up_scales': _L0_ffn_in['up_scales'], 'L0_ffn_down_W_packed': _L0_ffn_in['down_W_packed'], 'L0_ffn_down_scales': _L0_ffn_in['down_scales'], 'L1_xattn_Wq': _L1_xattn_in['Wq'], 'L1_xattn_Wkv': _L1_xattn_in['Wkv'], 'L1_xattn_Wout': _L1_xattn_in['Wout'], 'L1_xattn_bout': _L1_xattn_in['bout'], 'L1_ffn_w_gate': _L1_ffn_in['w_gate'], 'L1_ffn_w_up': _L1_ffn_in['w_up'], 'L1_ffn_w_down': _L1_ffn_in['w_down'], 'L2_xattn_Wq': _L2_xattn_in['Wq'], 'L2_xattn_bq': _L2_xattn_in['bq'], 'L2_xattn_Wk': _L2_xattn_in['Wk'], 'L2_xattn_bk': _L2_xattn_in['bk'], 'L2_ffn_w1': _L2_ffn_in['w1'], 'L2_ffn_g1': _L2_ffn_in['g1'], 'L2_ffn_w2': _L2_ffn_in['w2'], 'L2_ffn_g2': _L2_ffn_in['g2'], 'L2_ffn_w3': _L2_ffn_in['w3'], 'L2_ffn_g3': _L2_ffn_in['g3'], 'L3_xattn_in_proj_w': _L3_xattn_in['in_proj_w'], 'L3_xattn_conv_w': _L3_xattn_in['conv_w'], 'L3_xattn_conv_b': _L3_xattn_in['conv_b'], 'L3_xattn_x_proj_w': _L3_xattn_in['x_proj_w'], 'L3_xattn_dt_proj_w': _L3_xattn_in['dt_proj_w'], 'L3_xattn_dt_proj_b': _L3_xattn_in['dt_proj_b'], 'L3_xattn_A_log': _L3_xattn_in['A_log'], 'L3_xattn_D': _L3_xattn_in['D'], 'L3_ffn_W_gate': _L3_ffn_in['W_gate'], 'L3_ffn_W_qkv': _L3_ffn_in['W_qkv']}

def reference(x, ctx_1024, fside_BxSx2_0, L0_xattn_in_proj_w, L0_xattn_conv_w, L0_xattn_conv_b, L0_xattn_x_proj_w, L0_xattn_dt_proj_w, L0_xattn_dt_proj_b, L0_xattn_A_log, L0_xattn_D, L0_ffn_gate_W_packed, L0_ffn_gate_scales, L0_ffn_up_W_packed, L0_ffn_up_scales, L0_ffn_down_W_packed, L0_ffn_down_scales, L1_xattn_Wq, L1_xattn_Wkv, L1_xattn_Wout, L1_xattn_bout, L1_ffn_w_gate, L1_ffn_w_up, L1_ffn_w_down, L2_xattn_Wq, L2_xattn_bq, L2_xattn_Wk, L2_xattn_bk, L2_ffn_w1, L2_ffn_g1, L2_ffn_w2, L2_ffn_g2, L2_ffn_w3, L2_ffn_g3, L3_xattn_in_proj_w, L3_xattn_conv_w, L3_xattn_conv_b, L3_xattn_x_proj_w, L3_xattn_dt_proj_w, L3_xattn_dt_proj_b, L3_xattn_A_log, L3_xattn_D, L3_ffn_W_gate, L3_ffn_W_qkv):
    import jax
    import jax.numpy as jnp

    def _L0_xattn_ref(hidden_states, z, in_proj_w, conv_w, conv_b, x_proj_w, dt_proj_w, dt_proj_b, A_log, D):
        import jax, jax.numpy as jnp
        import numpy as np
        import math
        B, L, DM = (2, 512, 256)
        DS, DC, EXP = (16, 4, 2)
        DI = EXP * DM
        DR = math.ceil(DM / 16)
        DT_MIN, DT_MAX, DT_FLOOR = (0.001, 0.1, 0.0001)

        def _ssm_forward(hidden_states, z, in_proj_w, conv_w, conv_b, x_proj_w, dt_proj_w, dt_proj_b, A_log, D):
            b = hidden_states.shape[0]
            x = jnp.einsum('ed,bld->bel', in_proj_w, hidden_states)
            xp = jnp.pad(x, ((0, 0), (0, 0), (DC - 1, 0)))
            xc = jax.lax.conv_general_dilated(xp, conv_w[:, None, :], window_strides=(1,), padding='VALID', dimension_numbers=('NCH', 'OIH', 'NCH'), feature_group_count=DI)
            u = jax.nn.silu(xc + conv_b[None, :, None])
            x_dbl = jnp.einsum('ke,bel->bkl', x_proj_w, u)
            dt_lo = x_dbl[:, :DR]
            Bm = x_dbl[:, DR:DR + DS]
            Cm = x_dbl[:, DR + DS:]
            delta = jax.nn.softplus(jnp.einsum('er,brl->bel', dt_proj_w, dt_lo) + dt_proj_b[None, :, None])
            A = -jnp.exp(A_log)

            def step(state, xs):
                d_t, B_t, C_t, u_t = xs
                dA = jnp.exp(d_t[..., None] * A)
                state = state * dA + (d_t * u_t)[..., None] * B_t[:, None, :]
                y_t = jnp.einsum('ben,bn->be', state, C_t)
                return (state, y_t)
            xs = (jnp.moveaxis(delta, -1, 0), jnp.moveaxis(Bm, -1, 0), jnp.moveaxis(Cm, -1, 0), jnp.moveaxis(u, -1, 0))
            state0 = jnp.zeros((b, DI, DS), delta.dtype)
            _, ys = jax.lax.scan(step, state0, xs)
            y = jnp.moveaxis(ys, 0, -1)
            y = y + D[None, :, None] * u
            y = y * jax.nn.silu(z)
            return jnp.swapaxes(y, 1, 2)
        return _ssm_forward(hidden_states, z, in_proj_w, conv_w, conv_b, x_proj_w, dt_proj_w, dt_proj_b, A_log, D)

    def _L0_ffn_ref(x, gate_W_packed, gate_scales, up_W_packed, up_scales, down_W_packed, down_scales):
        import jax, jax.numpy as jnp
        import numpy as np
        BLOCK_SIZE = 32
        HIDDEN_SIZE = 512
        MLP_DIM = 4096
        NVFP4_LUT = jnp.array([0.0, 0.5, 1.0, 1.5, 2.0, 3.0, 4.0, 6.0, 0.0, -0.5, -1.0, -1.5, -2.0, -3.0, -4.0, -6.0], dtype=jnp.float32)

        def dequant_nvfp4(W_packed, scales, block=BLOCK_SIZE):
            N = W_packed.shape[0]
            low = W_packed & 15
            high = W_packed >> 4 & 15
            idx = jnp.stack([low, high], axis=-1).reshape(N, -1)
            vals = NVFP4_LUT[idx]
            K = vals.shape[1]
            vals = vals.reshape(N, K // block, block) * scales[:, :, None]
            return vals.reshape(N, K)
        B, S, H = x.shape
        xt = x.reshape(B * S, H)
        Wg = dequant_nvfp4(gate_W_packed, gate_scales)
        Wu = dequant_nvfp4(up_W_packed, up_scales)
        Wd = dequant_nvfp4(down_W_packed, down_scales)
        gate = jnp.einsum('th,nh->tn', xt, Wg)
        up = jnp.einsum('th,nh->tn', xt, Wu)
        gelu = jnp.tanh(0.7978845608028654 * (gate + 0.044715 * gate ** 3)) * gate * 0.5 + gate * 0.5
        inter = gelu * up
        out = jnp.einsum('tn,hn->th', inter, Wd)
        return out.reshape(B, S, H)

    def _L1_xattn_ref(x, ctx, pos_map, ctx_pos_map, Wq, Wkv, Wout, bout):
        import jax, jax.numpy as jnp
        import numpy as np
        DIM = 512
        CTX_DIM = 256
        N_HEADS = 32
        HEAD_DIM = DIM // N_HEADS
        POS_DIM = 2
        B, N, CTXN = (2, 512, 512)
        ROPE_BASE = 10000.0

        def apply_axial_rope(x, pos):
            b, n, h, d = x.shape
            p = pos.shape[-1]
            dpa = d // p
            half = dpa // 2
            freqs = ROPE_BASE ** (-jnp.arange(half, dtype=x.dtype) / half)
            ang = pos[..., :, None] * freqs
            cos = jnp.cos(ang)[:, :, None, :, :]
            sin = jnp.sin(ang)[:, :, None, :, :]
            xr = x.reshape(b, n, h, p, half, 2)
            x1, x2 = (xr[..., 0], xr[..., 1])
            out = jnp.stack([x1 * cos - x2 * sin, x1 * sin + x2 * cos], axis=-1)
            return out.reshape(b, n, h, d)
        b, n, _ = x.shape
        ctx_n = ctx.shape[1]
        q = (x @ Wq).reshape(b, n, N_HEADS, HEAD_DIM)
        k, v = jnp.split(ctx @ Wkv, 2, axis=-1)
        k = k.reshape(b, ctx_n, N_HEADS, HEAD_DIM)
        v = v.reshape(b, ctx_n, N_HEADS, HEAD_DIM)
        q = apply_axial_rope(q, pos_map)
        k = apply_axial_rope(k, ctx_pos_map)
        scale = 1.0 / np.sqrt(HEAD_DIM).astype(np.float32)
        logits = jnp.einsum('bqhd,bkhd->bhqk', q, k) * scale
        w = jax.nn.softmax(logits, axis=-1)
        attn = jnp.einsum('bhqk,bkhd->bqhd', w, v)
        attn = attn.reshape(b, n, N_HEADS * HEAD_DIM)
        return attn @ Wout + bout

    def _L1_ffn_ref(x, w_gate, w_up, w_down):
        import jax, jax.numpy as jnp
        import numpy as np
        EPS = 1e-05

        def _quant_weight(w):
            scale = jnp.mean(jnp.abs(w)) + EPS
            wq = jnp.clip(jnp.round(w / scale), -1.0, 1.0) * scale
            return w + jax.lax.stop_gradient(wq - w)

        def _quant_act(x):
            scale = jnp.maximum(jnp.max(jnp.abs(x), axis=-1, keepdims=True), EPS) / 127.0
            xq = jnp.clip(jnp.round(x / scale), -128.0, 127.0) * scale
            return x + jax.lax.stop_gradient(xq - x)

        def bitlinear(x, w):
            return jnp.einsum('bsi,oi->bso', _quant_act(x), _quant_weight(w))
        gate = jax.nn.sigmoid(bitlinear(x, w_gate))
        up = bitlinear(x, w_up)
        h = gate * up
        return bitlinear(h, w_down)

    def _L2_xattn_ref(teacher_logits, teacher_features, Wq, bq, Wk, bk):
        import jax, jax.numpy as jnp
        import numpy as np
        query = jnp.einsum('bnc,dc->bnd', teacher_features, Wq) + bq
        key = jnp.einsum('bnc,dc->bnd', teacher_features, Wk) + bk
        energy = jnp.einsum('bnd,bmd->bnm', query, key)
        attention = jax.nn.softmax(energy, axis=-1)
        x_m = jnp.einsum('bln,bmn->blm', teacher_logits, attention)
        return x_m

    def _L2_ffn_ref(x, w1, g1, w2, g2, w3, g3):
        import jax, jax.numpy as jnp
        import numpy as np
        EPS = 1e-08

        def _rmsnorm(x, g):
            return g * (x * jax.lax.rsqrt(jnp.mean(x * x, axis=-1, keepdims=True) + EPS))

        def _act_quant(x):
            scale = 127.0 / jnp.clip(jnp.max(jnp.abs(x), axis=-1, keepdims=True), 0.0001, None)
            y = jnp.clip(jnp.round(x * scale), -128, 127) / scale
            return x + jax.lax.stop_gradient(y - x)

        def _ternary_quant(w):
            s = jnp.mean(jnp.abs(w))
            wq = jnp.round(jnp.tanh(w / (s + EPS))) * jnp.arctanh(s)
            return w + jax.lax.stop_gradient(wq - w)

        def _linear_bit(x, w, g):
            xq = _act_quant(_rmsnorm(x, g))
            wq = _ternary_quant(w)
            return jnp.einsum('bsd,od->bso', xq, wq)
        swish = jax.nn.silu(_linear_bit(x, w1, g1))
        x_v = _linear_bit(x, w2, g2)
        h = swish * x_v
        return _linear_bit(h, w3, g3)

    def _L3_xattn_ref(hidden_states, z, in_proj_w, conv_w, conv_b, x_proj_w, dt_proj_w, dt_proj_b, A_log, D):
        import jax, jax.numpy as jnp
        import numpy as np
        B_, L_, D_MODEL = (4, 512, 256)
        D_STATE, D_CONV, EXPAND = (16, 4, 2)
        D_INNER = EXPAND * D_MODEL
        DT_RANK = (D_MODEL + 15) // 16

        def silu(x):
            return x * jax.nn.sigmoid(x)
        Bsz, L, _ = hidden_states.shape
        d_inner, _, d_conv = conv_w.shape
        dt_rank = dt_proj_w.shape[1]
        d_state = A_log.shape[1]
        x = jnp.einsum('bld,ed->bel', hidden_states, in_proj_w)
        xc = jax.lax.conv_general_dilated(x, conv_w, window_strides=(1,), padding=[(d_conv - 1, 0)], feature_group_count=d_inner, dimension_numbers=('NCH', 'OIH', 'NCH'))
        x = silu(xc + conv_b[None, :, None])
        x_dbl = jnp.einsum('bdl,ed->bel', x, x_proj_w)
        dt_low, Bm, Cm = jnp.split(x_dbl, [dt_rank, dt_rank + d_state], axis=1)
        dt = jnp.einsum('brl,dr->bdl', dt_low, dt_proj_w)
        dt = jax.nn.softplus(dt + dt_proj_b[None, :, None])
        A = -jnp.exp(A_log)
        dt_t = jnp.moveaxis(dt, -1, 0)
        B_t = jnp.moveaxis(Bm, -1, 0)
        C_t = jnp.moveaxis(Cm, -1, 0)
        u_t = jnp.moveaxis(x, -1, 0)

        def step(state, inp):
            d, b, c, u = inp
            dA = jnp.exp(d[..., None] * A)
            state = state * dA + (d * u)[..., None] * b[:, None, :]
            y = jnp.einsum('bdn,bn->bd', state, c)
            return (state, y)
        state0 = jnp.zeros((Bsz, d_inner, d_state), x.dtype)
        _, ys = jax.lax.scan(step, state0, (dt_t, B_t, C_t, u_t))
        y = jnp.moveaxis(ys, 0, 2)
        y = y + D[None, :, None] * x
        y = y * silu(z)
        return jnp.swapaxes(y, 1, 2)

    def _L3_ffn_ref(x, W_gate, W_qkv):
        import jax, jax.numpy as jnp
        import numpy as np
        import math
        N_EMBD = 512
        N_HEAD = 16
        HEAD_DIM = N_EMBD // N_HEAD
        B, T = (2, 512)
        Bb, Tt, C = x.shape
        H, hd = (N_HEAD, HEAD_DIM)
        gating = jax.nn.softmax(x @ W_gate.T, axis=-1)
        idx = jnp.argmax(gating, axis=-1)
        indicator = jax.nn.one_hot(idx, H, dtype=gating.dtype)
        top1_val = jnp.max(gating, axis=-1, keepdims=True)
        gating_top1 = indicator * top1_val
        qkv = x @ W_qkv.T
        q, k, v = jnp.split(qkv, 3, axis=-1)
        k = k.reshape(Bb, Tt, H, hd)
        v = v.reshape(Bb, Tt, H, hd)
        k_shared = jnp.einsum('bth,bthd->btd', indicator, k)
        v_shared = jnp.einsum('bth,bthd->btd', gating_top1, v)
        q = q.reshape(Bb, Tt, H, hd).transpose(0, 2, 1, 3)
        att = jnp.einsum('bhqd,bkd->bhqk', q, k_shared) * (1.0 / math.sqrt(hd))
        causal = jnp.tril(jnp.ones((Tt, Tt), dtype=bool))
        att = jnp.where(causal[None, None, :, :], att, -jnp.inf)
        att = jax.nn.softmax(att, axis=-1)
        y = jnp.einsum('bhqk,bkd->bhqd', att, v_shared)
        y = y.transpose(0, 2, 1, 3).reshape(Bb, Tt, C)
        return y
    x = x + _L0_xattn_ref(ctx_1024, _layernorm(x, axis=-1), L0_xattn_in_proj_w, L0_xattn_conv_w, L0_xattn_conv_b, L0_xattn_x_proj_w, L0_xattn_dt_proj_w, L0_xattn_dt_proj_b, L0_xattn_A_log, L0_xattn_D)
    x = x + _L0_ffn_ref(_layernorm(x, axis=-1), L0_ffn_gate_W_packed, L0_ffn_gate_scales, L0_ffn_up_W_packed, L0_ffn_up_scales, L0_ffn_down_W_packed, L0_ffn_down_scales)
    x = x + _L1_xattn_ref(_layernorm(x, axis=-1), ctx_1024, fside_BxSx2_0, fside_BxSx2_0, L1_xattn_Wq, L1_xattn_Wkv, L1_xattn_Wout, L1_xattn_bout)
    x = x + _L1_ffn_ref(_layernorm(x, axis=-1), L1_ffn_w_gate, L1_ffn_w_up, L1_ffn_w_down)
    x = x + _L2_xattn_ref(_layernorm(x, axis=-1), ctx_1024, L2_xattn_Wq, L2_xattn_bq, L2_xattn_Wk, L2_xattn_bk)
    x = x + _L2_ffn_ref(_layernorm(x, axis=-1), L2_ffn_w1, L2_ffn_g1, L2_ffn_w2, L2_ffn_g2, L2_ffn_w3, L2_ffn_g3)
    x = x + _L3_xattn_ref(ctx_1024, _layernorm(x, axis=-1), L3_xattn_in_proj_w, L3_xattn_conv_w, L3_xattn_conv_b, L3_xattn_x_proj_w, L3_xattn_dt_proj_w, L3_xattn_dt_proj_b, L3_xattn_A_log, L3_xattn_D)
    x = x + _L3_ffn_ref(_layernorm(x, axis=-1), L3_ffn_W_gate, L3_ffn_W_qkv)
    return x

_drawn_inputs = setup_inputs


def setup_inputs(seed=0):
    import zlib

    import numpy as np

    out = dict(_drawn_inputs(seed))
    spreads = {'L0_xattn_conv_b': (0.0, 0.1),
     'L0_xattn_D': (1.0, 0.2),
     'L1_xattn_bout': (0.0, 0.1),
     'L2_xattn_bq': (0.0, 0.1),
     'L2_xattn_bk': (0.0, 0.1),
     'L2_ffn_g1': (1.0, 0.2),
     'L2_ffn_g2': (1.0, 0.2),
     'L2_ffn_g3': (1.0, 0.2),
     'L3_xattn_D': (1.0, 0.2)}
    factors = {}
    for name, (base, spread) in spreads.items():
        noise = np.random.default_rng([zlib.crc32(name.encode()), seed]).standard_normal(out[name].shape)
        drawn = base * np.exp(spread * noise) if base else spread * noise
        out[name] = jnp.asarray(drawn.astype(out[name].dtype))
    for name, factor in factors.items():
        out[name] = (out[name] * factor).astype(out[name].dtype)
    return out
```

```python
from contextlib import ExitStack

import numpy as np

import concourse.bass as bass
from concourse import mybir

F32 = mybir.dt.float32
BF16 = mybir.dt.bfloat16
I32 = mybir.dt.int32
ALU = mybir.AluOpType
ACT = mybir.ActivationFunctionType
AX = mybir.AxisListType

P = 128
B, L, D = 4, 512, 512
C = 256
NT = B * L // P
TB = L // P
KD = D // P
KC = C // P
BANK = 512
MAGIC = 1.5 * 2.0 ** 23


class Chain:

    def __init__(self, eng, sem):
        self.eng, self.sem, self.n, self.base = eng, sem, 0, 0

    def did(self, ins):
        ins.then_inc(self.sem, 1)
        self.n += 1
        return self.base + self.n

    def settle(self):
        self.eng.wait_ge(self.sem, self.base + self.n)

    def step(self, ins):
        self.did(ins)
        self.settle()


class Chip:

    def __init__(self, nc, ctx):
        self.nc, self.ctx, self.count = nc, ctx, 0
        self.X = self.sb("X", [P, NT, D])
        self.XN = self.sb("XN", [P, NT, D])
        self.ctxT = self.sb("ctxT", [P, KC, B * L])
        self.ident = self.sb("ident", [P, P])
        self.identb = self.sb("identb", [P, P], BF16)

    def sb(self, name, shape, dt=F32, ctx=None):
        return (ctx or self.ctx).enter_context(self.nc.sbuf_tensor(name, shape, dt))

    def ps(self, name, shape, dt=F32, ctx=None):
        return (ctx or self.ctx).enter_context(self.nc.psum_tensor(name, shape, dt))

    def sem(self, name):
        return self.nc.alloc_semaphore(name)

    def run(self, stage, *args, **kw):
        with self.nc.cleanup_on_exit():
            stage(self, *args, **kw)
        self.nc.all_engine_barrier()


def stage_start(chip, x, ctx_dram):
    nc = chip.nc
    X, ctxT, ident = chip.X, chip.ctxT, chip.ident
    with ExitStack() as st:
        cn = chip.sb("ctx_rows", [P, NT, C], F32, st)
        pt = chip.ps("ctx_pt", [P, 2, 4, P], F32, st)
        s_x, s_c = chip.sem("start_x"), chip.sem("start_ctx")
        s_one, s_id, s_idb = chip.sem("start_zero"), chip.sem("start_ident"), chip.sem("start_identb")
        s_t, s_cp = chip.sem("start_transposed"), chip.sem("start_copied")
        block = st.enter_context(nc.Block())

        @block.sync
        def _(sp):
            sp.dma_start(cn[:], ctx_dram.rearrange("b (t p) c -> p (b t) c", p=P)).then_inc(s_c, 16)
            sp.dma_start(X[:], x.rearrange("b (t p) c -> p (b t) c", p=P)).then_inc(s_x, 16)
            sp.wait_ge(s_x, 16)

        @block.gpsimd
        def _(pool):
            pool.memset(ident[:], 0.0).then_inc(s_one, 1)
            pool.wait_ge(s_one, 1)
            pool.affine_select(out=ident[:], in_=ident[:], compare_op=ALU.not_equal, fill=1.0, base=0,
                               pattern=[[-1, P]], channel_multiplier=1).then_inc(s_id, 1)

        @block.tensor
        def _(pe):
            pe.wait_ge(s_id, 1)
            pe.wait_ge(s_c, 16)
            for k in range(KC):
                for g in range(NT // 4):
                    n = k * (NT // 4) + g
                    if n >= 2:
                        pe.wait_ge(s_cp, n - 1)
                    for j in range(4):
                        m = pe.transpose(pt[:, n % 2, j, :], cn[:, 4 * g + j, k * P:(k + 1) * P], ident[:])
                    m.then_inc(s_t, 1)

        @block.scalar
        def _(act):
            for k in range(KC):
                for g in range(NT // 4):
                    n = k * (NT // 4) + g
                    act.wait_ge(s_t, n + 1)
                    act.copy(ctxT[:, k, g * 4 * P:(g + 1) * 4 * P].rearrange("p (j t) -> p j t", j=4),
                             pt[:, n % 2]).then_inc(s_cp, 1)

        @block.vector
        def _(dve):
            dve.wait_ge(s_id, 1)
            dve.tensor_copy(chip.identb[:], ident[:]).then_inc(s_idb, 1)


def stage_norm(chip, name, eps=1e-5):
    nc, X, XN = chip.nc, chip.X, chip.XN
    with ExitStack() as st:
        stats = chip.sb(name + "_stats", [P, NT, 6], F32, st)
        mv = chip.sb(name + "_mv", [P, NT, 2], F32, st)
        std = chip.sb(name + "_std", [P, NT], F32, st)
        rstd = chip.sb(name + "_rstd", [P, NT], F32, st)
        shift = chip.sb(name + "_shift", [P, NT], F32, st)
        epst = chip.sb(name + "_eps", [P, 1], F32, st)
        s_st, s_mv, s_eps = chip.sem(name + "_stats"), chip.sem(name + "_mv"), chip.sem(name + "_eps")
        s_std, s_rs, s_sh = chip.sem(name + "_std"), chip.sem(name + "_rstd"), chip.sem(name + "_shift")
        s_xa, s_xd = chip.sem(name + "_xn_act"), chip.sem(name + "_xn_dve")
        block = st.enter_context(nc.Block())

        @block.vector
        def _(dve):
            dve.memset(epst[:], eps).then_inc(s_eps, 1)
            for t in range(NT):
                dve.bn_stats(stats[:, t, :], X[:, t, :]).then_inc(s_st, 1)
            for t in range(NT):
                dve.wait_ge(s_st, t + 1)
                dve.bn_aggr(mv[:, t, :], stats[:, t, :]).then_inc(s_mv, 1)
            dve.wait_ge(s_std, 1)
            dve.reciprocal(rstd[:], std[:]).then_inc(s_rs, 1)
            dve.wait_ge(s_rs, 1)
            dve.wait_ge(s_mv, NT)
            dve.scalar_tensor_tensor(out=shift[:], in0=mv[:, :, 0], scalar=-1.0, in1=rstd[:],
                                     op0=ALU.mult, op1=ALU.mult).then_inc(s_sh, 1)
            for t in range(0, NT, 2):
                dve.wait_ge(s_rs, 1)
                dve.tensor_scalar(XN[:, t, :], X[:, t, :], mv[:, t, 0:1], rstd[:, t:t + 1],
                                  ALU.subtract, ALU.mult).then_inc(s_xd, 1)

        @block.scalar
        def _(act):
            act.wait_ge(s_eps, 1)
            act.wait_ge(s_mv, NT)
            act.activation(std[:], mv[:, :, 1], ACT.Sqrt, bias=epst[:]).then_inc(s_std, 1)
            act.wait_ge(s_sh, 1)
            for t in range(1, NT, 2):
                act.activation(XN[:, t, :], X[:, t, :], ACT.Identity, bias=shift[:, t:t + 1],
                               scale=rstd[:, t:t + 1]).then_inc(s_xa, 1)


def stage_end(chip, out):
    with ExitStack() as st:
        s_o = chip.sem("end_out")
        block = st.enter_context(chip.nc.Block())

        @block.sync
        def _(sp):
            sp.dma_start(out.rearrange("b (t p) c -> p (b t) c", p=P), chip.X[:]).then_inc(s_o, 16)
            sp.wait_ge(s_o, 16)


def stage_mamba(chip, name, bc_dram, in_w, conv_w, conv_b, x_w, dt_w, dt_b, a_log, d_skip):
    nc, X, XN, ctxT, ident = chip.nc, chip.X, chip.XN, chip.ctxT, chip.ident
    EB = in_w.shape[0] // P
    R = dt_w.shape[1]
    N = a_log.shape[1]
    TAPS = conv_w.shape[1]
    W = R + 2 * N
    with ExitStack() as st:
        def sb(n, shape, dt=F32):
            return chip.sb(f"{name}_{n}", shape, dt, st)

        def sem(n):
            return chip.sem(f"{name}_{n}")

        in_rows, in_T = sb("in_rows", [P, EB, C]), sb("in_T", [P, KC, EB * P])
        x_rows, x_T = sb("x_rows", [W, EB * P]), sb("x_T", [P, EB, W])
        dt_rows, dt_T = sb("dt_rows", [P, EB, R]), sb("dt_T", [R, EB * P])
        small = sb("small", [P, EB, TAPS + 3])
        a_neg = sb("a_neg", [P, EB, N])
        a_in = sb("a_in", [P, EB, N])
        skip = sb("skip", [P, EB, P])
        xin = sb("xin", [P, EB, TAPS - 1 + L])
        u, delta, du = sb("u", [P, EB, L]), sb("delta", [P, EB, L]), sb("du", [P, EB, L])
        xdbl = sb("xdbl", [W, L])
        dA = [sb(f"dA{i}", [P, EB, L]) for i in range(2)]
        dB = [sb(f"dB{i}", [P, EB, L]) for i in range(2)]
        H = [sb(f"H{i}", [P, EB, L]) for i in range(2)]
        BC = [sb(f"BC{i}", [P, 2, L]) for i in range(2)]
        gate = sb("gate", [P, EB, L])
        ps_y = chip.ps(name + "_y", [P, EB, L], F32, st)
        ps_w = chip.ps(name + "_w", [P, EB, L], F32, st)
        flat = "p e t -> p (e t)"

        s_ld, s_wt, s_wc = sem("loaded"), sem("w_transposed"), sem("w_copied")
        s_a, s_skip, s_pad = sem("a"), sem("skip"), sem("padded")
        s_x, s_xin, s_conv, s_u = sem("x_proj_in"), sem("xin"), sem("conv"), sem("u")
        s_dbl, s_dblc, s_bcd = sem("xdbl"), sem("xdbl_copied"), sem("bc_stored")
        s_dt, s_ab, s_e, s_ln, s_del = sem("dt"), sem("dt_abs"), sem("dt_exp"), sem("dt_ln"), sem("delta")
        s_c = sem("dve_chain")
        s_bc = [sem(f"bc_loaded{i}") for i in range(2)]
        s_dA, s_dB, s_sc, s_hc, s_acc = sem("dA"), sem("dB"), sem("scanned"), sem("hc"), sem("accumulated")
        s_z, s_yz, s_yt, s_add = sem("gate"), sem("gated"), sem("y_transposed"), sem("added")
        block = st.enter_context(nc.Block())

        @block.sync
        def _(sp):
            sp.dma_start(in_rows[:], in_w.rearrange("(e p) c -> p e c", p=P)).then_inc(s_ld, 16)
            sp.dma_start(x_rows[:], x_w).then_inc(s_ld, 16)
            sp.dma_start(dt_rows[:], dt_w.rearrange("(e p) c -> p e c", p=P)).then_inc(s_ld, 16)
            sp.dma_start(small[:, :, 0:TAPS], conv_w.rearrange("(e p) c -> p e c", p=P)).then_inc(s_ld, 16)
            for i, v in enumerate((conv_b, dt_b, d_skip)):
                sp.dma_start(small[:, :, TAPS + i:TAPS + i + 1],
                             v.rearrange("(e p o) -> p e o", p=P, o=1), allow_slow_non_contiguous=True).then_inc(s_ld, 16)
            sp.dma_start(a_in[:], a_log.rearrange("(e p) c -> p e c", p=P)).then_inc(s_ld, 16)
            with sp.Fori(0, B) as b:
                sp.wait_ge(s_dblc, b + 1)
                sp.dma_start(bc_dram[b], xdbl[R:W, :]).then_inc(s_bcd, 16)
                with sp.Fori(0, N // 2) as k:
                    for j in range(2):
                        sp.wait_ge(s_bcd, 16 * b + 16)
                        sp.wait_ge(s_hc, b * N + k * 2 + 1)
                        sp.dma_start(BC[j][:], bc_dram[b].rearrange("(w n) t -> n w t", w=2)[
                            bass.ds(k * 2 + j, 1)].broadcast_to([P, 2, L])).then_inc(s_bc[j], 16)

        @block.tensor
        def _(pe):
            pe.sem_inc(s_acc, 1)
            pe.wait_ge(s_ld, 128)
            for e in range(EB):
                for k in range(KC):
                    m = pe.transpose(ps_w[:, k, e * P:(e + 1) * P], in_rows[:, e, k * P:(k + 1) * P], ident[:])
                m = pe.transpose(ps_w[:, 2, e * W:(e + 1) * W], x_rows[:, e * P:(e + 1) * P], ident[0:W, 0:W])
                m = pe.transpose(ps_w[0:R, 3, e * P:(e + 1) * P], dt_rows[:, e, :], ident[:])
            m.then_inc(s_wt, 1)
            pe.wait_ge(s_wc, 3)
            pe.wait_ge(s_skip, EB)
            with pe.Fori(0, B) as b:
                for e in range(EB):
                    for k in range(KC):
                        m = pe.matmul(ps_w[:, e, :], in_T[:, k, e * P:(e + 1) * P],
                                      ctxT[:, k, bass.ds(b * L, L)], start=(k == 0), stop=(k == KC - 1))
                    m.then_inc(s_x, 1)
                pe.wait_ge(s_u, b + 1)
                for e in range(EB):
                    m = pe.matmul(ps_w[0:W, 0, :], x_T[:, e, :], u[:, e, :], start=(e == 0), stop=(e == EB - 1))
                m.then_inc(s_dbl, 1)
                for e in range(EB):
                    pe.matmul(ps_y[:, e, :], skip[:, e, :], u[:, e, :], start=True, stop=True)
                pe.wait_ge(s_dblc, b + 1)
                for e in range(EB):
                    m = pe.matmul(ps_w[:, e, :], dt_T[:, e * P:(e + 1) * P], xdbl[0:R, :], start=True, stop=True)
                m.then_inc(s_dt, 1)
                with pe.Fori(0, N // 2) as k:
                    for j in range(2):
                        pe.wait_ge(s_hc, b * N + k * 2 + j + 2)
                        for e in range(EB):
                            m = pe.matmul(ps_y[:, e, :], ident[:], H[j][:, e, :], start=False, stop=True,
                                          skip_group_check=True)
                        m.then_inc(s_acc, 1)
                pe.wait_ge(s_yz, b + 1)
                for t in range(TB):
                    for e in range(EB):
                        m = pe.transpose(ps_w[:, t, e * P:(e + 1) * P], gate[:, e, t * P:(t + 1) * P], ident[:])
                    m.then_inc(s_yt, 1)
                pe.wait_ge(s_add, b + 1)

        @block.scalar
        def _(act):
            act.wait_ge(s_ld, 128)
            act.activation(a_neg[:], a_in[:], ACT.Exp).then_inc(s_a, 1)
            act.wait_ge(s_wt, 1)
            act.copy(in_T[:], ps_w[:, 0:KC, :]).then_inc(s_wc, 1)
            act.copy(x_T[:], ps_w[:, 2, 0:EB * W].rearrange("p (e w) -> p e w", e=EB)).then_inc(s_wc, 1)
            act.copy(dt_T[:], ps_w[0:R, 3, :]).then_inc(s_wc, 1)
            act.wait_ge(s_pad, 4)
            with act.Fori(0, B) as b:
                for e in range(EB):
                    act.wait_ge(s_x, b * EB + e + 1)
                    act.copy(xin[:, e, TAPS - 1:], ps_w[:, e, :]).then_inc(s_xin, 1)
                act.wait_ge(s_conv, b + 1)
                act.activation(u[:], delta[:], ACT.Silu).then_inc(s_u, 1)
                act.activation(gate[:], XN[:, bass.ds(b * TB, TB), :], ACT.Silu).then_inc(s_z, 1)
                act.wait_ge(s_dbl, b + 1)
                act.copy(xdbl[:], ps_w[0:W, 0, :]).then_inc(s_dblc, 1)
                act.wait_ge(s_dt, b + 1)
                act.wait_ge(s_u, b + 1)
                for e in range(EB):
                    act.activation(delta[:, e, :], ps_w[:, e, :], ACT.Abs,
                                   bias=small[:, e, TAPS + 1:TAPS + 2]).then_inc(s_ab, 1)
                act.wait_ge(s_ab, b * EB + EB)
                act.activation(dA[0][:], delta[:], ACT.Exp, scale=-1.0).then_inc(s_e, 1)
                act.wait_ge(s_e, b + 1)
                act.activation(delta[:], dA[0][:], ACT.Ln, bias=1.0).then_inc(s_ln, 1)
                act.wait_ge(s_del, b * 2 + 2)
                with act.Fori(0, N // 2) as k:
                    for j in range(2):
                        act.wait_ge(s_sc, b * N + k * 2 + 1)
                        for e in range(EB):
                            act.activation(dA[j][:, e, 1:], delta[:, e, 1:], ACT.Exp,
                                           scale=a_neg[:, e, bass.ds(k * 2 + j, 1)]).then_inc(s_dA, 1)

        @block.gpsimd
        def _(pool):
            with pool.Fori(0, B) as b:
                with pool.Fori(0, N // 2) as k:
                    for j in range(2):
                        pool.wait_ge(s_del, b * 2 + 2)
                        pool.wait_ge(s_bc[j], (b * (N // 2) + k + 1) * 16)
                        pool.wait_ge(s_sc, b * N + k * 2 + 1)
                        pool.tensor_tensor(dB[j][:], du[:], BC[j][:, 0:1, :].broadcast_to([P, EB, L]),
                                           ALU.mult).then_inc(s_dB, 1)

        @block.vector
        def _(dve):
            ch = Chain(dve, s_c)
            dve.sem_inc(s_sc, 1)
            dve.sem_inc(s_hc, 1)
            dve.memset(xin[:, :, 0:TAPS - 1], 0.0).then_inc(s_pad, 1)
            dve.wait_ge(s_a, 1)
            dve.tensor_scalar(a_neg[:], a_neg[:], -1.0, None, ALU.mult).then_inc(s_pad, 1)
            dve.wait_ge(s_ld, 128)
            for e in range(EB):
                dve.tensor_scalar(skip[:, e, :], ident[:], small[:, e, TAPS + 2:TAPS + 3], None,
                                  ALU.mult).then_inc(s_skip, 1)
            for i in range(2):
                dve.memset(dA[i][:, :, 0:1], 0.0).then_inc(s_pad, 1)
            dve.wait_ge(s_pad, 4)
            with dve.Fori(0, B) as b:
                PER = TAPS * EB + 6
                ch.base, ch.n = b * PER, 0
                for e in range(EB):
                    w = small[:, e, :]
                    dve.wait_ge(s_xin, b * EB + e + 1)
                    ch.step(dve.tensor_scalar(delta[:, e, :], xin[:, e, 0:L], w[:, 0:1], w[:, TAPS:TAPS + 1],
                                              ALU.mult, ALU.add))
                    for i in range(1, TAPS):
                        ch.step(dve.scalar_tensor_tensor(out=delta[:, e, :], in0=xin[:, e, i:i + L],
                                                         scalar=w[:, i:i + 1], in1=delta[:, e, :],
                                                         op0=ALU.mult, op1=ALU.add))
                dve.sem_inc(s_conv, 1)
                dve.wait_ge(s_ln, b + 1)
                t1, t2 = dB[0], dB[1]
                ch.step(dve.tensor_scalar(t1[:], dA[0][:], 1.0, -1.0, ALU.add, ALU.add))
                ch.step(dve.tensor_tensor(t2[:], dA[0][:], t1[:], ALU.subtract))
                ch.step(dve.tensor_tensor(delta[:], delta[:], t2[:], ALU.add))
                for e in range(EB):
                    last = dve.tensor_scalar(t1[:, e, :], ps_w[:, e, :], small[:, e, TAPS + 1:TAPS + 2], 0.0,
                                             ALU.add, ALU.max)
                ch.step(last)
                dve.tensor_tensor(delta[:], delta[:], t1[:], ALU.add).then_inc(s_del, 1)
                dve.memset(dA[0][:, :, 0:1], 0.0).then_inc(s_c, 1)
                ch.n += 1
                dve.wait_ge(s_del, b * 2 + 1)
                dve.wait_ge(s_u, b + 1)
                ch.settle()
                dve.tensor_tensor(du[:], delta[:], u[:], ALU.mult).then_inc(s_del, 1)
                with dve.Fori(0, N // 2) as k:
                    for j in range(2):
                        n = b * N + k * 2 + j
                        dve.wait_ge(s_dA, (n + 1) * EB)
                        dve.wait_ge(s_dB, n + 1)
                        dve.wait_ge(s_acc, b * N + k * 2 + 1)
                        dve.tensor_tensor_scan(H[j][:].rearrange(flat), dA[j][:].rearrange(flat),
                                               dB[j][:].rearrange(flat), 0.0, ALU.mult, ALU.add).then_inc(s_sc, 1)
                        dve.wait_ge(s_sc, n + 2)
                        dve.wait_ge(s_bc[j], (b * (N // 2) + k + 1) * 16)
                        dve.tensor_tensor(H[j][:], H[j][:], BC[j][:, 1:2, :].broadcast_to([P, EB, L]),
                                          ALU.mult).then_inc(s_hc, 1)
                dve.wait_ge(s_acc, b * N + N + 1)
                dve.wait_ge(s_z, b + 1)
                dve.tensor_tensor(gate[:], gate[:], ps_y[:], ALU.mult).then_inc(s_yz, 1)
                ch.n += 1
                for t in range(TB):
                    dve.wait_ge(s_yt, b * TB + t + 1)
                    at = X[:, bass.ds(b * TB + t, 1), :]
                    last = dve.tensor_tensor(at, at, ps_w[:, t:t + 1, :], ALU.add)
                last.then_inc(s_add, 1)
                dve.sem_inc(s_c, 1)
                assert ch.n == PER


def transpose_norm(chip, name, xnT):
    XN, ident = chip.XN, chip.ident
    with ExitStack() as st:
        pt = chip.ps(name + "_pt", [P, 8, BANK], F32, st)
        s_t, s_a, s_d = chip.sem(name + "_t"), chip.sem(name + "_act"), chip.sem(name + "_dve")
        block = st.enter_context(chip.nc.Block())
        width = xnT.shape[1]

        @block.tensor
        def _(pe):
            for t in range(NT):
                for g in range(1):
                    if t >= 8:
                        pe.wait_ge((s_a, s_d)[t % 2], (t - 8) // 2 + 1)
                    for k in range(width):
                        m = pe.transpose(pt[:, t % 8, k * P:(k + 1) * P], XN[:, t, k * P:(k + 1) * P], ident[:])
                    m.then_inc(s_t, 1)

        @block.scalar
        def _(act):
            for t in range(0, NT, 2):
                act.wait_ge(s_t, t + 1)
                act.copy(xnT[:, :, t * P:(t + 1) * P],
                         pt[:, t % 8, :].rearrange("p (k t) -> p k t", k=width)).then_inc(s_a, 1)

        @block.vector
        def _(dve):
            for t in range(1, NT, 2):
                dve.wait_ge(s_t, t + 1)
                dve.tensor_copy(xnT[:, :, t * P:(t + 1) * P],
                                pt[:, t % 8, :].rearrange("p (k t) -> p k t", k=width)).then_inc(s_d, 1)


def stage_ffn4(chip, name, gate_w, gate_s, up_w, up_s, down_w, down_s):
    nc, X, XN, ident = chip.nc, chip.X, chip.XN, chip.ident
    F = gate_w.shape[0]
    G = F // 512
    R = 4
    NM = 3
    BLK = 512 // (gate_s.shape[1])
    NS = 512 // BLK
    SLOTS = 16
    with ExitStack() as st:
        def sb(n, shape, dt=F32):
            return chip.sb(f"{name}_{n}", shape, dt, st)

        def sem(n):
            return chip.sem(f"{name}_{n}")

        xnT = sb("xnT", [P, KD, B * L])
        transpose_norm(chip, name + "_xnT", xnT)
        pk = [sb(f"packed{m}", [P, R, 256], I32) for m in range(NM)]
        sc = [sb(f"scales{m}", [P, R, NS]) for m in range(NM)]
        code = [sb(f"code{i}", [P, R, 256], I32) for i in range(2)]
        sign = [sb(f"sign{i}", [P, R, 256], I32) for i in range(2)]
        mag = [sb(f"mag{i}", [P, R, 256]) for i in range(2)]
        sgn = [s[:].bitcast(F32) for s in sign]
        sgs = sb("signed_scale", [P, R, 256])
        V = [XN[:, m * R:(m + 1) * R, :] for m in range(NM)]
        WT = [[sb(f"wT{i}_{m}", [P, R, 512]) for m in range(NM)] for i in range(2)]
        gel = [XN[:, NM * R + i, :] for i in range(2)]
        inter = [XN[:, NM * R + 2 + i, :] for i in range(2)]
        ps_acc = chip.ps(name + "_acc", [P, TB, D], F32, st)
        ps_g, ps_u = chip.ps(name + "_g", [P, 512], F32, st), chip.ps(name + "_u", [P, 512], F32, st)
        ps_t = chip.ps(name + "_t", [P, 2, 512], F32, st)

        s_pk = [sem(f"packed{m}") for m in range(NM)]
        s_code, s_sgn, s_mag, s_sgs, s_pc, s_V = sem("code"), sem("sgn"), sem("mag"), sem("sgs"), sem("pool"), sem("V")
        s_t, s_wt = sem("transposed"), sem("wT")
        s_g, s_u, s_gel, s_int, s_dn = sem("gate"), sem("up"), sem("gelu"), sem("inter"), sem("down")
        s_fold, s_dc = sem("folded"), sem("dve_chain")
        block = st.enter_context(nc.Block())


        @block.sync
        def _(sp):
            def load(g, first=False):
                for m, (w, s) in enumerate(((gate_w, gate_s), (up_w, up_s), (down_w, down_s))):
                    at = bass.ds(g * 512, 512), bass.ds(g * 256, 256), bass.ds(g * NS, NS)
                    src, ssrc = (w[at[0], :], s[at[0], :]) if m < 2 else (w[:, at[1]], s[:, at[2]])
                    if not first:
                        sp.wait_ge(s_V, (g - 1) * 6 + 2 * m + 4)
                    sp.dma_start(pk[m][:], src.rearrange("(r p) c -> p r c", p=P)).then_inc(s_pk[m], 16)
                    sp.dma_start(sc[m][:], ssrc.rearrange("(r p) c -> p r c", p=P)).then_inc(s_pk[m], 16)

            load(0, first=True)
            with sp.Fori(1, G) as g:
                load(g)

        def dve_decode(dve, g, step):
            m, nib, op = step // 12, step // 6 % 2, step % 6
            unit, i = g * 6 + m * 2 + nib, nib
            if op == 0:
                dve.wait_ge(s_pk[m], 32 * (g + 1))
                dve.wait_ge(s_V, unit + 1)
                dve.tensor_scalar(code[i][:], pk[m][:], 4 * nib, 7, ALU.logical_shift_right,
                                  ALU.bitwise_and).then_inc(s_code, 1)
            elif op == 1:
                dve.tensor_scalar(sign[i][:], pk[m][:], 4 * nib, 8, ALU.logical_shift_right,
                                  ALU.bitwise_and).then_inc(s_code, 1)
            elif op == 2:
                dve.wait_ge(s_code, 2 * unit + 2)
                dve.tensor_scalar(sgn[i], sign[i][:], -0.25, 1.0, ALU.mult, ALU.add).then_inc(s_sgn, 1)
            elif op == 3:
                dve.tensor_scalar(mag[i][:], code[i][:], 2.0, -8.0, ALU.mult, ALU.add).then_inc(s_mag, 1)
            elif op == 4:
                dve.wait_ge(s_mag, 3 * unit + 1)
                dve.scalar_tensor_tensor(out=mag[i][:], in0=code[i][:], scalar=-2.0, in1=mag[i][:],
                                         op0=ALU.add, op1=ALU.max).then_inc(s_mag, 1)
            else:
                dve.wait_ge(s_mag, 3 * unit + 2)
                dve.scalar_tensor_tensor(out=mag[i][:], in0=code[i][:], scalar=0.5, in1=mag[i][:],
                                         op0=ALU.mult, op1=ALU.max).then_inc(s_mag, 1)

        def pe_transposes(pe, g, m, r):
            n = g * 12 + m * 4 + r
            pe.wait_ge(s_V, g * 6 + 2 * m + 4)
            pe.wait_ge(s_wt, n + 1)
            for k in range(4):
                t = pe.transpose(ps_t[:, r % 2, k * P:(k + 1) * P], V[m][:, r, k * P:(k + 1) * P], ident[:])
            t.then_inc(s_t, 1)

        def act_wT(act, g, gb, m, r):
            n = g * 12 + m * 4 + r
            act.wait_ge(s_t, n + 1)
            act.copy(WT[gb][m][:, :, r * P:(r + 1) * P],
                     ps_t[:, r % 2, :].rearrange("p (k c) -> p k c", k=4)).then_inc(s_wt, 1)

        @block.tensor
        def _(pe):
            pe.sem_inc(s_dn, 2)

            def down(g, gb, q):
                n = g * SLOTS + q
                pe.wait_ge(s_int, n + 2)
                if q % 4 == 0:
                    pe.wait_ge(s_fold, g * 4 + q // 4 + 1)
                for t in range(TB):
                    m = pe.matmul(ps_acc[:, t, :], inter[q % 2][:, t * P:(t + 1) * P], WT[gb][2][:, q % 4, :],
                                  start=(q % 4 == 0), stop=(q % 4 == 3))
                m.then_inc(s_dn, 1)

            def group(g, gb, prepare):
                pe.wait_ge(s_wt, g * 12 + 12 + 2)
                for q in range(SLOTS):
                    tc, nt = q // 4, q % 4
                    n = g * SLOTS + q
                    cols = slice(nt * P, (nt + 1) * P)
                    toks = slice(tc * 512, (tc + 1) * 512)
                    pe.wait_ge(s_gel, n + 1)
                    for k in range(KD):
                        m = pe.matmul(ps_g[:], WT[gb][0][:, k, cols], xnT[:, k, toks],
                                      start=(k == 0), stop=(k == KD - 1))
                    m.then_inc(s_g, 1)
                    if prepare and q >= 4:
                        pe_transposes(pe, g + 1, (q - 4) // 4, q % 4)
                    pe.wait_ge(s_int, n + 1)
                    for k in range(KD):
                        m = pe.matmul(ps_u[:], WT[gb][1][:, k, cols], xnT[:, k, toks],
                                      start=(k == 0), stop=(k == KD - 1))
                    m.then_inc(s_u, 1)
                    if q:
                        down(g, gb, q - 1)
                down(g, gb, SLOTS - 1)

            for m in range(NM):
                for r in range(R):
                    pe_transposes(pe, 0, m, r)
            with pe.Fori(0, G // 2 - 1) as h:
                group(h * 2, 0, True)
                group(h * 2 + 1, 1, True)
            group(G - 2, 0, True)
            group(G - 1, 1, False)

        @block.scalar
        def _(act):
            act.sem_inc(s_gel, 1)
            act.sem_inc(s_wt, 2)

            def group(g, gb, prepare):
                for q in range(SLOTS):
                    n = g * SLOTS + q
                    act.wait_ge(s_g, n + 1)
                    act.wait_ge(s_int, n + 1)
                    act.activation(gel[q % 2], ps_g[:], ACT.Gelu_apprx_tanh).then_inc(s_gel, 1)
                    if prepare and q >= 4:
                        if q == 4:
                            act.wait_ge(s_dn, g * SLOTS + 2)
                        act_wT(act, g + 1, 1 - gb, (q - 4) // 4, q % 4)

            for m in range(NM):
                for r in range(R):
                    act_wT(act, 0, 0, m, r)
            with act.Fori(0, G // 2 - 1) as h:
                group(h * 2, 0, True)
                group(h * 2 + 1, 1, True)
            group(G - 2, 0, True)
            group(G - 1, 1, False)

        @block.gpsimd
        def _(pool):
            pool.sem_inc(s_V, 2)

            def unit(g, m, nib, first):
                n = g * 6 + m * 2 + nib
                i = nib
                pool.wait_ge(s_sgn, n + 1)
                pool.wait_ge(s_V, n + 2)
                v, sg = (x.rearrange("p r (s c) -> p (r s) c", c=BLK // 2) for x in (sgs[:], sgn[i]))
                pool.tensor_tensor(v, sg, sc[m][:].rearrange("p r (s o) -> p (r s) o", o=1).broadcast_to(
                    [P, R * NS, BLK // 2]), ALU.mult).then_inc(s_pc, 1)
                pool.wait_ge(s_pc, n + 1)
                pool.wait_ge(s_mag, 3 * n + 3)
                if nib == 0:
                    if not first:
                        pool.wait_ge(s_t, (g - 1) * 12 + m * 4 + 4)
                dst = V[m].rearrange("p r (c two) -> p r c two", two=2)[:, :, :, nib]
                pool.tensor_tensor(dst, mag[i][:], sgs[:], ALU.mult).then_inc(s_V, 1)

            def decode(g, first=False):
                for m in range(NM):
                    for nib in range(2):
                        unit(g, m, nib, first)

            decode(0, first=True)
            with pool.Fori(1, G) as g:
                decode(g)

        @block.vector
        def _(dve):
            dve.sem_inc(s_int, 1)
            dve.sem_inc(s_fold, 1)

            def fold(g, tc):
                dve.wait_ge(s_dn, g * SLOTS + 4 * tc + 4 + 2)
                x = X[:, tc * TB:(tc + 1) * TB, :]
                if tc == 0:
                    dve.wait_ge(s_fold, g * 4 + 1)
                dve.tensor_tensor(x, x, ps_acc[:], ALU.add).then_inc(s_fold, 1)

            def group(g, gb, prepare):
                for q in range(SLOTS):
                    n = g * SLOTS + q
                    dve.wait_ge(s_u, n + 1)
                    dve.wait_ge(s_gel, n + 2)
                    dve.wait_ge(s_dn, n + 1)
                    dve.tensor_tensor(inter[q % 2], gel[q % 2], ps_u[:], ALU.mult).then_inc(s_int, 1)
                    if prepare and q < 9:
                        for s in range(4 * q, 4 * q + 4):
                            dve_decode(dve, g + 1, s)
                    if q % 4 == 0 and q:
                        fold(g, q // 4 - 1)
                fold(g, 3)

            for s in range(36):
                dve_decode(dve, 0, s)
            with dve.Fori(0, G // 2 - 1) as h:
                group(h * 2, 0, True)
                group(h * 2 + 1, 1, True)
            group(G - 2, 0, True)
            group(G - 1, 1, False)


def stage_mix(chip, name, wq, bq, wk, bk):
    nc, X, XN, ctxT, ident = chip.nc, chip.X, chip.XN, chip.ctxT, chip.ident
    DH = wq.shape[0]
    with ExitStack() as st:
        def sb(n, shape, dt=F32):
            return chip.sb(f"{name}_{n}", shape, dt, st)

        def sem(n):
            return chip.sem(f"{name}_{n}")

        w_rows, wT, bias = sb("w_rows", [DH, 2, C]), sb("wT", [P, 2, KC, DH]), sb("bias", [DH, 2])
        qkT = sb("qkT", [DH, 2, L])
        rows = sb("rows", [P, TB, D])
        top, tot, inv = sb("top", [P, TB]), sb("tot", [P, TB]), sb("inv", [P, TB])
        att = sb("att", [P, TB, L])
        xT, aT = sb("xT", [P, TB, L]), sb("aT", [P, TB, L])
        ps_e = chip.ps(name + "_e", [P, TB, L], F32, st)
        ps_t, ps_o = chip.ps(name + "_t", [P, 2, 512], F32, st), chip.ps(name + "_o", [P, 2, 512], F32, st)
        s_ld, s_w, s_wc = sem("loaded"), sem("wT"), sem("wT_copied")
        s_qk, s_qc, s_e, s_top, s_exp, s_inv, s_att = (sem(n) for n in (
            "qk", "qk_copied", "energy", "top", "exp", "inverse", "attention"))
        s_rows, s_t, s_tc, s_o, s_f = (sem(n) for n in ("rows", "t", "t_copied", "out", "folded"))
        block = st.enter_context(nc.Block())

        @block.sync
        def _(sp):
            for i, (w, v) in enumerate(((wq, bq), (wk, bk))):
                sp.dma_start(w_rows[:, i, :], w).then_inc(s_ld, 16)
                sp.dma_start(bias[:, i:i + 1], v.rearrange("(p o) -> p o", o=1)).then_inc(s_ld, 16)

        @block.gpsimd
        def _(pool):
            with pool.Fori(0, B) as b:
                pool.wait_ge(s_t, b * 8 + 1)
                pool.tensor_copy(rows[:], XN[:, bass.ds(b * TB, TB), :]).then_inc(s_rows, 1)

        @block.tensor
        def _(pe):
            pe.sem_inc(s_t, 1)
            pe.wait_ge(s_ld, 64)
            for i in range(2):
                for k in range(KC):
                    t = pe.transpose(ps_t[:, 0, (2 * i + k) * DH:(2 * i + k + 1) * DH],
                                     w_rows[:, i, k * P:(k + 1) * P], ident[:])
            t.then_inc(s_w, 1)
            pe.wait_ge(s_wc, 1)

            def turn(b, i, src):
                n = b * 8 + i
                pe.wait_ge(s_tc, n + 1)
                for c in range(TB):
                    t = pe.transpose(ps_t[:, i % 2, c * P:(c + 1) * P], src[:, i % TB, c * P:(c + 1) * P], ident[:])
                t.then_inc(s_t, 1)

            with pe.Fori(0, B) as b:
                pe.wait_ge(s_f, b * TB + 2)
                for i in range(2):
                    for k in range(KC):
                        m = pe.matmul(ps_o[:, i, :], wT[:, i, k, :], ctxT[:, k, bass.ds(b * L, L)],
                                      start=(k == 0), stop=(k == KC - 1))
                    m.then_inc(s_qk, 1)
                pe.wait_ge(s_qc, b * 2 + 2)
                for r in range(TB):
                    pe.matmul(ps_e[:, r, :], qkT[:, 0, r * P:(r + 1) * P], qkT[:, 1, :],
                              start=True, stop=True).then_inc(s_e, 1)
                pe.wait_ge(s_rows, b + 1)
                for i in range(TB):
                    turn(b, i, rows)
                for r in range(TB):
                    pe.wait_ge(s_att, b * TB + r + 1)
                    turn(b, TB + r, att)
                pe.wait_ge(s_tc, b * 8 + 8 + 2)
                for l in range(TB):
                    pe.wait_ge(s_f, b * TB + l + 1)
                    for c in range(TB):
                        m = pe.matmul(ps_o[:, l % 2, :], xT[:, c, l * P:(l + 1) * P], aT[:, c, :],
                                      start=(c == 0), stop=(c == TB - 1))
                    m.then_inc(s_o, 1)

        @block.scalar
        def _(act):
            act.sem_inc(s_tc, 2)
            act.wait_ge(s_w, 1)
            act.copy(wT[:].rearrange("p i k d -> p (i k d)"), ps_t[:, 0, 0:4 * DH]).then_inc(s_wc, 1)
            with act.Fori(0, B) as b:
                for i in range(2):
                    act.wait_ge(s_qk, b * 2 + i + 1)
                    act.activation(qkT[:, i, :], ps_o[:, i, :], ACT.Identity, bias=bias[:, i:i + 1]).then_inc(s_qc, 1)
                for r in range(TB):
                    act.wait_ge(s_top, b * TB + r + 1)
                    act.activation(att[:, r, :], ps_e[:, r, :], ACT.Exp, bias=top[:, r:r + 1],
                                   accum_out=tot[:, r:r + 1]).then_inc(s_exp, 1)
                for i in range(8):
                    act.wait_ge(s_t, b * 8 + i + 2)
                    dst = xT if i < TB else aT
                    act.copy(dst[:, :, i % TB * P:(i % TB + 1) * P],
                             ps_t[:, i % 2, :].rearrange("p (c t) -> p c t", c=TB)).then_inc(s_tc, 1)

        @block.vector
        def _(dve):
            dve.sem_inc(s_f, 2)
            with dve.Fori(0, B) as b:
                for r in range(TB):
                    dve.wait_ge(s_e, b * TB + r + 1)
                    dve.tensor_reduce(top[:, r:r + 1], ps_e[:, r, :], AX.X, ALU.max, negate=True).then_inc(s_top, 1)
                for r in range(TB):
                    dve.wait_ge(s_exp, b * TB + r + 1)
                    dve.reciprocal(inv[:, r:r + 1], tot[:, r:r + 1]).then_inc(s_inv, 1)
                    dve.wait_ge(s_inv, b * TB + r + 1)
                    dve.tensor_scalar(att[:, r, :], att[:, r, :], inv[:, r:r + 1], None, ALU.mult).then_inc(s_att, 1)
                for l in range(TB):
                    dve.wait_ge(s_o, b * TB + l + 1)
                    x = X[:, bass.ds(b * TB + l, 1), :].rearrange("p o d -> p (o d)")
                    dve.tensor_tensor(x, x, ps_o[:, l % 2, :], ALU.add).then_inc(s_f, 1)


class Heads:

    def __init__(self, nc, name, hd, k_heads, chunks, causal):
        self.H, self.hd, self.KH, self.chunks, self.causal = 16, hd, k_heads, chunks, causal
        self.U = B * (D // hd) // self.H
        self.VH = k_heads
        self.scale = float(hd) ** -0.5
        self.ROWS = len(chunks[0]) * hd
        assert self.ROWS + 2 <= P
        self.q = nc.dram_tensor(name + "_q_parts", (self.U, 3, self.H * hd, L), BF16).ap()
        self.k = nc.dram_tensor(name + "_k_parts", (self.U, 3, self.KH * hd, L), BF16).ap()
        self.v = nc.dram_tensor(name + "_v", (self.U, P, TB, self.VH * (hd + 1)), F32).ap()
        self.m = nc.dram_tensor(name + "_max", (self.U, 2, 2, self.H // 2, L), BF16).ap()


def attention_core(chip, name, hs, add):
    nc, X, XN, identb = chip.nc, chip.X, chip.XN, chip.identb
    U, H, hd, KH, NCH, ROWS = hs.U, hs.H, hs.hd, hs.KH, len(hs.chunks), hs.ROWS
    V = hd + 1
    HH = H // 2
    NB = 3
    UB = U // B
    dst = X if add else XN
    with ExitStack() as st:
        def sb(n, shape, dt=F32):
            return chip.sb(f"{name}_{n}", shape, dt, st)

        def sem(n):
            return chip.sem(f"{name}_{n}")

        R0 = ROWS + 2
        qS = [[sb(f"q{i}_{c}", [R0 if c == 0 else ROWS, H, L], BF16) for c in range(NCH)] for i in range(NB)]
        kS = [[sb(f"k{i}_{c}", [R0 if c == 0 else ROWS, KH, L], BF16) for c in range(NCH)] for i in range(NB)]
        vS = [sb(f"v{i}", [P, TB, KH * V]) for i in range(NB)]
        prob = [sb(f"prob{i}", [P, 2, L]) for i in range(2)]
        mx = [sb(f"minus_max{i}", [P, TB, H]) for i in range(2)]
        mh = [sb(f"max_parts{i}", [P, TB, 2, HH], BF16) for i in range(2)]
        mrow = [sb(f"max_rows{i}", [2 * HH, L], BF16) for i in range(2)]
        inv = [sb(f"inv{i}", [P, TB, 1]) for i in range(2)]
        y = [sb(f"y{i}", [P, TB, hd]) for i in range(2)]
        maskA, maskB = sb("mask_q", [P, P], BF16), sb("mask_k", [P, P], BF16)
        ps_a = chip.ps(name + "_a", [P, 2, 512], F32, st)
        ps_s = [chip.ps(f"{name}_s{i}", [P, 2, 512], F32, st) for i in range(2)]
        ps_v = [chip.ps(f"{name}_pv{i}", [P, 512], F32, st)[:, 0:TB * V].rearrange("p (q v) -> p q v", q=TB)
                for i in range(2)]
        ps_m = ps_a[0:2 * HH, 0, 0:TB * P // 2].bitcast(BF16).rearrange("p (q t) -> p q t", q=TB)

        s_in = [sem(f"stack{i}") for i in range(NB)]
        s_one, s_mask = sem("ones"), sem("mask")
        s_a, s_red, s_qk, s_exp, s_pv, s_norm, s_inv = (sem(n) for n in (
            "a", "reduced", "qk", "exp", "pv", "normalised", "inverse"))
        s_mh, s_mt, s_mc, s_ms, s_ml = (sem(n) for n in ("m_parts", "m_turned", "m_copied", "m_stored", "m_loaded"))
        s_sp = sem("m_high")
        block = st.enter_context(nc.Block())
        NIN = 2 * sum(len(c) for c in hs.chunks) + 1

        @block.sync
        def _(sp):
            def load(u):
                i = u % NB
                if u >= NB:
                    sp.wait_ge(s_pv, 2 * H * (u - NB + 1) + 2)
                for c, pairs in enumerate(hs.chunks):
                    for j, (qp, kp) in enumerate(pairs):
                        rows = slice(j * hd, (j + 1) * hd)
                        sp.dma_start(qS[i][c][rows], hs.q[u, qp].rearrange("(h d) t -> d h t", d=hd)
                                     ).then_inc(s_in[i], 16)
                        sp.dma_start(kS[i][c][rows], hs.k[u, kp].rearrange("(h d) t -> d h t", d=hd)
                                     ).then_inc(s_in[i], 16)
                sp.dma_start(vS[i][:], hs.v[u]).then_inc(s_in[i], 16)

            def max_rows(u, hh):
                n = 2 * u + hh
                sp.wait_ge(s_mc, n + 1)
                sp.dma_start(hs.m[u, hh].rearrange("a h t -> (a h) t"), mrow[hh][:]).then_inc(s_ms, 16)
                sp.wait_ge(s_ms, 16 * (n + 1))
                sp.dma_start(qS[u % NB][0][ROWS:R0, hh * HH:(hh + 1) * HH, :], hs.m[u, hh]).then_inc(s_ml, 16)

            for u in range(NB):
                load(u)
            for u in range(U):
                max_rows(u, 0)
                max_rows(u, 1)
                if u + NB - 1 < U and u >= 1:
                    load(u + NB - 1)

        @block.gpsimd
        def _(pool):
            for i in range(NB):
                pool.memset(kS[i][0][ROWS:R0], 1.0).then_inc(s_one, 1)
            pool.wait_ge(s_one, NB)
            if hs.causal:
                pool.memset(maskA[:], 0.0).then_inc(s_mask, 1)
                pool.memset(maskB[:], 0.0).then_inc(s_mask, 1)
                pool.wait_ge(s_mask, 2)
                pool.affine_select(out=maskA[:], in_=maskA[:], compare_op=ALU.is_ge, fill=-1e30, base=0,
                                   pattern=[[-1, P]], channel_multiplier=1).then_inc(s_mask, 1)
                pool.affine_select(out=maskB[:], in_=maskB[:], compare_op=ALU.is_ge, fill=-1e30, base=0,
                                   pattern=[[1, P]], channel_multiplier=-1).then_inc(s_mask, 1)

        @block.tensor
        def _(pe):
            def logits(out, lhs, rhs, cols, mask, diag, rows0):
                for c in range(NCH):
                    k = rows0 if c == 0 else ROWS
                    pe_last = pe.matmul(out[:, cols], lhs(c, k), rhs(c, k), start=(c == 0),
                                        stop=(c == NCH - 1 and not hs.causal))
                if hs.causal:
                    pe_last = pe.matmul(out[:, diag], identb[:], mask[:], start=False, stop=True)
                return pe_last

            turned = [0]

            def A(u, h, half):
                n2, i = (u * H + h) * 2 + half, u % NB
                if turned[0]:
                    pe.wait_ge(s_mc, turned[0])
                pe.wait_ge(s_red, n2 + 1)
                if half == 0:
                    pe.wait_ge(s_in[i], 16 * NIN * (u // NB + 1))
                for j in range(2):
                    qt = 2 * half + j
                    n = (qt + 1) * P if hs.causal else L
                    kh = h if KH > 1 else 0
                    m = logits(ps_a[:, j, :],
                               lambda c, k: qS[i][c][0:k, bass.ds(h, 1), qt * P:(qt + 1) * P].rearrange("p o t -> p (o t)"),
                               lambda c, k: kS[i][c][0:k, bass.ds(kh, 1), 0:n].rearrange("p o t -> p (o t)"),
                               slice(0, n), maskA, slice(qt * P, (qt + 1) * P), ROWS)
                m.then_inc(s_a, 1)

            def QK(u, h, pair):
                m2, i = (u * H + h) * 2 + pair, u % NB
                pe.wait_ge(s_exp, m2 + 1)
                for j in range(2):
                    kt = 2 * pair + j
                    q0 = kt * P if hs.causal else 0
                    kh = h if KH > 1 else 0
                    m = logits(ps_s[pair][:, j, :],
                               lambda c, k: kS[i][c][0:k, bass.ds(kh, 1), kt * P:(kt + 1) * P].rearrange("p o t -> p (o t)"),
                               lambda c, k: qS[i][c][0:k, bass.ds(h, 1), q0:L].rearrange("p o t -> p (o t)"),
                               slice(q0, L), maskB, slice(kt * P, (kt + 1) * P), R0)
                m.then_inc(s_qk, 1)

            def PV(u, h, pair, e):
                n, i = u * H + h, u % NB
                pe.wait_ge(s_exp, 2 * n + pair + 3)
                if pair == 0:
                    pe.wait_ge(s_norm, n + 1)
                for j in range(2):
                    kt = 2 * pair + j
                    for qt in range(kt if hs.causal else 0, TB):
                        v = vS[i][:, kt, bass.ds(h * V if KH > 1 else 0, V)]
                        m = pe.matmul(ps_v[e][:, qt, :], prob[pair][:, j, qt * P:(qt + 1) * P], v,
                                      start=(kt == 0 and qt == 0), stop=True, skip_group_check=True)
                m.then_inc(s_pv, 1)

            def pair_of_heads(u, h, first=False):
                a, b = u + 1 < U, u >= 0
                if b and first:
                    pe.wait_ge(s_ml, 16 * (2 * u + (h // HH) + 1))
                if b:
                    QK(u, h, 0)
                if a:
                    A(u + 1, h, 0)
                if b:
                    QK(u, h, 1)
                    PV(u, h, 0, 0)
                    QK(u, h + 1, 0)
                    PV(u, h, 1, 0)
                if a:
                    A(u + 1, h, 1)
                if b:
                    QK(u, h + 1, 1)
                    PV(u, h + 1, 0, 1)
                if a:
                    A(u + 1, h + 1, 0)
                if b:
                    PV(u, h + 1, 1, 1)
                if a:
                    A(u + 1, h + 1, 1)

            def turn_max(n, reduced):
                pe.wait_ge(s_mh, n + 1)
                pe.wait_ge(s_red, reduced)
                for qt in range(TB):
                    m = pe.transpose(ps_m[:, qt, :], mh[n % 2][:, qt].rearrange("p a h -> p (a h)"), identb[:])
                m.then_inc(s_mt, 1)

            pe.sem_inc(s_pv, 2)
            pe.wait_ge(s_one, NB)
            if hs.causal:
                pe.wait_ge(s_mask, 4)
            for u in range(-1, U):
                for hh in range(2):
                    pair_of_heads(u, hh * HH, True)
                    n = 2 * u + 1 + hh
                    if 0 <= n < 2 * U:
                        turn_max(n, 2 * HH * (n + 1) + 1 + (4 if u + 1 < U else 0))
                        turned[0] = n + 1
                    with pe.Fori(1, HH // 2) as i:
                        pair_of_heads(u, i * 2 + hh * HH)

        @block.scalar
        def _(act):
            def exp(u, h, pair):
                m2 = (u * H + h) * 2 + pair
                act.wait_ge(s_qk, m2 + 1)
                act.wait_ge(s_pv, m2 + 1)
                if hs.causal:
                    for j in range(2):
                        q0 = (2 * pair + j) * P
                        last = act.activation(prob[pair][:, j, q0:], ps_s[pair][:, j, q0:], ACT.Exp, scale=hs.scale)
                else:
                    last = act.activation(prob[pair][:], ps_s[pair][:], ACT.Exp, scale=hs.scale)
                last.then_inc(s_exp, 1)

            def pair_of_heads(u, h):
                if u >= 0:
                    for e in range(2):
                        for pair in range(2):
                            exp(u, h + e, pair)

            def copy_max(n):
                act.wait_ge(s_mt, n + 1)
                if n >= 2:
                    act.wait_ge(s_ms, 16 * (n - 1))
                act.copy(mrow[n % 2][:], ps_m.rearrange("p q t -> p (q t)")).then_inc(s_mc, 1)

            act.sem_inc(s_exp, 2)
            for u in range(-1, U):
                for hh in range(2):
                    pair_of_heads(u, hh * HH)
                    n = 2 * u + 1 + hh
                    if 0 <= n < 2 * U:
                        copy_max(n)
                    if u >= 0:
                        with act.Fori(1, HH // 2) as i:
                            pair_of_heads(u, i * 2 + hh * HH)

        @block.vector
        def _(dve):
            dve.sem_inc(s_red, 1)
            dve.sem_inc(s_norm, 2)

            def red(u, h, half):
                n2 = (u * H + h) * 2 + half
                dve.wait_ge(s_a, n2 + 1)
                out = mx[u % 2][:, 2 * half:2 * half + 2, bass.ds(h, 1)]
                if hs.causal:
                    for j in range(2):
                        n = (2 * half + j + 1) * P
                        last = dve.tensor_reduce(out[:, j], ps_a[:, j, 0:n], AX.X, ALU.max, negate=True)
                else:
                    last = dve.tensor_reduce(out.rearrange("p q o -> p (q o)"), ps_a[:], AX.X, ALU.max, negate=True)
                last.then_inc(s_red, 1)

            def norm(u, h, e):
                n, b = u * H + h, u // UB
                dve.wait_ge(s_pv, 2 * n + 4)
                dve.reciprocal(inv[e][:], ps_v[e][:, :, hd:V]).then_inc(s_inv, 1)
                dve.wait_ge(s_inv, (2 if add else 1) * n + 1)
                cols = bass.ds((u % UB) * H * hd + h * hd, hd)
                out = dst[:, b * TB:(b + 1) * TB, cols]
                f = inv[e][:].broadcast_to([P, TB, hd])
                if add:
                    dve.tensor_tensor(y[e][:], ps_v[e][:, :, 0:hd], f, ALU.mult).then_inc(s_inv, 1)
                    dve.wait_ge(s_inv, 2 * n + 2)
                    dve.tensor_tensor(out, out, y[e][:], ALU.add).then_inc(s_norm, 1)
                else:
                    dve.tensor_tensor(out, ps_v[e][:, :, 0:hd], f, ALU.mult).then_inc(s_norm, 1)

            def pair_of_heads(u, h):
                a, b = u + 1 < U, u >= 0
                if a:
                    red(u + 1, h, 0)
                if b:
                    norm(u, h, 0)
                if a:
                    red(u + 1, h, 1)
                    red(u + 1, h + 1, 0)
                if b:
                    norm(u, h + 1, 1)
                if a:
                    red(u + 1, h + 1, 1)

            def split_max(n):
                u, hh = n // 2, n % 2
                m = mx[u % 2][:, :, hh * HH:(hh + 1) * HH]
                dve.wait_ge(s_red, 2 * HH * (n + 1) + 1)
                if n >= 2:
                    dve.wait_ge(s_mt, n - 1)
                dve.tensor_copy(mh[n % 2][:, :, 0, :], m).then_inc(s_sp, 1)
                dve.wait_ge(s_sp, n + 1)
                dve.tensor_tensor(mh[n % 2][:, :, 1, :], m, mh[n % 2][:, :, 0, :], ALU.subtract).then_inc(s_mh, 1)

            for u in range(-1, U):
                for hh in range(2):
                    pair_of_heads(u, hh * HH)
                    with dve.Fori(1, HH // 2) as i:
                        pair_of_heads(u, i * 2 + hh * HH)
                    if u + 1 < U:
                        split_max(2 * u + 2 + hh)


def rope_tables(chip, name, pos, freq, cosT, sinT):
    nc, ident = chip.nc, chip.ident
    PI = float(np.pi)
    C1 = 6.28125
    C2 = 2 * PI - C1
    with ExitStack() as st:
        def sb(n, shape, dt=F32):
            return chip.sb(f"{name}_{n}", shape, dt, st)

        def sem(n):
            return chip.sem(f"{name}_{n}")

        A = pos.shape[2]
        prow, posT, fr = sb("pos", [P, NT, A]), sb("posT", [A, B, L]), sb("freq", [A, P])
        ang, turns = sb("angle", [P, B, L]), sb("turns", [P, B, L])
        ps = chip.ps(name + "_ps", [P, B, L], F32, st)
        s_ld, s_t, s_pc, s_a, s_ac, s_c, s_r = (sem(n) for n in ("ld", "t", "pos", "angle", "ac", "chain", "reduced"))
        s_sin = sem("sin")
        block = st.enter_context(nc.Block())

        @block.sync
        def _(sp):
            sp.dma_start(prow[:], pos.rearrange("b (t p) a -> p (b t) a", p=P)).then_inc(s_ld, 16)
            sp.dma_start(fr[:], freq).then_inc(s_ld, 16)

        @block.tensor
        def _(pe):
            pe.wait_ge(s_ld, 32)
            for t in range(NT):
                m = pe.transpose(ps[0:A, t // TB, t % TB * P:(t % TB + 1) * P], prow[:, t, :], ident[:])
            m.then_inc(s_t, 1)
            pe.wait_ge(s_pc, 1)
            for b in range(B):
                m = pe.matmul(ps[:, b, :], fr[:], posT[:, b, :], start=True, stop=True)
            m.then_inc(s_a, 1)

        @block.scalar
        def _(act):
            act.wait_ge(s_t, 1)
            act.copy(posT[:], ps[0:A]).then_inc(s_pc, 1)
            for i, out in enumerate((sinT, cosT)):
                act.wait_ge(s_r, i + 1)
                act.activation(out[:], ang[:], ACT.Sin).then_inc(s_sin, 1)

        @block.vector
        def _(dve):
            ch = Chain(dve, s_c)
            dve.wait_ge(s_a, 1)
            for i in range(2):
                if i:
                    dve.wait_ge(s_sin, 1)
                ch.step(dve.tensor_scalar(ang[:], ps[:], i * PI / 2, None, ALU.add))
                ch.step(dve.tensor_scalar(turns[:], ang[:], 1 / (2 * PI), MAGIC, ALU.mult, ALU.add))
                ch.step(dve.tensor_scalar(turns[:], turns[:], -MAGIC, None, ALU.add))
                ch.step(dve.scalar_tensor_tensor(out=ang[:], in0=turns[:], scalar=-C1, in1=ang[:],
                                                 op0=ALU.mult, op1=ALU.add))
                ch.step(dve.scalar_tensor_tensor(out=ang[:], in0=turns[:], scalar=-C2, in1=ang[:],
                                                 op0=ALU.mult, op1=ALU.add))
                dve.tensor_scalar(ang[:], ang[:], 3.1415925, -3.1415925, ALU.min, ALU.max).then_inc(s_r, 1)


def stage_attention(chip, name, hs, pos, freq, wq, wkv, wout, bout):
    nc, X, XN, ctxT, ident = chip.nc, chip.X, chip.XN, chip.ctxT, chip.ident
    V = hs.hd + 1
    NH = D // hs.hd
    with ExitStack() as st:
        def sb(n, shape, dt=F32, c=st):
            return chip.sb(f"{name}_{n}", shape, dt, c)

        def sem(n):
            return chip.sem(f"{name}_{n}")

        cosT, sinT = sb("cos", [P, B, L]), sb("sin", [P, B, L])
        rope_tables(chip, name + "_rope", pos, freq, cosT, sinT)
        xnT = sb("xnT", [P, KD, B * L])
        transpose_norm(chip, name + "_xnT", xnT)
        W = {"q": [sb(f"wq{i}", [P, KD, D]) for i in range(2)], "k": [sb(f"wk{i}", [P, KC, D]) for i in range(2)]}
        wv = sb("wv", [P, KC, D])
        ra = [sb(f"ra{i}", [P, L]) for i in range(2)]
        rb = [sb(f"rb{i}", [P, L]) for i in range(2)]
        parts = [sb(f"parts{i}", [P, 3, L], BF16) for i in range(2)]
        vrow = [sb(f"vrow{i}", [P, NH, V]) for i in range(2)]
        ps = chip.ps(name + "_ps", [P, 2, 2, 512], F32, st)
        ps_v = chip.ps(name + "_pv", [P, 2, 512], F32, st)
        s_w, s_sw, s_p, s_t1, s_t2, s_ro, s_p1, s_r1, s_p2, s_p3 = (sem(n) for n in (
            "w", "swapped", "product", "cosine", "sine", "turned", "part1", "rest1", "part2", "part3"))
        s_st = [sem(f"stored{i}") for i in range(2)]
        s_one, s_pv, s_vc = sem("ones"), sem("v"), sem("v_copied")
        s_vs = [sem(f"v_stored{i}") for i in range(2)]
        ITEMS = [(w, b, g) for b in range(B) for g in range(KD) for w in "qk"]
        block = st.enter_context(nc.Block())

        @block.sync
        def _(sp):
            sp.dma_start(W["q"][0][:], wq.rearrange("(k p) n -> p k n", p=P)).then_inc(s_w, 16)
            sp.dma_start(W["k"][0][:], wkv[:, 0:D].rearrange("(k p) n -> p k n", p=P)).then_inc(s_w, 16)
            sp.dma_start(wv[:], wkv[:, D:2 * D].rearrange("(k p) n -> p k n", p=P)).then_inc(s_w, 16)
            UB = hs.U // B
            for n, (w, b, g) in enumerate(ITEMS):
                sp.wait_ge(s_p3, n + 1)
                u, r = b * UB + g * UB // KD, g % (KD // UB) * P
                sp.dma_start((hs.q if w == "q" else hs.k)[u, :, r:r + P, :].rearrange("a p t -> p a t"),
                             parts[n % 2][:]).then_inc(s_st[n % 2], 16)
                if n % 2:
                    t = n // 2
                    sp.wait_ge(s_vc, t + 1)
                    for h in range(UB):
                        sp.dma_start(hs.v[t // TB * UB + h, :, t % TB, :],
                                     vrow[t % 2][:, h * hs.H:(h + 1) * hs.H, :].rearrange("p h d -> p (h d)")
                                     ).then_inc(s_vs[t % 2], 16)
            for i in range(2):
                sp.wait_ge(s_st[i], 16 * len(ITEMS) // 2)
                sp.wait_ge(s_vs[i], 16 * UB * NT // 2)

        @block.tensor
        def _(pe):
            pe.wait_ge(s_w, 48)
            pe.wait_ge(s_sw, 4)
            for n, (w, b, g) in enumerate(ITEMS):
                src, K = (xnT, KD) if w == "q" else (ctxT, KC)
                if n >= 2:
                    pe.wait_ge(s_t1, n - 1)
                    pe.wait_ge(s_t2, n - 1)
                for i in range(2):
                    for k in range(K):
                        m = pe.matmul(ps[:, n % 2, i, :], W[w][i][:, k, g * P:(g + 1) * P],
                                      src[:, k, b * L:(b + 1) * L], start=(k == 0), stop=(k == K - 1))
                m.then_inc(s_p, 1)
                if n % 2:
                    t = n // 2
                    if t >= 2:
                        pe.wait_ge(s_vc, t - 1)
                    for k in range(KC):
                        m = pe.matmul(ps_v[:, t % 2, :], ctxT[:, k, t * P:(t + 1) * P], wv[:, k, :],
                                      start=(k == 0), stop=(k == KC - 1))
                    m.then_inc(s_pv, 1)

        @block.vector
        def _(dve):
            dve.wait_ge(s_w, 48)
            for w in "qk":
                a, s = (x[:].rearrange("p k (n two) -> p k n two", two=2) for x in W[w])
                dve.tensor_scalar(s[:, :, :, 0], a[:, :, :, 1], -1.0, None, ALU.mult).then_inc(s_sw, 1)
                dve.tensor_copy(s[:, :, :, 1], a[:, :, :, 0]).then_inc(s_sw, 1)

            def last_part(n):
                dve.wait_ge(s_p2, n + 1)
                dve.tensor_tensor(parts[n % 2][:, 2, :], ra[n % 2][:], parts[n % 2][:, 1, :],
                                  ALU.subtract).then_inc(s_p3, 1)

            for n, (w, b, g) in enumerate(ITEMS):
                i = n % 2
                dve.wait_ge(s_p, n + 1)
                if n >= 2:
                    dve.wait_ge(s_p3, n - 1)
                    dve.wait_ge(s_r1, n - 1)
                dve.tensor_tensor(ra[i][:], ps[:, i, 0, :], cosT[:, b, :], ALU.mult).then_inc(s_t1, 1)
                dve.tensor_tensor(rb[i][:], ps[:, i, 1, :], sinT[:, b, :], ALU.mult).then_inc(s_t2, 1)
                if n:
                    last_part(n - 1)
            last_part(len(ITEMS) - 1)

        @block.gpsimd
        def _(pool):
            for i in range(2):
                pool.memset(vrow[i][:, :, hs.hd:V], 1.0).then_inc(s_one, 1)
            for n in range(len(ITEMS)):
                i = n % 2
                pool.wait_ge(s_t1, n + 1)
                pool.wait_ge(s_t2, n + 1)
                pool.tensor_tensor(rb[i][:], ra[i][:], rb[i][:], ALU.add).then_inc(s_ro, 1)
                pool.wait_ge(s_p1, n + 1)
                pool.tensor_tensor(ra[i][:], rb[i][:], parts[i][:, 0, :], ALU.subtract).then_inc(s_r1, 1)

        @block.scalar
        def _(act):
            act.wait_ge(s_one, 2)
            for n in range(len(ITEMS)):
                i = n % 2
                act.wait_ge(s_ro, n + 1)
                if n >= 2:
                    act.wait_ge(s_st[i], 16 * (n // 2))
                act.copy(parts[i][:, 0, :], rb[i][:]).then_inc(s_p1, 1)
                act.wait_ge(s_r1, n + 1)
                act.copy(parts[i][:, 1, :], ra[i][:]).then_inc(s_p2, 1)
                if n % 2:
                    t = n // 2
                    act.wait_ge(s_pv, t + 1)
                    if t >= 2:
                        act.wait_ge(s_vs[t % 2], 16 * (hs.U // B) * (t // 2))
                    act.copy(vrow[t % 2][:, :, 0:hs.hd],
                             ps_v[:, t % 2, :].rearrange("p (h d) -> p h d", d=hs.hd)).then_inc(s_vc, 1)

    attention_core(chip, name + "_core", hs, add=False)
    out_projection(chip, name + "_out", wout, bout)


def out_projection(chip, name, wout, bout):
    nc, X = chip.nc, chip.X
    with ExitStack() as st:
        aT = chip.sb(name + "_aT", [P, KD, B * L], F32, st)
        transpose_norm(chip, name + "_aT", aT)
        w, bias = chip.sb(name + "_w", [P, KD, D], F32, st), chip.sb(name + "_bias", [P, D], F32, st)
        ps = chip.ps(name + "_ps", [P, 4, 512], F32, st)
        s_w, s_o, s_b, s_f = (chip.sem(f"{name}_{n}") for n in ("w", "product", "biased", "folded"))
        block = st.enter_context(nc.Block())

        @block.sync
        def _(sp):
            sp.dma_start(w[:], wout.rearrange("(k p) n -> p k n", p=P)).then_inc(s_w, 16)
            sp.dma_start(bias[:], bout.rearrange("(o n) -> o n", o=1).broadcast_to([P, D])).then_inc(s_w, 16)

        @block.tensor
        def _(pe):
            pe.wait_ge(s_w, 32)
            for t in range(NT):
                if t >= 4:
                    pe.wait_ge(s_f, t - 3)
                for k in range(KD):
                    m = pe.matmul(ps[:, t % 4, :], aT[:, k, t * P:(t + 1) * P], w[:, k, :],
                                  start=(k == 0), stop=(k == KD - 1))
                m.then_inc(s_o, 1)

        @block.gpsimd
        def _(pool):
            pool.wait_ge(s_w, 32)
            for t in range(NT):
                pool.tensor_tensor(X[:, t, :], X[:, t, :], bias[:], ALU.add).then_inc(s_b, 1)

        @block.vector
        def _(dve):
            for t in range(NT):
                dve.wait_ge(s_b, t + 1)
                dve.wait_ge(s_o, t + 1)
                dve.tensor_tensor(X[:, t, :], X[:, t, :], ps[:, t % 4, :], ALU.add).then_inc(s_f, 1)


def stage_routed_attention(chip, name, hs, w_gate, w_qkv):
    nc, X, XN, ident = chip.nc, chip.X, chip.XN, chip.ident
    NH, hd = w_gate.shape[0], hs.hd
    V = hd + 1
    with ExitStack() as st:
        def sb(n, shape, dt=F32):
            return chip.sb(f"{name}_{n}", shape, dt, st)

        def sem(n):
            return chip.sem(f"{name}_{n}")

        xnT = sb("xnT", [P, KD, B * L])
        transpose_norm(chip, name + "_xnT", xnT)
        wT, gT = sb("wT", [P, KD, 3 * D]), sb("gT", [P, KD, NH])
        with ExitStack() as s2:
            wr = chip.sb(name + "_w_rows", [P, 3 * KD, D], F32, s2)
            gr = chip.sb(name + "_g_rows", [NH, D], F32, s2)
            ps = chip.ps(name + "_wps", [P, 4, 512], F32, s2)
            s_w, s_t, s_c = sem("w"), sem("wt"), sem("wc")
            block = s2.enter_context(nc.Block())

            @block.sync
            def _(sp):
                sp.dma_start(wr[:], w_qkv.rearrange("(r p) k -> p r k", p=P)).then_inc(s_w, 16)
                sp.dma_start(gr[:], w_gate).then_inc(s_w, 16)

            @block.tensor
            def _(pe):
                pe.wait_ge(s_w, 32)
                for r in range(3 * KD):
                    if r >= 4:
                        pe.wait_ge(s_c, r - 3)
                    for k in range(KD):
                        m = pe.transpose(ps[:, r % 4, k * P:(k + 1) * P], wr[:, r, k * P:(k + 1) * P], ident[:])
                    m.then_inc(s_t, 1)
                pe.wait_ge(s_c, 3 * KD - 3)
                for k in range(KD):
                    m = pe.transpose(ps[:, 0, k * NH:(k + 1) * NH], gr[:, k * P:(k + 1) * P], ident[0:NH, 0:NH])
                m.then_inc(s_t, 1)

            @block.scalar
            def _(act):
                for r in range(3 * KD):
                    act.wait_ge(s_t, r + 1)
                    act.copy(wT[:, :, r * P:(r + 1) * P],
                             ps[:, r % 4, :].rearrange("p (k n) -> p k n", k=KD)).then_inc(s_c, 1)
                act.wait_ge(s_t, 3 * KD + 1)
                act.copy(gT[:].rearrange("p k n -> p (k n)"), ps[:, 0, 0:KD * NH]).then_inc(s_c, 1)

        gate = sb("gate", [P, NT, NH])
        top, tot, inv = sb("top", [P, NT]), sb("tot", [P, NT]), sb("inv", [P, NT])
        pick, pickv = sb("pick", [P, NT, NH]), sb("pick_value", [P, NT, NH])
        rank, best = sb("rank", [P, 1, NH]), sb("best", [P, NT])
        sel = [sb(f"sel{i}", [P, 2, NH, hd]) for i in range(2)]
        kv = [sb(f"kv{i}", [P, 2, V]) for i in range(2)]
        rest = [sb(f"rest{i}", [P, L]) for i in range(2)]
        parts = [sb(f"parts{i}", [P, 3, L], BF16) for i in range(2)]
        ps_q, ps_kv = chip.ps(name + "_pq", [P, 2, 512], F32, st), chip.ps(name + "_pkv", [P, 2, 2, 512], F32, st)
        ps_g, ps_k = chip.ps(name + "_pg", [P, NT, NH], F32, st), chip.ps(name + "_pk", [hd, 512], F32, st)
        s_g, s_ch, s_top, s_e = sem("g"), sem("chain"), sem("gtop"), sem("gexp")
        s_rank, s_kv, s_sel, s_kvr, s_kt = (sem(n) for n in ("rank", "kv", "selected", "kv_reduced", "key_turned"))
        s_p, s_p1, s_r1, s_p2, s_p3 = (sem(n) for n in (
            "product", "part1", "rest1", "part2", "part3"))
        s_st, s_vs = ([sem(f"{n}{i}") for i in range(2)] for n in ("stored", "v_stored"))
        ITEMS = [(b, g) for b in range(B) for g in range(KD + 1)]
        block = st.enter_context(nc.Block())

        @block.tensor
        def _(pe):
            for t in range(NT):
                for k in range(KD):
                    m = pe.matmul(ps_g[:, t, :], xnT[:, k, t * P:(t + 1) * P], gT[:, k, :],
                                  start=(t == 0 and k == 0), stop=True, skip_group_check=True)
            m.then_inc(s_g, 1)
            for b in range(B):
                for g in range(KD + 1):
                    n = b * (KD + 1) + g
                    if g < KD:
                        if n >= 2:
                            pe.wait_ge(s_r1, n - 1)
                        for k in range(KD):
                            m = pe.matmul(ps_q[:, n % 2, :], wT[:, k, g * P:(g + 1) * P],
                                          xnT[:, k, b * L:(b + 1) * L], start=(k == 0), stop=(k == KD - 1))
                        m.then_inc(s_p, 1)
                        t = b * TB + g
                        if t >= 2:
                            pe.wait_ge(s_sel, 2 * (t - 1))
                        for i in range(2):
                            for k in range(KD):
                                m = pe.matmul(ps_kv[:, t % 2, i, :], xnT[:, k, t * P:(t + 1) * P],
                                              wT[:, k, (i + 1) * D:(i + 2) * D], start=(k == 0), stop=(k == KD - 1))
                        m.then_inc(s_kv, 1)
                        if g:
                            turn = t - 1
                            pe.wait_ge(s_kvr, turn + 1)
                            if g == 1 and b:
                                pe.wait_ge(s_r1, n - 1)
                            pe.transpose(ps_k[:, turn % TB * P:(turn % TB + 1) * P], kv[turn % 2][:, 0, 0:hd],
                                         ident[:]).then_inc(s_kt, 1)
                    else:
                        turn = b * TB + TB - 1
                        pe.wait_ge(s_kvr, turn + 1)
                        pe.transpose(ps_k[:, (TB - 1) * P:], kv[turn % 2][:, 0, 0:hd], ident[:]).then_inc(s_kt, 1)

        @block.gpsimd
        def _(pool):
            pool.iota(rank[:, 0, :], [[-1, NH]], base=NH, channel_multiplier=0,
                      allow_small_or_imprecise_dtypes=True).then_inc(s_rank, 1)
            for i in range(2):
                pool.memset(kv[i][:, 1, hd:V], 1.0).then_inc(s_rank, 1)

        @block.vector
        def _(dve):
            ch = Chain(dve, s_ch)
            wide = [P, NT, NH]

            def over(x):
                return x[:].rearrange("p (t o) -> p t o", o=1).broadcast_to(wide)

            dve.wait_ge(s_g, 1)
            dve.wait_ge(s_rank, 3)
            ch.step(dve.tensor_reduce(top[:], ps_g[:], AX.X, ALU.max))
            dve.tensor_tensor(gate[:], ps_g[:], over(top), ALU.subtract).then_inc(s_top, 1)
            dve.wait_ge(s_e, 1)
            ch.step(dve.tensor_reduce(tot[:], gate[:], AX.X, ALU.add))
            ch.step(dve.reciprocal(inv[:], tot[:]))
            ch.step(dve.tensor_tensor(gate[:], gate[:], over(inv), ALU.mult))
            ch.step(dve.tensor_reduce(top[:], gate[:], AX.X, ALU.max))
            ch.step(dve.tensor_tensor(pick[:], gate[:], over(top), ALU.is_equal))
            rk = rank[:].broadcast_to(wide)
            ch.step(dve.tensor_tensor(pickv[:], pick[:], rk, ALU.mult))
            ch.step(dve.tensor_reduce(best[:], pickv[:], AX.X, ALU.max))
            ch.step(dve.tensor_tensor(pick[:], rk, over(best), ALU.is_equal))
            ch.step(dve.tensor_tensor(pickv[:], pick[:], over(top), ALU.mult))

            def select(t):
                i = t % 2
                dve.wait_ge(s_kv, t + 1)
                if t >= 2:
                    dve.wait_ge(s_kvr, t - 1)
                for j, p in enumerate((pick, pickv)):
                    w = p[:, t, :].rearrange("p (h o) -> p h o", o=1).broadcast_to([P, NH, hd])
                    dve.tensor_tensor(sel[i][:, j], ps_kv[:, i, j, :].rearrange("p (h d) -> p h d", h=NH), w,
                                      ALU.mult).then_inc(s_sel, 1)
                dve.wait_ge(s_sel, 2 * t + 2)
                if t >= 2:
                    dve.wait_ge(s_kt, t - 1)
                    dve.wait_ge(s_vs[i], 16 * (t // 2))
                dve.tensor_reduce(kv[i][:, :, 0:hd], sel[i][:].rearrange("p j h d -> p j d h"), AX.X,
                                  ALU.add).then_inc(s_kvr, 1)

            def split(n):
                i, (b, g) = n % 2, ITEMS[n]
                src, rows = (ps_q[:, i, :], P) if g < KD else (ps_k[:], hd)
                dve.wait_ge(s_p1, n + 1)
                if n >= 2:
                    dve.wait_ge(s_p3, n - 1)
                dve.tensor_tensor(rest[i][0:rows], src, parts[i][0:rows, 0, :], ALU.subtract).then_inc(s_r1, 1)
                dve.wait_ge(s_p2, n + 1)
                dve.tensor_tensor(parts[i][0:rows, 2, :], rest[i][0:rows], parts[i][0:rows, 1, :],
                                  ALU.subtract).then_inc(s_p3, 1)

            for n, (b, g) in enumerate(ITEMS):
                if g < KD:
                    select(b * TB + g)
                split(n)

        @block.scalar
        def _(act):
            act.wait_ge(s_top, 1)
            act.activation(gate[:], gate[:], ACT.Exp).then_inc(s_e, 1)
            for n, (b, g) in enumerate(ITEMS):
                i = n % 2
                if g < KD:
                    src, rows = ps_q[:, i, :], P
                    act.wait_ge(s_p, b * KD + g + 1)
                else:
                    src, rows = ps_k[:], hd
                    act.wait_ge(s_kt, (b + 1) * TB)
                if n >= 2:
                    act.wait_ge(s_st[i], 16 * (n // 2))
                act.copy(parts[i][0:rows, 0, :], src).then_inc(s_p1, 1)
                act.wait_ge(s_r1, n + 1)
                act.copy(parts[i][0:rows, 1, :], rest[i][0:rows]).then_inc(s_p2, 1)

        @block.sync
        def _(sp):
            for n, (b, g) in enumerate(ITEMS):
                i = n % 2
                if g < KD:
                    t = b * TB + g
                    sp.wait_ge(s_kvr, t + 1)
                    sp.dma_start(hs.v[b, :, g, :], kv[t % 2][:, 1, :]).then_inc(s_vs[t % 2], 16)
                    dst, rows = hs.q[b, :, g * P:(g + 1) * P, :], P
                else:
                    dst, rows = hs.k[b], hd
                sp.wait_ge(s_p3, n + 1)
                sp.dma_start(dst.rearrange("a p t -> p a t"), parts[i][0:rows]).then_inc(s_st[i], 16)
            for i in range(2):
                sp.wait_ge(s_st[i], 16 * len(ITEMS) // 2)
                sp.wait_ge(s_vs[i], 16 * NT // 2)

    attention_core(chip, name + "_core", hs, add=True)


def ternary_weights(chip, name, mats, wT, wscale, tanh_rule):
    nc = chip.nc
    STEPS = 10 if tanh_rule else 3
    COUNT = float(mats[0].shape[0] * mats[0].shape[1])
    with ExitStack() as st:
        def sb(n, shape, dt=F32):
            return chip.sb(f"{name}_{n}", shape, dt, st)

        def sem(n):
            return chip.sem(f"{name}_{n}")

        W = sb("w", [P, 4, 2048])
        neg = [sb(f"neg{i}", [P, 2048]) for i in range(2)]
        tern = [sb(f"tern{i}", [P, 4, 512], BF16) for i in range(2)]
        part, ones = sb("part", [P, 3, 4]), sb("ones", [P, P])
        psum1, s, th = sb("sum1", [P, 3]), sb("s", [P, 3]), sb("th", [P, 3, 2])
        tmp, junk = sb("tmp", [P, 6]), sb("junk", [P, 2048], BF16)
        ps = chip.ps(name + "_ps", [P, 2, 2 * BANK], BF16, st)
        ps_s = chip.ps(name + "_sum", [P, 3, BANK], F32, st)
        s_w = [sem(f"w{c}") for c in range(4)]
        s_abs, s_one, s_p1, s_sum, s_ch = sem("abs"), sem("ones"), sem("part"), sem("sum"), sem("chain")
        s_ln, s_neg, s_tern, s_t, s_cp = sem("ln"), sem("negative"), sem("ternary"), sem("t"), sem("copied")
        block = st.enter_context(nc.Block())

        @block.sync
        def _(sp):
            for m, w in enumerate(mats):
                for c in range(4):
                    if m:
                        sp.wait_ge(s_tern, 4 * (m - 1) + c + 1)
                    if m < 2:
                        sp.dma_start(W[:, c, :].rearrange("p (j k) -> p j k", j=4),
                                     w[c * 512:(c + 1) * 512, :].rearrange("(j p) k -> p j k", p=P)
                                     ).then_inc(s_w[c], 16)
                    else:
                        sp.dma_start(W[:, c, :], w[c * P:(c + 1) * P, :]).then_inc(s_w[c], 16)

        @block.tensor
        def _(pe):
            pe.wait_ge(s_one, 1)

            def total(m):
                pe.wait_ge(s_p1, m + 1)
                pe.matmul(ps_s[:, m, 0:1], ones[:], psum1[:, m:m + 1], start=True, stop=True).then_inc(s_sum, 1)

            total(0)
            for m in range(3):
                for c in range(4):
                    pe.wait_ge(s_tern, 4 * m + c + 1)
                    for g in range(4):
                        n = 16 * m + 4 * c + g
                        if n >= 2:
                            pe.wait_ge(s_cp, n - 1)
                        for j in range(4):
                            src = tern[c % 2][:, j, g * P:(g + 1) * P] if m < 2 else \
                                tern[c % 2][:, g, j * P:(j + 1) * P]
                            t = pe.transpose(ps[:, n % 2, j * P:(j + 1) * P], src, chip.identb[:])
                        t.then_inc(s_t, 1)
                if m < 2:
                    total(m + 1)

        @block.scalar
        def _(act):
            def sums(m):
                for c in range(4):
                    act.wait_ge(s_w[c], 16 * (m + 1))
                    if c or m:
                        act.wait_ge(s_abs, 4 * m + c)
                    act.activation(junk[:], W[:, c, :], ACT.Abs, accum_out=part[:, m, c:c + 1]).then_inc(s_abs, 1)

            def log(m):
                act.wait_ge(s_ch, STEPS * m + 7)
                act.activation(tmp[:, 3:4], tmp[:, 1:2], ACT.Ln).then_inc(s_ln, 1)

            sums(0)
            if tanh_rule:
                log(0)
            for m in range(3):
                for c in range(4):
                    for g in range(4):
                        n = 16 * m + 4 * c + g
                        act.wait_ge(s_t, n + 1)
                        if m < 2:
                            dst = wT[m][:, g, c * 512:(c + 1) * 512].rearrange("p (j k) -> p j k", j=4)
                        else:
                            dst = wT[m][:, 4 * g:4 * g + 4, c * P:(c + 1) * P]
                        act.copy(dst, ps[:, n % 2, 0:512].rearrange("p (j k) -> p j k", j=4)).then_inc(s_cp, 1)
                if m < 2:
                    sums(m + 1)
                    if tanh_rule:
                        log(m + 1)

        @block.vector
        def _(dve):
            ch = Chain(dve, s_ch)
            dve.memset(ones[:], 1.0).then_inc(s_one, 1)
            for m in range(3):
                a, b = th[:, m, 0:1], th[:, m, 1:2]
                one = slice(m, m + 1)
                dve.wait_ge(s_abs, 4 * m + 4)
                dve.tensor_reduce(psum1[:, one], part[:, m, :], AX.X, ALU.add).then_inc(s_p1, 1)
                dve.wait_ge(s_sum, m + 1)
                if tanh_rule:
                    ch.step(dve.tensor_scalar(s[:, one], ps_s[:, m, 0:1], 1.0 / COUNT, None, ALU.mult))
                    ch.step(dve.tensor_scalar(a, s[:, one], 1e-8, float(np.arctanh(0.5)), ALU.add, ALU.mult))
                    ch.step(dve.tensor_scalar(b, a, -1.0, None, ALU.mult))
                    ch.step(dve.tensor_scalar(tmp[:, 0:1], s[:, one], -1.0, 1.0, ALU.mult, ALU.add))
                    ch.step(dve.reciprocal(tmp[:, 2:3], tmp[:, 0:1]))
                    ch.step(dve.scalar_tensor_tensor(out=tmp[:, 0:1], in0=s[:, one], scalar=2.0,
                                                     in1=tmp[:, 2:3], op0=ALU.mult, op1=ALU.mult))
                    ch.step(dve.tensor_scalar(tmp[:, 1:2], tmp[:, 0:1], 1.0, None, ALU.add))
                    ch.step(dve.tensor_scalar(tmp[:, 2:3], tmp[:, 1:2], -1.0, 2.0 ** -24, ALU.add, ALU.max))
                    ch.step(dve.reciprocal(tmp[:, 4:5], tmp[:, 2:3]))
                    dve.wait_ge(s_ln, m + 1)
                    ch.step(dve.scalar_tensor_tensor(out=tmp[:, 5:6], in0=tmp[:, 3:4], scalar=0.5,
                                                     in1=tmp[:, 0:1], op0=ALU.mult, op1=ALU.mult))
                    dve.tensor_tensor(wscale[:, one], tmp[:, 5:6], tmp[:, 4:5], ALU.mult)
                else:
                    ch.step(dve.tensor_scalar(wscale[:, one], ps_s[:, m, 0:1], 1.0 / COUNT, 1e-5,
                                              ALU.mult, ALU.add))
                    ch.step(dve.tensor_scalar(a, wscale[:, one], 0.5, None, ALU.mult))
                    ch.step(dve.tensor_scalar(b, wscale[:, one], -0.5, None, ALU.mult))
                for c in range(4):
                    n = 4 * m + c
                    if n >= 2:
                        dve.wait_ge(s_t, 4 * (n - 1))
                    dve.tensor_scalar(neg[c % 2][:], W[:, c, :], b, None, ALU.is_lt).then_inc(s_neg, 1)
                    dve.wait_ge(s_neg, n + 1)
                    dve.scalar_tensor_tensor(out=tern[c % 2][:].rearrange("p j k -> p (j k)"), in0=W[:, c, :],
                                             scalar=a, in1=neg[c % 2][:], op0=ALU.is_gt,
                                             op1=ALU.subtract).then_inc(s_tern, 1)


def quantised_input(chip, name, gains, wscale, xqT, gsc):
    nc, XN = chip.nc, chip.XN
    NX = len(xqT)
    with ExitStack() as st:
        def sb(n, shape, dt=F32):
            return chip.sb(f"{name}_{n}", shape, dt, st)

        def sem(n):
            return chip.sem(f"{name}_{n}")

        m, q, c = sb("max", [P, NX, NT]), sb("q", [P, NX, NT]), sb("c", [P, NX, NT])
        ss, root, rroot = sb("ss", [P, NT]), sb("root", [P, NT]), sb("rroot", [P, NT])
        xg = [sb(f"xg{i}", [P, D]) for i in range(NX)]
        r1 = [sb(f"r{i}", [P, D]) for i in range(2)]
        xq = [sb(f"xq{i}", [P, D], BF16) for i in range(2)]
        junk, eps = sb("junk", [P, D]), sb("eps", [P, 1])
        g = [sb(f"g{j}", [P, D]) for j in range(NX)] if gains else None
        ps = chip.ps(name + "_ps", [P, 4, 2 * BANK], BF16, st)
        s_g, s_eps, s_ss, s_rt, s_xg = sem("g"), sem("eps"), sem("squares"), sem("root"), sem("xg")
        s_m, s_c, s_r, s_xq, s_t, s_cp = sem("max"), sem("chain"), sem("r"), sem("xq"), sem("t"), sem("copied")
        block = st.enter_context(nc.Block())

        @block.sync
        def _(sp):
            if gains:
                for j in range(NX):
                    sp.dma_start(g[j][:], gains[j].rearrange("(o n) -> o n", o=1).broadcast_to([P, D])
                                 ).then_inc(s_g, 16)
                sp.wait_ge(s_g, 32)

        @block.gpsimd
        def _(pool):
            if gains:
                pool.wait_ge(s_g, 32)
                for t in range(NT):
                    for j in range(NX):
                        if t:
                            pool.wait_ge(s_m, (t - 1) * NX + j + 1)
                        pool.tensor_tensor(xg[j][:], XN[:, t, :], g[j][:], ALU.mult).then_inc(s_xg, 1)

        @block.scalar
        def _(act):
            if gains:
                for t in range(NT):
                    if t:
                        act.wait_ge(s_ss, t)
                    act.activation(junk[:], XN[:, t, :], ACT.Square, accum_out=ss[:, t:t + 1]).then_inc(s_ss, 1)
                act.wait_ge(s_eps, 1)
                act.wait_ge(s_ss, NT)
                act.activation(root[:], ss[:], ACT.Sqrt, scale=1.0 / D, bias=eps[:]).then_inc(s_rt, 1)
            for t in range(NT):
                for j in range(NX):
                    n = t * NX + j
                    act.wait_ge(s_t, n + 1)
                    act.copy(xqT[j][:, t], ps[:, n % 4, 0:D].rearrange("p (k t) -> p k t", k=KD)).then_inc(s_cp, 1)

        @block.tensor
        def _(pe):
            for n in range(NT * NX):
                pe.wait_ge(s_xq, n + 1)
                if n >= 4:
                    pe.wait_ge(s_cp, n - 3)
                for k in range(KD):
                    i = pe.transpose(ps[:, n % 4, k * P:(k + 1) * P], xq[n % 2][:, k * P:(k + 1) * P],
                                     chip.identb[:])
                i.then_inc(s_t, 1)

        @block.vector
        def _(dve):
            ch = Chain(dve, s_c)
            ch.did(dve.memset(gsc[:, :, NT:NT + 1], 0.0))
            if gains:
                dve.memset(eps[:], 1e-8).then_inc(s_eps, 1)
                dve.wait_ge(s_g, 32)
                for t in range(NT):
                    for j in range(NX):
                        dve.wait_ge(s_xg, t * NX + j + 1)
                        dve.tensor_reduce(m[:, j, t:t + 1], xg[j][:], AX.X, ALU.max,
                                          apply_absolute_value=True).then_inc(s_m, 1)
                dve.wait_ge(s_m, NT * NX)
                dve.wait_ge(s_rt, 1)
                ch.step(dve.reciprocal(rroot[:], root[:]))
                for j in range(NX):
                    ch.step(dve.scalar_tensor_tensor(out=c[:, j], in0=root[:], scalar=1e-4, in1=m[:, j],
                                                     op0=ALU.mult, op1=ALU.max))
                ch.step(dve.tensor_scalar(c[:], c[:], 1.0 / 127, None, ALU.mult))
                ch.step(dve.reciprocal(q[:], c[:]))
                for j in range(NX):
                    ch.step(dve.scalar_tensor_tensor(out=gsc[:, j, 0:NT], in0=c[:, j], scalar=wscale[:, j:j + 1],
                                                     in1=rroot[:], op0=ALU.mult, op1=ALU.mult))
            else:
                ch.step(dve.tensor_reduce(m[:, 0], XN[:], AX.X, ALU.max, apply_absolute_value=True))
                ch.step(dve.tensor_scalar(c[:], m[:], 1e-5, 1.0 / 127, ALU.max, ALU.mult))
                ch.step(dve.reciprocal(q[:], c[:]))
                for j in range(2):
                    ch.step(dve.tensor_scalar(gsc[:, j, 0:NT], c[:, 0], wscale[:, j:j + 1], None, ALU.mult))
            for n in range(NT * NX):
                t, j, i = n // NX, n % NX, n % 2
                if n >= 2:
                    dve.wait_ge(s_xq, n - 1)
                if gains:
                    dve.scalar_tensor_tensor(out=r1[i][:], in0=XN[:, t, :], scalar=q[:, j, t:t + 1], in1=g[j][:],
                                             op0=ALU.mult, op1=ALU.mult).then_inc(s_r, 1)
                else:
                    dve.tensor_scalar(r1[i][:], XN[:, t, :], q[:, j, t:t + 1], None, ALU.mult).then_inc(s_r, 1)
                dve.wait_ge(s_r, n + 1)
                if n >= 2:
                    dve.wait_ge(s_t, n - 1)
                dve.tensor_scalar(xq[i][:], r1[i][:], MAGIC, -MAGIC, ALU.add, ALU.add).then_inc(s_xq, 1)


def stage_bitffn(chip, name, mats, gains=None):
    nc, X, XN = chip.nc, chip.X, chip.XN
    F = mats[0].shape[0]
    NC = F // 512
    NJ = F // P
    NX = 2 if gains else 1
    with ExitStack() as st0:
        wT = [chip.sb(f"{name}_wT{m}", [P, KD, F] if m < 2 else [P, NJ, D], BF16, st0) for m in range(3)]
        wscale = chip.sb(name + "_wscale", [P, 3], F32, st0)
        ternary_weights(chip, name + "_w", mats, wT, wscale, gains is not None)
        st = st0.enter_context(ExitStack())

        def sb(n, shape, dt=F32):
            return chip.sb(f"{name}_{n}", shape, dt, st)

        def sem(n):
            return chip.sem(f"{name}_{n}")

        xqT = [sb(f"xqT{j}", [P, NT, KD, P], BF16) for j in range(NX)]
        gsc = sb("gate_up_scale", [P, 2, NT + 1])
        quantised_input(chip, name + "_x", gains, wscale, xqT, gsc)

        gsel = [sb(f"gate_up_scale{i}", [P, 2]) for i in range(2)]
        sig = [sb(f"act{i}", [P, 512]) for i in range(2)]
        h = [XN[:, i * NC:(i + 1) * NC, :].rearrange("p c n -> p (c n)") for i in range(2)]
        r1 = XN[:, 2 * NC:3 * NC, :].rearrange("p c n -> p (c n)")
        hq = [sb(f"hq{i}", [P, F], BF16) for i in range(2)]
        hqT = [sb(f"hqT{i}", [P, NJ, P], BF16) for i in range(2)]
        sm = [sb(f"small{i}", [P, 8]) for i in range(2)]
        dsc = [sb(f"down_scale{i}", [P, 1]) for i in range(2)]
        if gains:
            g3 = XN[:, 3 * NC:4 * NC, :].rearrange("p c n -> p (c n)")
            eps = sb("eps", [P, 1])
        ps_g, ps_u = chip.ps(name + "_g", [P, 2, 512], F32, st), chip.ps(name + "_u", [P, 2, 512], F32, st)
        ps_h = chip.ps(name + "_hT", [P, NJ, P], BF16, st)
        ps_d = chip.ps(name + "_d", [P, 512], F32, st)

        s_g, s_u, s_sig, s_h = sem("gate"), sem("up"), sem("act"), sem("h")
        s_hg, s_ss, s_rt, s_c, s_q = sem("h_gained"), sem("squares"), sem("root"), sem("chain"), sem("quantised")
        s_ht, s_hc, s_d, s_f = sem("hT"), sem("hT_copied"), sem("down"), sem("folded")
        s_g3, s_ep, s_gs = sem("g3"), sem("eps"), sem("scales")
        block = st.enter_context(nc.Block())
        LAST = NT - 1

        @block.sync
        def _(sp):
            if gains:
                sp.dma_start(g3, gains[2].rearrange("(o n) -> o n", o=1).broadcast_to([P, F])).then_inc(s_g3, 16)
                sp.wait_ge(s_g3, 16)

        @block.tensor
        def _(pe):
            pe.sem_inc(s_ht, 2)
            pe.sem_inc(s_d, 2)

            def gate_up(t):
                for c in range(NC):
                    n = t * NC + c
                    pe.wait_ge(s_sig, n + 1)
                    for m, (bank, sem_, j) in enumerate(((ps_g, s_g, 0), (ps_u, s_u, NX - 1))):
                        if m:
                            pe.wait_ge(s_h, n + 1)
                        for k in range(KD):
                            i = pe.matmul(bank[:, c % 2, :], xqT[j][:, bass.ds(t, 1), k, :].rearrange(
                                "p o t -> p (o t)"), wT[m][:, k, c * 512:(c + 1) * 512],
                                start=(k == 0), stop=(k == KD - 1))
                        i.then_inc(sem_, 1)

            def turn_h(t, p):
                pe.wait_ge(s_q, t + 3)
                pe.wait_ge(s_hc, t + 1)
                for j in range(NJ):
                    i = pe.transpose(ps_h[:, j, :], hq[p][:, j * P:(j + 1) * P], chip.identb[:])
                i.then_inc(s_ht, 1)

            def down(t, p):
                pe.wait_ge(s_hc, t + 2)
                pe.wait_ge(s_f, t + 2)
                for j in range(NJ):
                    i = pe.matmul(ps_d[:], hqT[p][:, j, :], wT[2][:, j, :], start=(j == 0), stop=(j == NJ - 1))
                i.then_inc(s_d, 1)

            gate_up(0)
            gate_up(1)
            turn_h(0, 0)
            with pe.Fori(0, LAST // 2) as i:
                t = i * 2 + 1
                for p in range(2):
                    gate_up(t + p + 1)
                    turn_h(t + p, 1 - p)
                    down(t + p - 1, p)
            turn_h(LAST, 1)
            down(LAST - 1, 0)
            down(LAST, 1)

        @block.scalar
        def _(act):
            act.sem_inc(s_sig, 2)
            act.sem_inc(s_hc, 1)

            def gate(t, c, p):
                n = t * NC + c
                act.wait_ge(s_gs, t + 1)
                act.wait_ge(s_g, n + 1)
                act.wait_ge(s_h, n + 1)
                act.activation(sig[c % 2][:], ps_g[:, c % 2, :], ACT.Silu if gains else ACT.Sigmoid,
                               scale=gsel[p][:, 0:1]).then_inc(s_sig, 1)

            def root(t, p):
                if gains:
                    act.wait_ge(s_h, t * NC + NC + 2)
                    act.wait_ge(s_q, t + 1)
                    act.wait_ge(s_ht, t + 1)
                    act.wait_ge(s_ss, t + 1)
                    act.activation(hq[p][:], h[p], ACT.Square, accum_out=sm[p][:, 0:1]).then_inc(s_ss, 1)
                    act.wait_ge(s_ss, t + 2)
                    act.activation(sm[p][:, 1:2], sm[p][:, 0:1], ACT.Sqrt, scale=1.0 / F,
                                   bias=eps[:]).then_inc(s_rt, 1)

            def copy_h(t, p):
                act.wait_ge(s_ht, t + 3)
                act.wait_ge(s_d, t + 1)
                act.copy(hqT[p][:], ps_h[:]).then_inc(s_hc, 1)

            if gains:
                act.wait_ge(s_ep, 1)
                act.sem_inc(s_ss, 1)
            for c in range(NC):
                gate(0, c, 0)
            root(0, 0)
            for c in range(NC):
                gate(1, c, 1)
            copy_h(0, 0)
            root(1, 1)
            with act.Fori(0, LAST // 2) as i:
                t = i * 2 + 1
                for p in range(2):
                    for c in range(NC):
                        gate(t + p + 1, c, p)
                    copy_h(t + p, 1 - p)
                    root(t + p + 1, p)
            copy_h(LAST, 1)

        @block.gpsimd
        def _(pool):
            if gains:
                def gained(t, p):
                    pool.wait_ge(s_g3, 16)
                    pool.wait_ge(s_ss, t + 2)
                    pool.wait_ge(s_h, t * NC + NC + 2)
                    pool.tensor_tensor(h[p], h[p], g3, ALU.mult).then_inc(s_hg, 1)

                with pool.Fori(0, NT // 2) as i:
                    for p in range(2):
                        gained(i * 2 + p, p)

        @block.vector
        def _(dve):
            dve.sem_inc(s_h, 2)
            dve.sem_inc(s_q, 2)
            dve.sem_inc(s_f, 2)
            if gains:
                dve.memset(eps[:], 1e-8).then_inc(s_ep, 1)
            ch = Chain(dve, s_c)
            PER = 7 if gains else 5

            def pick(t, p):
                dve.tensor_copy(gsel[p][:].rearrange("q (j o) -> q j o", o=1),
                                gsc[:, :, bass.ds(t, 1)]).then_inc(s_gs, 1)

            def chunk(t, p, c):
                n = t * NC + c
                dve.wait_ge(s_u, n + 1)
                dve.wait_ge(s_sig, n + 3)
                if c == 0:
                    dve.wait_ge(s_gs, t + 1)
                    dve.wait_ge(s_q, t + 1)
                dve.scalar_tensor_tensor(out=h[p][:, c * 512:(c + 1) * 512], in0=ps_u[:, c % 2, :],
                                         scalar=gsel[p][:, 1:2], in1=sig[c % 2][:],
                                         op0=ALU.mult, op1=ALU.mult).then_inc(s_h, 1)

            def quantise(t, p, part):
                v = sm[p]
                if part == 0:
                    ch.base, ch.n = t * PER, 0
                    dve.wait_ge(s_h, t * NC + NC + 2)
                    if gains:
                        dve.wait_ge(s_hg, t + 1)
                    ch.step(dve.tensor_reduce(v[:, 2:3], h[p], AX.X, ALU.max, apply_absolute_value=True))
                elif part == 1:
                    dve.wait_ge(s_f, t + 1)
                    if gains:
                        dve.wait_ge(s_rt, t + 1)
                        ch.step(dve.scalar_tensor_tensor(out=v[:, 3:4], in0=v[:, 1:2], scalar=1e-4,
                                                         in1=v[:, 2:3], op0=ALU.mult, op1=ALU.max))
                        ch.did(dve.tensor_scalar(v[:, 4:5], v[:, 3:4], 1.0 / 127, None, ALU.mult))
                        ch.did(dve.reciprocal(v[:, 6:7], v[:, 1:2]))
                        ch.settle()
                        ch.did(dve.reciprocal(v[:, 5:6], v[:, 4:5]))
                        ch.did(dve.scalar_tensor_tensor(out=dsc[p][:], in0=v[:, 4:5], scalar=wscale[:, 2:3],
                                                        in1=v[:, 6:7], op0=ALU.mult, op1=ALU.mult))
                    else:
                        ch.step(dve.tensor_scalar(v[:, 4:5], v[:, 2:3], 1e-5, 1.0 / 127, ALU.max, ALU.mult))
                        ch.did(dve.reciprocal(v[:, 5:6], v[:, 4:5]))
                        ch.did(dve.tensor_tensor(dsc[p][:], v[:, 4:5], wscale[:, 2:3], ALU.mult))
                    ch.settle()
                    ch.did(dve.tensor_scalar(r1, h[p], v[:, 5:6], MAGIC, ALU.mult, ALU.add))
                    assert ch.n == PER
                else:
                    ch.settle()
                    dve.wait_ge(s_ht, t + 1)
                    dve.tensor_scalar(hq[p][:], r1, -MAGIC, 127.0, ALU.add, ALU.min).then_inc(s_q, 1)

            def fold(t, p):
                dve.wait_ge(s_d, t + 3)
                x = X[:, bass.ds(t, 1), :].rearrange("p o d -> p (o d)")
                dve.scalar_tensor_tensor(out=x, in0=ps_d[:], scalar=dsc[p][:], in1=x,
                                         op0=ALU.mult, op1=ALU.add).then_inc(s_f, 1)

            def tile(t, p, last=False, first=False):
                for c in range(NC):
                    if not last:
                        chunk(t + 1, 1 - p, c)
                    if c < 3:
                        quantise(t, p, c)
                if not first:
                    fold(t - 1, 1 - p)
                if not last:
                    pick(t + 2, p)

            pick(0, 0)
            pick(1, 1)
            for c in range(NC):
                chunk(0, 0, c)
            tile(0, 0, first=True)
            with dve.Fori(0, LAST // 2) as i:
                t = i * 2 + 1
                for p in range(2):
                    tile(t + p, 1 - p)
            tile(LAST, 1, last=True)
            fold(LAST, 1)


ONE_PASS = [[(0, 0), (0, 1), (0, 2), (1, 0), (1, 1), (2, 0)]]
TWO_PASSES = [[(0, 0), (0, 1), (0, 2)], [(1, 0), (1, 1), (2, 0)]]


def mamba_args(a, layer):
    names = ("in_proj_w", "conv_w", "conv_b", "x_proj_w", "dt_proj_w", "dt_proj_b", "A_log", "D")
    got = [a[f"{layer}_xattn_{n}"] for n in names]
    if len(got[1].shape) == 3:
        got[1] = got[1].rearrange("e o t -> e (o t)")
    return got


def build(nc, a, out):
    with ExitStack() as ctx:
        chip = Chip(nc, ctx)
        bc = nc.dram_tensor("bc_rows", (B, 32, L), F32).ap()
        chip.run(stage_start, a["x"], a["ctx_1024"])

        chip.run(stage_norm, "n0")
        chip.run(stage_mamba, "m0", bc, *mamba_args(a, "L0"))

        chip.run(stage_norm, "n1")
        names = ("gate_W_packed", "gate_scales", "up_W_packed", "up_scales", "down_W_packed", "down_scales")
        chip.run(stage_ffn4, "f0", *[a["L0_ffn_" + n] for n in names])

        chip.run(stage_norm, "n2")
        heads = Heads(nc, "a1", D // 32, 16, ONE_PASS, False)
        names = ("Wq", "Wkv", "Wout", "bout")
        chip.run(stage_attention, "a1", heads, a["fside_BxSx2_0"], a["freq"], *[a["L1_xattn_" + n] for n in names])

        chip.run(stage_norm, "n3")
        chip.run(stage_bitffn, "f1", [a["L1_ffn_w_" + n] for n in ("gate", "up", "down")])

        chip.run(stage_norm, "n4")
        chip.run(stage_mix, "a2", *[a["L2_xattn_" + n] for n in ("Wq", "bq", "Wk", "bk")])

        chip.run(stage_norm, "n5")
        chip.run(stage_bitffn, "f2", [a["L2_ffn_w" + n] for n in "123"], [a["L2_ffn_g" + n] for n in "123"])

        chip.run(stage_norm, "n6")
        chip.run(stage_mamba, "m3", bc, *mamba_args(a, "L3"))

        chip.run(stage_norm, "n7")
        heads = Heads(nc, "f3", D // 16, 1, TWO_PASSES, True)
        chip.run(stage_routed_attention, "f3", heads, a["L3_ffn_W_gate"], a["L3_ffn_W_qkv"])

        chip.run(stage_end, out)

_INS = ['x',
        'ctx_1024',
        'fside_BxSx2_0',
        'L0_xattn_in_proj_w',
        'L0_xattn_conv_w',
        'L0_xattn_conv_b',
        'L0_xattn_x_proj_w',
        'L0_xattn_dt_proj_w',
        'L0_xattn_dt_proj_b',
        'L0_xattn_A_log',
        'L0_xattn_D',
        'L0_ffn_gate_W_packed',
        'L0_ffn_gate_scales',
        'L0_ffn_up_W_packed',
        'L0_ffn_up_scales',
        'L0_ffn_down_W_packed',
        'L0_ffn_down_scales',
        'L1_xattn_Wq',
        'L1_xattn_Wkv',
        'L1_xattn_Wout',
        'L1_xattn_bout',
        'L1_ffn_w_gate',
        'L1_ffn_w_up',
        'L1_ffn_w_down',
        'L2_xattn_Wq',
        'L2_xattn_bq',
        'L2_xattn_Wk',
        'L2_xattn_bk',
        'L2_ffn_w1',
        'L2_ffn_g1',
        'L2_ffn_w2',
        'L2_ffn_g2',
        'L2_ffn_w3',
        'L2_ffn_g3',
        'L3_xattn_in_proj_w',
        'L3_xattn_conv_w',
        'L3_xattn_conv_b',
        'L3_xattn_x_proj_w',
        'L3_xattn_dt_proj_w',
        'L3_xattn_dt_proj_b',
        'L3_xattn_A_log',
        'L3_xattn_D',
        'L3_ffn_W_gate',
        'L3_ffn_W_qkv']


def kernel(**inputs):
    import numpy as _np
    import concourse.bacc as _bacc
    from concourse import mybir as _mybir
    from concourse.bass_utils import run_bass_kernel_spmd as _run

    nc = _bacc.Bacc("TRN2", target_bir_lowering=False, num_devices=1)
    arrays, args = {}, {}
    for name in _INS:
        a = _np.ascontiguousarray(inputs[name])
        arrays[f"in_{name}_dram"] = a
        args[name] = nc.dram_tensor(f"in_{name}_dram", a.shape, _mybir.dt.from_np(a.dtype), kind="ExternalInput").ap()
    half = 4
    freq = _np.zeros((2, 128), _np.float32)
    rates = _np.float32(10000.0) ** (-_np.arange(half, dtype=_np.float32) / _np.float32(half))
    for p in range(128):
        freq[p % 16 // 8, p] = rates[p % 8 // 2]
    arrays["in_freq_dram"] = freq
    args["freq"] = nc.dram_tensor("in_freq_dram", freq.shape, _mybir.dt.float32, kind="ExternalInput").ap()
    out = nc.dram_tensor("out_0_dram", (B, L, D), _mybir.dt.float32, kind="ExternalOutput").ap()
    build(nc, args, out)
    r = _run(nc, [arrays], core_ids=[0])
    return r.results[0]["out_0_dram"]
```

```python
from contextlib import ExitStack

import numpy as np

import concourse.bass as bass
from concourse import mybir

F32 = mybir.dt.float32
BF16 = mybir.dt.bfloat16
F16 = mybir.dt.float16
I32 = mybir.dt.int32
ALU = mybir.AluOpType
ACT = mybir.ActivationFunctionType
AX = mybir.AxisListType

P = 128
B, L, D = 4, 512, 512
C = 256
NT = B * L // P
TB = L // P
KD = D // P
KC = C // P
BANK = 512
MAGIC = 1.5 * 2.0 ** 23


class Chain:

    def __init__(self, eng, sem):
        self.eng, self.sem, self.n, self.base = eng, sem, 0, 0

    def did(self, ins):
        ins.then_inc(self.sem, 1)
        self.n += 1
        return self.base + self.n

    def settle(self):
        self.eng.wait_ge(self.sem, self.base + self.n)

    def step(self, ins):
        self.did(ins)
        self.settle()


class Chip:

    def __init__(self, nc, ctx):
        self.nc, self.ctx, self.count = nc, ctx, 0
        self.X = self.sb("X", [P, NT, D])
        self.XN = self.sb("XN", [P, NT, D])
        self.ctxT = self.sb("ctxT", [P, KC, B * L])
        self.ident = self.sb("ident", [P, P])
        self.identb = self.sb("identb", [P, P], BF16)
        self.stored = nc.alloc_semaphore("output_stored")

    def sb(self, name, shape, dt=F32, ctx=None):
        return (ctx or self.ctx).enter_context(self.nc.sbuf_tensor(name, shape, dt))

    def ps(self, name, shape, dt=F32, ctx=None):
        return (ctx or self.ctx).enter_context(self.nc.psum_tensor(name, shape, dt))

    def sem(self, name):
        return self.nc.alloc_semaphore(name)

    def run(self, stage, *args, **kw):
        with self.nc.cleanup_on_exit():
            stage(self, *args, **kw)
        self.nc.all_engine_barrier()


def stage_start(chip, x, ctx_dram):
    nc = chip.nc
    X, ctxT, ident = chip.X, chip.ctxT, chip.ident
    with ExitStack() as st:
        cn = chip.sb("ctx_rows", [P, NT, C], F32, st)
        pt = chip.ps("ctx_pt", [P, 2, 4, P], F32, st)
        s_x, s_c = chip.sem("start_x"), chip.sem("start_ctx")
        s_one, s_id, s_idb = chip.sem("start_zero"), chip.sem("start_ident"), chip.sem("start_identb")
        s_t, s_cp = chip.sem("start_transposed"), chip.sem("start_copied")
        block = st.enter_context(nc.Block())

        @block.sync
        def _(sp):
            sp.dma_start(cn[:], ctx_dram.rearrange("b (t p) c -> p (b t) c", p=P)).then_inc(s_c, 16)
            sp.dma_start(X[:], x.rearrange("b (t p) c -> p (b t) c", p=P)).then_inc(s_x, 16)
            sp.wait_ge(s_x, 16)

        @block.gpsimd
        def _(pool):
            pool.memset(ident[:], 0.0).then_inc(s_one, 1)
            pool.wait_ge(s_one, 1)
            pool.affine_select(out=ident[:], in_=ident[:], compare_op=ALU.not_equal, fill=1.0, base=0,
                               pattern=[[-1, P]], channel_multiplier=1).then_inc(s_id, 1)

        @block.tensor
        def _(pe):
            pe.wait_ge(s_id, 1)
            pe.wait_ge(s_c, 16)
            for k in range(KC):
                for g in range(NT // 4):
                    n = k * (NT // 4) + g
                    if n >= 2:
                        pe.wait_ge(s_cp, n - 1)
                    for j in range(4):
                        m = pe.transpose(pt[:, n % 2, j, :], cn[:, 4 * g + j, k * P:(k + 1) * P], ident[:])
                    m.then_inc(s_t, 1)

        @block.scalar
        def _(act):
            for k in range(KC):
                for g in range(NT // 4):
                    n = k * (NT // 4) + g
                    act.wait_ge(s_t, n + 1)
                    act.copy(ctxT[:, k, g * 4 * P:(g + 1) * 4 * P].rearrange("p (j t) -> p j t", j=4),
                             pt[:, n % 2]).then_inc(s_cp, 1)

        @block.vector
        def _(dve):
            dve.wait_ge(s_id, 1)
            dve.tensor_copy(chip.identb[:], ident[:]).then_inc(s_idb, 1)


class Norm:

    def __init__(self, chip, name, st, eps=1e-5):
        self.X, self.XN, self.eps = chip.X, chip.XN, eps
        self.statistics = chip.sb(name + "_stats", [P, NT, 6], F32, st)
        self.mv = chip.sb(name + "_mv", [P, NT, 2], F32, st)
        self.std, self.rstd, self.shift = (chip.sb(f"{name}_{n}", [P, NT], F32, st) for n in ("std", "rstd", "shift"))
        self.epst = chip.sb(name + "_eps", [P, 1], F32, st)
        self.s_st, self.s_mv, self.s_eps, self.s_std, self.s_rs, self.s_sh, self.s_xa, self.s_xd = (
            chip.sem(f"{name}_{n}") for n in (
                "stats", "mv", "eps", "std", "rstd", "shift", "xn_act", "xn_dve"))

    def moments(self, dve):
        dve.memset(self.epst[:], self.eps).then_inc(self.s_eps, 1)
        for t in range(NT):
            dve.bn_stats(self.statistics[:, t, :], self.X[:, t, :]).then_inc(self.s_st, 1)
        for t in range(NT):
            dve.wait_ge(self.s_st, t + 1)
            dve.bn_aggr(self.mv[:, t, :], self.statistics[:, t, :]).then_inc(self.s_mv, 1)

    def root(self, act):
        act.wait_ge(self.s_eps, 1)
        act.wait_ge(self.s_mv, NT)
        act.activation(self.std[:], self.mv[:, :, 1], ACT.Sqrt, bias=self.epst[:]).then_inc(self.s_std, 1)

    def inverse(self, dve):
        dve.wait_ge(self.s_std, 1)
        dve.reciprocal(self.rstd[:], self.std[:]).then_inc(self.s_rs, 1)
        dve.wait_ge(self.s_rs, 1)
        dve.wait_ge(self.s_mv, NT)
        dve.scalar_tensor_tensor(out=self.shift[:], in0=self.mv[:, :, 0], scalar=-1.0, in1=self.rstd[:],
                                 op0=ALU.mult, op1=ALU.mult).then_inc(self.s_sh, 1)

    def even_rows(self, dve):
        for t in range(0, NT, 2):
            dve.tensor_scalar(self.XN[:, t, :], self.X[:, t, :], self.mv[:, t, 0:1], self.rstd[:, t:t + 1],
                              ALU.subtract, ALU.mult).then_inc(self.s_xd, 1)

    def odd_rows(self, act):
        act.wait_ge(self.s_sh, 1)
        for t in range(1, NT, 2):
            act.activation(self.XN[:, t, :], self.X[:, t, :], ACT.Identity, bias=self.shift[:, t:t + 1],
                           scale=self.rstd[:, t:t + 1]).then_inc(self.s_xa, 1)

    def wait(self, eng):
        eng.wait_ge(self.s_xd, NT // 2)
        eng.wait_ge(self.s_xa, NT // 2)


def stage_norm(chip, name):
    with ExitStack() as st:
        norm = Norm(chip, name, st)
        block = st.enter_context(chip.nc.Block())

        @block.vector
        def _(dve):
            norm.moments(dve)
            norm.inverse(dve)
            norm.even_rows(dve)

        @block.scalar
        def _(act):
            norm.root(act)
            norm.odd_rows(act)


def stage_end(chip, out):
    with ExitStack() as st:
        block = st.enter_context(chip.nc.Block())

        @block.sync
        def _(sp):
            sp.dma_start(out.rearrange("b (t p) c -> p (b t) c", p=P), chip.X[:]).then_inc(chip.stored, 16)
            sp.wait_ge(chip.stored, 16)


def stage_mamba(chip, name, bc_dram, in_w, conv_w, conv_b, x_w, dt_w, dt_b, a_log, d_skip):
    nc, X, XN, ctxT, ident = chip.nc, chip.X, chip.XN, chip.ctxT, chip.ident
    EB = in_w.shape[0] // P
    R = dt_w.shape[1]
    N = a_log.shape[1]
    TAPS = conv_w.shape[1]
    W = R + 2 * N
    with ExitStack() as st:
        def sb(n, shape, dt=F32):
            return chip.sb(f"{name}_{n}", shape, dt, st)

        def sem(n):
            return chip.sem(f"{name}_{n}")

        in_T, x_T, dt_T = sb("in_T", [P, KC, EB * P]), sb("x_T", [P, EB, W]), sb("dt_T", [R, EB * P])
        small = sb("small", [P, EB, TAPS + 3])
        a_in, a_neg = sb("a_in", [P, EB, N]), sb("a_neg", [P, EB, N])
        skip = sb("skip", [P, EB, P])
        xin = sb("xin", [P, EB, TAPS - 1 + L])
        u, xdbl = sb("u", [P, EB, L]), sb("xdbl", [W, L])
        delta, du = ([sb(f"{n}{i}", [P, EB, L]) for i in range(2)] for n in ("delta", "du"))
        dA, dB, H = ([sb(f"{n}{i}", [P, EB, L]) for i in range(2)] for n in ("dA", "dB", "H"))
        NS = 4
        BC = [sb(f"BC{i}", [P, 2, L]) for i in range(NS)]
        in_rows, x_rows, dt_rows = H[0][:, :, 0:C], H[1][0:W, 0, :], dB[0][:, :, 0:R]
        norm = Norm(chip, name + "_norm", st)
        ps_y, ps_w = chip.ps(name + "_y", [P, EB, L], F32, st), chip.ps(name + "_w", [P, EB, L], F32, st)
        flat = "p e t -> p (e t)"

        def gate(b):
            return XN[:, b * TB:(b + 1) * TB, :]

        s_ld, s_wt, s_wc = sem("loaded"), sem("w_transposed"), sem("w_copied")
        s_a, s_skip, s_pad = sem("a"), sem("skip"), sem("padded")
        s_x, s_xin, s_conv, s_u = sem("x_proj_in"), sem("xin"), sem("conv"), sem("u")
        s_dbl, s_dblc, s_bcd = sem("xdbl"), sem("xdbl_copied"), sem("bc_stored")
        s_dt, s_ab, s_e, s_ln = sem("dt"), sem("dt_abs"), sem("dt_exp"), sem("dt_ln")
        s_c, s_err, s_log, s_del, s_du = sem("dve_chain"), sem("log_error"), sem("log"), sem("delta"), sem("du")
        s_bc = [sem(f"bc_loaded{i}") for i in range(NS)]
        s_dA, s_dB, s_sc, s_hc, s_acc = sem("dA"), sem("dB"), sem("scanned"), sem("hc"), sem("accumulated")
        s_z, s_y0, s_yz, s_yt, s_add = sem("gate"), sem("y_start"), sem("gated"), sem("y_transposed"), sem("added")
        block = st.enter_context(nc.Block())

        PROJECT, GATED, COPY_IN, CONV, TURN, ADD, SILU = 2, 1, 2, 3, 5, 7, 8
        XDBL, STEP, COPY_XDBL, EXP, LOG, ERROR, ADD_ERROR, DELTA = 8, 10, 11, 13, 14, 14, 15, 15

        @block.sync
        def _(sp):
            sp.dma_start(in_rows, in_w.rearrange("(e p) c -> p e c", p=P)).then_inc(s_ld, 16)
            sp.dma_start(x_rows, x_w).then_inc(s_ld, 16)
            sp.dma_start(dt_rows, dt_w.rearrange("(e p) c -> p e c", p=P)).then_inc(s_ld, 16)
            sp.dma_start(small[:, :, 0:TAPS], conv_w.rearrange("(e p) c -> p e c", p=P)).then_inc(s_ld, 16)
            for i, v in enumerate((conv_b, dt_b, d_skip)):
                sp.dma_start(small[:, :, TAPS + i:TAPS + i + 1],
                             v.rearrange("(e p o) -> p e o", p=P, o=1), allow_slow_non_contiguous=True).then_inc(s_ld, 16)
            sp.dma_start(a_in[:], a_log.rearrange("(e p) c -> p e c", p=P)).then_inc(s_ld, 16)
            for b in range(B):
                sp.wait_ge(s_dblc, b + 1)
                sp.dma_start(bc_dram[b], xdbl[R:W, :]).then_inc(s_bcd, 16)
                sp.wait_ge(s_bcd, 16 * (b + 1))
                for s in range(N):
                    n = b * N + s
                    if n >= NS:
                        sp.wait_ge(s_hc, n - NS + 1)
                    sp.dma_start(BC[n % NS][:], bc_dram[b].rearrange("(w n) t -> n w t", w=2)[s:s + 1].broadcast_to(
                        [P, 2, L])).then_inc(s_bc[n % NS], 16)

        @block.tensor
        def _(pe):
            pe.wait_ge(s_ld, 128)
            for e in range(EB):
                for k in range(KC):
                    m = pe.transpose(ps_w[:, k, e * P:(e + 1) * P], in_rows[:, e, k * P:(k + 1) * P], ident[:])
                m = pe.transpose(ps_w[:, 2, e * W:(e + 1) * W], x_rows[:, e * P:(e + 1) * P], ident[0:W, 0:W])
                m = pe.transpose(ps_w[0:R, 3, e * P:(e + 1) * P], dt_rows[:, e, :], ident[:])
            m.then_inc(s_wt, 1)
            pe.wait_ge(s_wc, 3)
            pe.wait_ge(s_skip, EB)

            def project(b, e):
                if e == 0 and b:
                    pe.wait_ge(s_del, b)
                if e == 0 and b >= 3:
                    pe.wait_ge(s_add, b - 2)
                for k in range(KC):
                    m = pe.matmul(ps_w[:, e, :], in_T[:, k, e * P:(e + 1) * P],
                                  ctxT[:, k, b * L:(b + 1) * L], start=(k == 0), stop=(k == KC - 1))
                m.then_inc(s_x, 1)

            def xdbl_product(b):
                pe.wait_ge(s_u, b + 1)
                if b >= 2:
                    pe.wait_ge(s_add, b - 1)
                for e in range(EB):
                    m = pe.matmul(ps_w[0:W, 0, :], x_T[:, e, :], u[:, e, :], start=(e == 0), stop=(e == EB - 1))
                m.then_inc(s_dbl, 1)

            def step_product(b):
                pe.wait_ge(s_dblc, b + 1)
                for e in range(EB):
                    m = pe.matmul(ps_w[:, e, :], dt_T[:, e * P:(e + 1) * P], xdbl[0:R, :], start=True, stop=True)
                m.then_inc(s_dt, 1)

            def y_start(b):
                if b:
                    pe.wait_ge(s_yz, b)
                for e in range(EB):
                    m = pe.matmul(ps_y[:, e, :], skip[:, e, :], u[:, e, :], start=True, stop=True)
                m.then_inc(s_y0, 1)

            def turn_y(b):
                pe.wait_ge(s_yz, b + 1)
                if b + 2 < B:
                    pe.wait_ge(s_xin, (b + 3) * EB)
                for t in range(TB):
                    for e in range(EB):
                        m = pe.transpose(ps_w[:, t, e * P:(e + 1) * P], gate(b)[:, e, t * P:(t + 1) * P], ident[:])
                    m.then_inc(s_yt, 1)

            for e in range(EB):
                project(0, e)
            xdbl_product(0)
            step_product(0)
            for b in range(B):
                if b + 1 < B:
                    for e in range(PROJECT):
                        project(b + 1, e)
                y_start(b)
                for s in range(N):
                    if s == TURN and b:
                        turn_y(b - 1)
                    if b + 1 < B:
                        if PROJECT <= s < EB:
                            project(b + 1, s)
                        if s == XDBL:
                            xdbl_product(b + 1)
                        if s == STEP:
                            step_product(b + 1)
                    pe.wait_ge(s_hc, b * N + s + 1)
                    for e in range(EB):
                        m = pe.matmul(ps_y[:, e, :], ident[:], H[s % 2][:, e, :], start=False, stop=True,
                                      skip_group_check=True)
                    m.then_inc(s_acc, 1)
            turn_y(B - 1)

        @block.scalar
        def _(act):
            act.wait_ge(s_ld, 128)
            act.activation(a_neg[:], a_in[:], ACT.Exp).then_inc(s_a, 1)
            act.wait_ge(s_wt, 1)
            act.copy(in_T[:], ps_w[:, 0:KC, :]).then_inc(s_wc, 1)
            act.copy(x_T[:], ps_w[:, 2, 0:EB * W].rearrange("p (e w) -> p e w", e=EB)).then_inc(s_wc, 1)
            act.copy(dt_T[:], ps_w[0:R, 3, :]).then_inc(s_wc, 1)
            act.wait_ge(s_pad, 4)
            norm.root(act)

            def copy_in(b, e):
                act.wait_ge(s_x, b * EB + e + 1)
                if b:
                    act.wait_ge(s_err, b)
                    act.wait_ge(s_ln, b)
                act.copy(xin[:, e, TAPS - 1:], ps_w[:, e, :]).then_inc(s_xin, 1)

            def silus(b):
                act.wait_ge(s_conv, b + 1)
                if b:
                    act.wait_ge(s_du, b)
                    act.wait_ge(s_y0, b)
                act.activation(u[:], delta[b % 2][:], ACT.Silu).then_inc(s_u, 1)
                for g in (0, 1) if b == 1 else (b,):
                    if b:
                        norm.wait(act)
                        act.activation(gate(g), gate(g), ACT.Silu).then_inc(s_z, 1)

            def copy_xdbl(b):
                act.wait_ge(s_dbl, b + 1)
                if b:
                    act.wait_ge(s_bcd, 16 * b)
                    act.wait_ge(s_dt, b)
                act.copy(xdbl[:], ps_w[0:W, 0, :]).then_inc(s_dblc, 1)

            def exp_part(b):
                act.wait_ge(s_dt, b + 1)
                act.wait_ge(s_u, b + 1)
                for e in range(EB):
                    act.activation(delta[b % 2][:, e, :], ps_w[:, e, :], ACT.Abs,
                                   bias=small[:, e, TAPS + 1:TAPS + 2]).then_inc(s_ab, 1)
                act.wait_ge(s_ab, (b + 1) * EB)
                act.activation(xin[:, :, TAPS - 1:], delta[b % 2][:], ACT.Exp, scale=-1.0).then_inc(s_e, 1)

            def log_part(b):
                act.wait_ge(s_e, b + 1)
                act.activation(delta[b % 2][:], xin[:, :, TAPS - 1:], ACT.Ln, bias=1.0).then_inc(s_ln, 1)

            for e in range(EB):
                copy_in(0, e)
            silus(0)
            copy_xdbl(0)
            exp_part(0)
            log_part(0)
            norm.odd_rows(act)
            for b in range(B):
                act.wait_ge(s_del, b + 1)
                for s in range(N):
                    if b + 1 < B:
                        if COPY_IN <= s < COPY_IN + EB:
                            copy_in(b + 1, s - COPY_IN)
                        if s == SILU:
                            silus(b + 1)
                        if s == COPY_XDBL:
                            copy_xdbl(b + 1)
                        if s == EXP:
                            exp_part(b + 1)
                        if s == LOG:
                            log_part(b + 1)
                    n = b * N + s
                    if n >= 2:
                        act.wait_ge(s_sc, n - 1)
                    for e in range(EB):
                        act.activation(dA[s % 2][:, e, 1:], delta[b % 2][:, e, 1:], ACT.Exp,
                                       scale=a_neg[:, e, s:s + 1]).then_inc(s_dA, 1)

        @block.gpsimd
        def _(pool):
            def add_error(b):
                pool.wait_ge(s_ln, b + 1)
                pool.wait_ge(s_err, b + 1)
                pool.tensor_tensor(delta[b % 2][:], delta[b % 2][:], du[b % 2][:], ALU.add).then_inc(s_log, 1)

            add_error(0)
            for b in range(B):
                for s in range(N):
                    if b + 1 < B:
                        if s == ADD_ERROR:
                            add_error(b + 1)
                    n = b * N + s
                    pool.wait_ge(s_du, b + 1)
                    pool.wait_ge(s_bc[n % NS], 16 * (n // NS + 1))
                    if n >= 2:
                        pool.wait_ge(s_sc, n - 1)
                    pool.tensor_tensor(dB[s % 2][:], du[b % 2][:], BC[n % NS][:, 0:1, :].broadcast_to([P, EB, L]),
                                       ALU.mult).then_inc(s_dB, 1)

        @block.vector
        def _(dve):
            ch = Chain(dve, s_c)
            dve.memset(xin[:, :, 0:TAPS - 1], 0.0).then_inc(s_pad, 1)
            dve.wait_ge(s_a, 1)
            dve.tensor_scalar(a_neg[:], a_neg[:], -1.0, None, ALU.mult).then_inc(s_pad, 1)
            dve.wait_ge(s_ld, 128)
            for e in range(EB):
                dve.tensor_scalar(skip[:, e, :], ident[:], small[:, e, TAPS + 2:TAPS + 3], None,
                                  ALU.mult).then_inc(s_skip, 1)
            for i in range(2):
                dve.memset(dA[i][:, :, 0:1], 0.0).then_inc(s_pad, 1)
            dve.wait_ge(s_pad, 4)
            norm.moments(dve)

            def conv(b, e):
                w, out = small[:, e, :], delta[b % 2][:, e, :]
                dve.wait_ge(s_xin, b * EB + e + 1)
                ch.step(dve.tensor_scalar(out, xin[:, e, 0:L], w[:, 0:1], w[:, TAPS:TAPS + 1],
                                          ALU.mult, ALU.add))
                for i in range(1, TAPS):
                    last = dve.scalar_tensor_tensor(out=out, in0=xin[:, e, i:i + L],
                                                    scalar=w[:, i:i + 1], in1=out,
                                                    op0=ALU.mult, op1=ALU.add)
                    ch.step(last)
                if e == EB - 1:
                    dve.sem_inc(s_conv, 1)

            def log_error(b):
                ex, t = xin[:, :, TAPS - 1:], du[b % 2]
                dve.wait_ge(s_e, b + 1)
                ch.step(dve.tensor_scalar(t[:], ex, 1.0, -1.0, ALU.add, ALU.add))
                dve.tensor_tensor(t[:], ex, t[:], ALU.subtract).then_inc(s_err, 1)

            def softplus(b):
                t = du[b % 2]
                dve.wait_ge(s_log, b + 1)
                dve.wait_ge(s_dt, b + 1)
                for e in range(EB):
                    last = dve.tensor_scalar(t[:, e, :], ps_w[:, e, :], small[:, e, TAPS + 1:TAPS + 2], 0.0,
                                             ALU.add, ALU.max)
                ch.step(last)
                dve.tensor_tensor(delta[b % 2][:], delta[b % 2][:], t[:], ALU.add).then_inc(s_del, 1)
                dve.wait_ge(s_del, b + 1)
                dve.wait_ge(s_u, b + 1)
                dve.tensor_tensor(t[:], delta[b % 2][:], u[:], ALU.mult).then_inc(s_du, 1)

            def gated(b):
                dve.wait_ge(s_acc, (b + 1) * N)
                dve.wait_ge(s_z, b + 1)
                dve.tensor_tensor(gate(b), gate(b), ps_y[:], ALU.mult).then_inc(s_yz, 1)

            def add_y(b):
                for t in range(TB):
                    dve.wait_ge(s_yt, b * TB + t + 1)
                    at = X[:, b * TB + t, :]
                    last = dve.tensor_tensor(at, at, ps_w[:, t, :], ALU.add)
                last.then_inc(s_add, 1)

            for e in range(EB):
                conv(0, e)
            log_error(0)
            norm.inverse(dve)
            norm.even_rows(dve)
            softplus(0)
            for b in range(B):
                for s in range(N):
                    if b and s == GATED:
                        gated(b - 1)
                    if b and s == ADD:
                        add_y(b - 1)
                    if b + 1 < B:
                        if CONV <= s < CONV + EB:
                            conv(b + 1, s - CONV)
                        if s == ERROR:
                            log_error(b + 1)
                        if s == DELTA:
                            softplus(b + 1)
                    n, i = b * N + s, s % 2
                    dve.wait_ge(s_dA, (n + 1) * EB)
                    dve.wait_ge(s_dB, n + 1)
                    if n >= 2:
                        dve.wait_ge(s_acc, n - 1)
                    dve.tensor_tensor_scan(H[i][:].rearrange(flat), dA[i][:].rearrange(flat),
                                           dB[i][:].rearrange(flat), 0.0, ALU.mult, ALU.add).then_inc(s_sc, 1)
                    dve.wait_ge(s_sc, n + 1)
                    dve.wait_ge(s_bc[n % NS], 16 * (n // NS + 1))
                    dve.tensor_tensor(H[i][:], H[i][:], BC[n % NS][:, 1:2, :].broadcast_to([P, EB, L]),
                                      ALU.mult).then_inc(s_hc, 1)
            gated(B - 1)
            add_y(B - 1)


def transpose_norm(chip, name, xnT):
    XN, ident = chip.XN, chip.ident
    with ExitStack() as st:
        pt = chip.ps(name + "_pt", [P, 8, BANK], F32, st)
        s_t, s_a, s_d = chip.sem(name + "_t"), chip.sem(name + "_act"), chip.sem(name + "_dve")
        block = st.enter_context(chip.nc.Block())
        width = xnT.shape[1]

        @block.tensor
        def _(pe):
            for t in range(NT):
                for g in range(1):
                    if t >= 8:
                        pe.wait_ge((s_a, s_d)[t % 2], (t - 8) // 2 + 1)
                    for k in range(width):
                        m = pe.transpose(pt[:, t % 8, k * P:(k + 1) * P], XN[:, t, k * P:(k + 1) * P], ident[:])
                    m.then_inc(s_t, 1)

        @block.scalar
        def _(act):
            for t in range(0, NT, 2):
                act.wait_ge(s_t, t + 1)
                act.copy(xnT[:, :, t * P:(t + 1) * P],
                         pt[:, t % 8, :].rearrange("p (k t) -> p k t", k=width)).then_inc(s_a, 1)

        @block.vector
        def _(dve):
            for t in range(1, NT, 2):
                dve.wait_ge(s_t, t + 1)
                dve.tensor_copy(xnT[:, :, t * P:(t + 1) * P],
                                pt[:, t % 8, :].rearrange("p (k t) -> p k t", k=width)).then_inc(s_d, 1)


X_UP = 2.0 ** 10
W_UP = 8


def transpose_norm_split(chip, name, high, low):
    XN, ident = chip.XN, chip.ident
    with ExitStack() as st:
        pt = chip.ps(name + "_pt", [P, 8, BANK], F32, st)
        s_t, s_h, s_l = chip.sem(name + "_t"), chip.sem(name + "_high"), chip.sem(name + "_low")
        block = st.enter_context(chip.nc.Block())

        def at(x, t):
            return x[:, :, t * P:(t + 1) * P]

        def bank(t):
            return pt[:, t % 8, :].rearrange("p (k t) -> p k t", k=KD)

        @block.tensor
        def _(pe):
            for t in range(NT):
                if t >= 8:
                    pe.wait_ge(s_l, t - 7)
                for k in range(KD):
                    m = pe.transpose(pt[:, t % 8, k * P:(k + 1) * P], XN[:, t, k * P:(k + 1) * P], ident[:])
                m.then_inc(s_t, 1)

        @block.scalar
        def _(act):
            for t in range(NT):
                act.wait_ge(s_t, t + 1)
                act.activation(at(high, t), bank(t), ACT.Copy, scale=X_UP).then_inc(s_h, 1)

        @block.vector
        def _(dve):
            for t in range(NT):
                dve.wait_ge(s_h, t + 1)
                dve.scalar_tensor_tensor(out=at(low, t), in0=bank(t), scalar=X_UP, in1=at(high, t),
                                         op0=ALU.mult, op1=ALU.subtract).then_inc(s_l, 1)


def stage_ffn4(chip, name, gate_w, gate_s, up_w, up_s, down_w, down_s):
    nc, X, XN, ident = chip.nc, chip.X, chip.XN, chip.ident
    F = gate_w.shape[0]
    G = F // 512
    R = 4
    NM = 3
    BLK = 512 // (gate_s.shape[1])
    NS = 512 // BLK
    SLOTS = 16
    with ExitStack() as st:
        def sb(n, shape, dt=F32):
            return chip.sb(f"{name}_{n}", shape, dt, st)

        def sem(n):
            return chip.sem(f"{name}_{n}")

        xh, xl = sb("xn_high", [P, KD, B * L], F16), sb("xn_low", [P, KD, B * L], F16)
        transpose_norm_split(chip, name + "_xnT", xh, xl)
        pk = [sb(f"packed{m}", [P, R, 256], I32) for m in range(NM)]
        sc = [sb(f"scales{m}", [P, R, NS]) for m in range(NM)]
        code = [sb(f"code{i}", [P, R, 256], I32) for i in range(2)]
        sign = [sb(f"sign{i}", [P, R, 256], I32) for i in range(2)]
        mag = [sb(f"mag{i}", [P, R, 256]) for i in range(2)]
        sgn = [s[:].bitcast(F32) for s in sign]
        sgs = sb("signed_scale", [P, R, 256])
        V = [XN[:, m * R:(m + 1) * R, :] for m in range(NM)]
        WH, WL = ([[sb(f"w{n}{i}_{m}", [P, R, 512], F16) for m in range(2)] for i in range(2)] for n in "hl")
        WD = [sb(f"wdown{i}", [P, R, 512]) for i in range(2)]
        expo, inv = sb("exponent", [P, R, NS], I32), sb("inverse_power", [P, R], I32)
        power, back = sb("power", [P, R]), [sb(f"power_back{i}", [P, 2, R]) for i in range(2)]
        gel = [XN[:, NM * R + i, :] for i in range(2)]
        inter = [XN[:, NM * R + 2 + i, :] for i in range(2)]
        ps_acc = chip.ps(name + "_acc", [P, TB, D], F32, st)
        ps_g, ps_u = chip.ps(name + "_g", [P, 512], F32, st), chip.ps(name + "_u", [P, 512], F32, st)
        ps_t = chip.ps(name + "_t", [P, 2, 512], F32, st)

        s_pk = [sem(f"packed{m}") for m in range(NM)]
        s_code, s_sgn, s_mag, s_sgs, s_pc, s_V = sem("code"), sem("sgn"), sem("mag"), sem("sgs"), sem("pool"), sem("V")
        s_t, s_wt = sem("transposed"), sem("wT")
        s_g, s_u, s_gel, s_int, s_dn = sem("gate"), sem("up"), sem("gelu"), sem("inter"), sem("down")
        s_fold, s_lo, s_pow, s_norm = sem("folded"), sem("low"), sem("power"), sem("scale_normed")
        block = st.enter_context(nc.Block())


        @block.sync
        def _(sp):
            def load(g, first=False):
                for m, (w, s) in enumerate(((gate_w, gate_s), (up_w, up_s), (down_w, down_s))):
                    at = bass.ds(g * 512, 512), bass.ds(g * 256, 256), bass.ds(g * NS, NS)
                    src, ssrc = (w[at[0], :], s[at[0], :]) if m < 2 else (w[:, at[1]], s[:, at[2]])
                    if not first:
                        sp.wait_ge(s_V, (g - 1) * 6 + 2 * m + 4)
                    sp.dma_start(pk[m][:], src.rearrange("(r p) c -> p r c", p=P)).then_inc(s_pk[m], 16)
                    sp.dma_start(sc[m][:], ssrc.rearrange("(r p) c -> p r c", p=P)).then_inc(s_pk[m], 16)

            load(0, first=True)
            with sp.Fori(1, G) as g:
                load(g)

        def dve_decode(dve, g, step):
            m, nib, op = step // 12, step // 6 % 2, step % 6
            unit, i = g * 6 + m * 2 + nib, nib
            if op == 0:
                dve.wait_ge(s_pk[m], 32 * (g + 1))
                dve.wait_ge(s_V, unit + 1)
                dve.tensor_scalar(code[i][:], pk[m][:], 4 * nib, 7, ALU.logical_shift_right,
                                  ALU.bitwise_and).then_inc(s_code, 1)
            elif op == 1:
                dve.tensor_scalar(sign[i][:], pk[m][:], 4 * nib, 8, ALU.logical_shift_right,
                                  ALU.bitwise_and).then_inc(s_code, 1)
            elif op == 2:
                dve.wait_ge(s_code, 2 * unit + 2)
                dve.tensor_scalar(sgn[i], sign[i][:], -0.25, 1.0, ALU.mult, ALU.add).then_inc(s_sgn, 1)
            elif op == 3:
                dve.tensor_scalar(mag[i][:], code[i][:], 2.0, -8.0, ALU.mult, ALU.add).then_inc(s_mag, 1)
            elif op == 4:
                dve.wait_ge(s_mag, 3 * unit + 1)
                dve.scalar_tensor_tensor(out=mag[i][:], in0=code[i][:], scalar=-2.0, in1=mag[i][:],
                                         op0=ALU.add, op1=ALU.max).then_inc(s_mag, 1)
            else:
                dve.wait_ge(s_mag, 3 * unit + 2)
                dve.scalar_tensor_tensor(out=mag[i][:], in0=code[i][:], scalar=0.5, in1=mag[i][:],
                                         op0=ALU.mult, op1=ALU.max).then_inc(s_mag, 1)

        def normed_scales(dve, g, gb, m):
            n = g * 2 + m
            dve.wait_ge(s_pk[m], 32 * (g + 1))
            dve.tensor_scalar(expo[:], sc[m][:].bitcast(I32), 0x7F800000, None, ALU.bitwise_and).then_inc(s_pow, 1)
            dve.wait_ge(s_pow, n * 4 + 1)
            dve.tensor_reduce(power[:], expo[:].bitcast(F32), AX.X, ALU.max).then_inc(s_pow, 1)
            dve.wait_ge(s_pow, n * 4 + 2)
            dve.tensor_scalar(power[:], power[:], 2.0 ** -100, 2.0 ** 100, ALU.max, ALU.min).then_inc(s_pow, 1)
            dve.wait_ge(s_pow, n * 4 + 3)
            dve.tensor_scalar(inv[:], power[:].bitcast(I32), -1.0, float((254 + W_UP) << 23), ALU.mult,
                              ALU.add).then_inc(s_pow, 1)
            dve.tensor_scalar(back[gb][:, m, :], power[:], 2.0 ** -W_UP / X_UP, None, ALU.mult).then_inc(s_norm, 1)
            dve.wait_ge(s_pow, n * 4 + 4)
            dve.tensor_tensor(sc[m][:], sc[m][:], inv[:].bitcast(F32).rearrange("p (r o) -> p r o", o=1).broadcast_to(
                [P, R, NS]), ALU.mult).then_inc(s_norm, 1)

        def dve_low(dve, g, gb, m, r):
            n = g * 8 + m * 4 + r
            dve.wait_ge(s_wt, g * 12 + m * 4 + r + 3)
            cols = slice(r * P, (r + 1) * P)
            dve.tensor_tensor(WL[gb][m][:, :, cols], ps_t[:, r % 2, :].rearrange("p (k c) -> p k c", k=4),
                              WH[gb][m][:, :, cols], ALU.subtract).then_inc(s_lo, 1)

        def pe_transposes(pe, g, m, r):
            n = g * 12 + m * 4 + r
            pe.wait_ge(s_V, g * 6 + 2 * m + 4)
            pe.wait_ge(s_wt, n + 1)
            if m * 4 + r < 10:
                pe.wait_ge(s_lo, g * 8 + m * 4 + r + 1)
            for k in range(4):
                t = pe.transpose(ps_t[:, r % 2, k * P:(k + 1) * P], V[m][:, r, k * P:(k + 1) * P], ident[:])
            t.then_inc(s_t, 1)

        def act_wT(act, g, gb, m, r):
            n = g * 12 + m * 4 + r
            act.wait_ge(s_t, n + 1)
            act.copy((WH[gb] + [WD[gb]])[m][:, :, r * P:(r + 1) * P],
                     ps_t[:, r % 2, :].rearrange("p (k c) -> p k c", k=4)).then_inc(s_wt, 1)

        @block.tensor
        def _(pe):
            pe.sem_inc(s_dn, 2)

            def down(g, gb, q):
                n = g * SLOTS + q
                pe.wait_ge(s_int, n + 2)
                if q % 4 == 0:
                    pe.wait_ge(s_fold, g * 4 + q // 4 + 1)
                for t in range(TB):
                    m = pe.matmul(ps_acc[:, t, :], inter[q % 2][:, t * P:(t + 1) * P], WD[gb][:, q % 4, :],
                                  start=(q % 4 == 0), stop=(q % 4 == 3))
                m.then_inc(s_dn, 1)

            def product(out, gb, m, cols, toks):
                for k in range(KD):
                    w = WH[gb][m][:, k, cols], WL[gb][m][:, k, cols]
                    pe.matmul(out, w[0], xh[:, k, toks], start=(k == 0), stop=False)
                    pe.matmul(out, w[0], xl[:, k, toks], start=False, stop=False)
                    last = pe.matmul(out, w[1], xh[:, k, toks], start=False, stop=(k == KD - 1))
                return last

            def group(g, gb, prepare):
                pe.wait_ge(s_wt, g * 12 + 12 + 2)
                pe.wait_ge(s_lo, g * 8 + 8 + 2)
                for q in range(SLOTS):
                    tc, nt = q // 4, q % 4
                    n = g * SLOTS + q
                    cols = slice(nt * P, (nt + 1) * P)
                    toks = slice(tc * 512, (tc + 1) * 512)
                    pe.wait_ge(s_gel, n + 1)
                    product(ps_g[:], gb, 0, cols, toks).then_inc(s_g, 1)
                    if prepare and q >= 4:
                        pe_transposes(pe, g + 1, (q - 4) // 4, q % 4)
                    pe.wait_ge(s_int, n + 1)
                    product(ps_u[:], gb, 1, cols, toks).then_inc(s_u, 1)
                    if q:
                        down(g, gb, q - 1)
                down(g, gb, SLOTS - 1)

            for m in range(NM):
                for r in range(R):
                    pe_transposes(pe, 0, m, r)
            with pe.Fori(0, G // 2 - 1) as h:
                group(h * 2, 0, True)
                group(h * 2 + 1, 1, True)
            group(G - 2, 0, True)
            group(G - 1, 1, False)

        @block.scalar
        def _(act):
            act.sem_inc(s_gel, 1)
            act.sem_inc(s_wt, 2)

            def group(g, gb, prepare):
                for q in range(SLOTS):
                    n = g * SLOTS + q
                    act.wait_ge(s_g, n + 1)
                    act.wait_ge(s_int, n + 1)
                    if q == 0:
                        act.wait_ge(s_norm, g * 4 + 4)
                    act.activation(gel[q % 2], ps_g[:], ACT.Gelu_apprx_tanh,
                                   scale=back[gb][:, 0, q % 4:q % 4 + 1]).then_inc(s_gel, 1)
                    if prepare and q >= 4:
                        if q == 4:
                            act.wait_ge(s_dn, g * SLOTS + 2)
                        act_wT(act, g + 1, 1 - gb, (q - 4) // 4, q % 4)

            for m in range(NM):
                for r in range(R):
                    act_wT(act, 0, 0, m, r)
            with act.Fori(0, G // 2 - 1) as h:
                group(h * 2, 0, True)
                group(h * 2 + 1, 1, True)
            group(G - 2, 0, True)
            group(G - 1, 1, False)

        @block.gpsimd
        def _(pool):
            pool.sem_inc(s_V, 2)

            def unit(g, m, nib, first):
                n = g * 6 + m * 2 + nib
                i = nib
                pool.wait_ge(s_sgn, n + 1)
                if m < 2:
                    pool.wait_ge(s_norm, g * 4 + 2 * m + 2)
                pool.wait_ge(s_V, n + 2)
                v, sg = (x.rearrange("p r (s c) -> p (r s) c", c=BLK // 2) for x in (sgs[:], sgn[i]))
                pool.tensor_tensor(v, sg, sc[m][:].rearrange("p r (s o) -> p (r s) o", o=1).broadcast_to(
                    [P, R * NS, BLK // 2]), ALU.mult).then_inc(s_pc, 1)
                pool.wait_ge(s_pc, n + 1)
                pool.wait_ge(s_mag, 3 * n + 3)
                if nib == 0:
                    if not first:
                        pool.wait_ge(s_t, (g - 1) * 12 + m * 4 + 4)
                dst = V[m].rearrange("p r (c two) -> p r c two", two=2)[:, :, :, nib]
                pool.tensor_tensor(dst, mag[i][:], sgs[:], ALU.mult).then_inc(s_V, 1)

            def decode(g, first=False):
                for m in range(NM):
                    for nib in range(2):
                        unit(g, m, nib, first)

            decode(0, first=True)
            with pool.Fori(1, G) as g:
                decode(g)

        @block.vector
        def _(dve):
            dve.sem_inc(s_int, 1)
            dve.sem_inc(s_fold, 1)
            dve.sem_inc(s_lo, 2)

            def fold(g, tc):
                dve.wait_ge(s_dn, g * SLOTS + 4 * tc + 4 + 2)
                x = X[:, tc * TB:(tc + 1) * TB, :]
                if tc == 0:
                    dve.wait_ge(s_fold, g * 4 + 1)
                dve.tensor_tensor(x, x, ps_acc[:], ALU.add).then_inc(s_fold, 1)

            def group(g, gb, prepare):
                for q in range(SLOTS):
                    n = g * SLOTS + q
                    dve.wait_ge(s_u, n + 1)
                    dve.wait_ge(s_gel, n + 2)
                    dve.wait_ge(s_dn, n + 1)
                    dve.scalar_tensor_tensor(out=inter[q % 2], in0=ps_u[:], scalar=back[gb][:, 1, q % 4:q % 4 + 1],
                                             in1=gel[q % 2], op0=ALU.mult, op1=ALU.mult).then_inc(s_int, 1)
                    if prepare:
                        if q < 2:
                            normed_scales(dve, g + 1, 1 - gb, q)
                        if q < 9:
                            for s in range(4 * q, 4 * q + 4):
                                dve_decode(dve, g + 1, s)
                        if 4 <= q < 12:
                            dve_low(dve, g + 1, 1 - gb, (q - 4) // 4, q % 4)
                    if q % 4 == 0 and q:
                        fold(g, q // 4 - 1)
                fold(g, 3)

            for m in range(2):
                normed_scales(dve, 0, 0, m)
            for s in range(36):
                dve_decode(dve, 0, s)
            for m in range(2):
                for r in range(R):
                    dve_low(dve, 0, 0, m, r)
            with dve.Fori(0, G // 2 - 1) as h:
                group(h * 2, 0, True)
                group(h * 2 + 1, 1, True)
            group(G - 2, 0, True)
            group(G - 1, 1, False)


def stage_mix(chip, name, wq, bq, wk, bk):
    nc, X, XN, ctxT, ident = chip.nc, chip.X, chip.XN, chip.ctxT, chip.ident
    DH = wq.shape[0]
    with ExitStack() as st:
        def sb(n, shape, dt=F32):
            return chip.sb(f"{name}_{n}", shape, dt, st)

        def sem(n):
            return chip.sem(f"{name}_{n}")

        w_rows, wT, bias = sb("w_rows", [DH, 2, C]), sb("wT", [P, 2, KC, DH]), sb("bias", [DH, 2])
        qkT = sb("qkT", [DH, 2, L])
        rows = sb("rows", [P, TB, D])
        top, tot, inv = sb("top", [P, TB]), sb("tot", [P, TB]), sb("inv", [P, TB])
        att = sb("att", [P, TB, L])
        xT, aT = sb("xT", [P, TB, L]), sb("aT", [P, TB, L])
        ps_e = chip.ps(name + "_e", [P, TB, L], F32, st)
        ps_t, ps_o = chip.ps(name + "_t", [P, 2, 512], F32, st), chip.ps(name + "_o", [P, 2, 512], F32, st)
        s_ld, s_w, s_wc = sem("loaded"), sem("wT"), sem("wT_copied")
        s_qk, s_qc, s_e, s_top, s_exp, s_inv, s_att = (sem(n) for n in (
            "qk", "qk_copied", "energy", "top", "exp", "inverse", "attention"))
        s_rows, s_t, s_tc, s_o, s_f = (sem(n) for n in ("rows", "t", "t_copied", "out", "folded"))
        block = st.enter_context(nc.Block())

        @block.sync
        def _(sp):
            for i, (w, v) in enumerate(((wq, bq), (wk, bk))):
                sp.dma_start(w_rows[:, i, :], w).then_inc(s_ld, 16)
                sp.dma_start(bias[:, i:i + 1], v.rearrange("(p o) -> p o", o=1)).then_inc(s_ld, 16)

        @block.gpsimd
        def _(pool):
            with pool.Fori(0, B) as b:
                pool.wait_ge(s_t, b * 8 + 1)
                pool.tensor_copy(rows[:], XN[:, bass.ds(b * TB, TB), :]).then_inc(s_rows, 1)

        @block.tensor
        def _(pe):
            pe.sem_inc(s_t, 1)
            pe.wait_ge(s_ld, 64)
            for i in range(2):
                for k in range(KC):
                    t = pe.transpose(ps_t[:, 0, (2 * i + k) * DH:(2 * i + k + 1) * DH],
                                     w_rows[:, i, k * P:(k + 1) * P], ident[:])
            t.then_inc(s_w, 1)
            pe.wait_ge(s_wc, 1)

            def turn(b, i, src):
                n = b * 8 + i
                pe.wait_ge(s_tc, n + 1)
                for c in range(TB):
                    t = pe.transpose(ps_t[:, i % 2, c * P:(c + 1) * P], src[:, i % TB, c * P:(c + 1) * P], ident[:])
                t.then_inc(s_t, 1)

            with pe.Fori(0, B) as b:
                pe.wait_ge(s_f, b * TB + 2)
                for i in range(2):
                    for k in range(KC):
                        m = pe.matmul(ps_o[:, i, :], wT[:, i, k, :], ctxT[:, k, bass.ds(b * L, L)],
                                      start=(k == 0), stop=(k == KC - 1))
                    m.then_inc(s_qk, 1)
                pe.wait_ge(s_qc, b * 2 + 2)
                for r in range(TB):
                    pe.matmul(ps_e[:, r, :], qkT[:, 0, r * P:(r + 1) * P], qkT[:, 1, :],
                              start=True, stop=True).then_inc(s_e, 1)
                pe.wait_ge(s_rows, b + 1)
                for i in range(TB):
                    turn(b, i, rows)
                for r in range(TB):
                    pe.wait_ge(s_att, b * TB + r + 1)
                    turn(b, TB + r, att)
                pe.wait_ge(s_tc, b * 8 + 8 + 2)
                for l in range(TB):
                    pe.wait_ge(s_f, b * TB + l + 1)
                    for c in range(TB):
                        m = pe.matmul(ps_o[:, l % 2, :], xT[:, c, l * P:(l + 1) * P], aT[:, c, :],
                                      start=(c == 0), stop=(c == TB - 1))
                    m.then_inc(s_o, 1)

        @block.scalar
        def _(act):
            act.sem_inc(s_tc, 2)
            act.wait_ge(s_w, 1)
            act.copy(wT[:].rearrange("p i k d -> p (i k d)"), ps_t[:, 0, 0:4 * DH]).then_inc(s_wc, 1)
            with act.Fori(0, B) as b:
                for i in range(2):
                    act.wait_ge(s_qk, b * 2 + i + 1)
                    act.activation(qkT[:, i, :], ps_o[:, i, :], ACT.Identity, bias=bias[:, i:i + 1]).then_inc(s_qc, 1)
                for r in range(TB):
                    act.wait_ge(s_top, b * TB + r + 1)
                    act.activation(att[:, r, :], ps_e[:, r, :], ACT.Exp, bias=top[:, r:r + 1],
                                   accum_out=tot[:, r:r + 1]).then_inc(s_exp, 1)
                for i in range(8):
                    act.wait_ge(s_t, b * 8 + i + 2)
                    dst = xT if i < TB else aT
                    act.copy(dst[:, :, i % TB * P:(i % TB + 1) * P],
                             ps_t[:, i % 2, :].rearrange("p (c t) -> p c t", c=TB)).then_inc(s_tc, 1)

        @block.vector
        def _(dve):
            dve.sem_inc(s_f, 2)
            with dve.Fori(0, B) as b:
                for r in range(TB):
                    dve.wait_ge(s_e, b * TB + r + 1)
                    dve.tensor_reduce(top[:, r:r + 1], ps_e[:, r, :], AX.X, ALU.max, negate=True).then_inc(s_top, 1)
                for r in range(TB):
                    dve.wait_ge(s_exp, b * TB + r + 1)
                    dve.reciprocal(inv[:, r:r + 1], tot[:, r:r + 1]).then_inc(s_inv, 1)
                    dve.wait_ge(s_inv, b * TB + r + 1)
                    dve.tensor_scalar(att[:, r, :], att[:, r, :], inv[:, r:r + 1], None, ALU.mult).then_inc(s_att, 1)
                for l in range(TB):
                    dve.wait_ge(s_o, b * TB + l + 1)
                    x = X[:, bass.ds(b * TB + l, 1), :].rearrange("p o d -> p (o d)")
                    dve.tensor_tensor(x, x, ps_o[:, l % 2, :], ALU.add).then_inc(s_f, 1)


class Heads:

    def __init__(self, nc, name, hd, k_heads, chunks, causal):
        self.H, self.hd, self.KH, self.chunks, self.causal = 16, hd, k_heads, chunks, causal
        self.U = B * (D // hd) // self.H
        self.VH = k_heads
        self.scale = float(hd) ** -0.5
        self.ROWS = len(chunks[0]) * hd
        assert self.ROWS + 2 <= P
        self.q = nc.dram_tensor(name + "_q_parts", (self.U, 3, self.H * hd, L), BF16).ap()
        self.k = nc.dram_tensor(name + "_k_parts", (self.U, 3, self.KH * hd, L), BF16).ap()
        self.v = nc.dram_tensor(name + "_v", (self.U, P, TB, self.VH * (hd + 1)), F32).ap()
        self.m = nc.dram_tensor(name + "_max", (self.U, 2, 2, self.H // 2, L), BF16).ap()


def attention_core(chip, name, hs, add):
    nc, X, XN, ident, identb = chip.nc, chip.X, chip.XN, chip.ident, chip.identb
    U, H, hd, KH, NCH, ROWS = hs.U, hs.H, hs.hd, hs.KH, len(hs.chunks), hs.ROWS
    V = hd + 1
    VP = -(-V // 32) * 32
    G = P // VP
    HH = H // 2
    NB = 3
    UB = U // B
    dst = X if add else XN
    with ExitStack() as st:
        def sb(n, shape, dt=F32):
            return chip.sb(f"{name}_{n}", shape, dt, st)

        def sem(n):
            return chip.sem(f"{name}_{n}")

        R0 = ROWS + 2
        qS = [[sb(f"q{i}_{c}", [R0 if c == 0 else ROWS, H, L], BF16) for c in range(NCH)] for i in range(NB)]
        kS = [[sb(f"k{i}_{c}", [R0 if c == 0 else ROWS, KH, L], BF16) for c in range(NCH)] for i in range(NB)]
        vS = [sb(f"v{i}", [P, TB, KH * V + VP - V]) for i in range(NB)]
        prob = [sb(f"prob{i}", [P, 2, L]) for i in range(2)]
        mx = [sb(f"minus_max{i}", [P, TB, H]) for i in range(2)]
        mh = [sb(f"max_parts{i}", [P, TB, 2, HH], BF16) for i in range(2)]
        mrow = [sb(f"max_rows{i}", [2 * HH, L], BF16) for i in range(2)]
        yT = sb("yT", [P, L])
        inv, y = sb("inv", [P, TB, G]), sb("y", [P, TB, G, hd])
        maskA, maskB = sb("mask_q", [P, P], BF16), sb("mask_k", [P, P], BF16)
        ps_a = chip.ps(name + "_a", [P, 2, 512], F32, st)
        ps_s = [chip.ps(f"{name}_s{i}", [P, 2, 512], F32, st) for i in range(2)]
        ps_v, ps_y = chip.ps(name + "_pv", [P, L], F32, st), chip.ps(name + "_turned", [P, TB, P], F32, st)
        heads_y = ps_y[:].rearrange("p q (g v) -> p q g v", g=G)
        ps_m = ps_a[0:2 * HH, 0, 0:TB * P // 2].bitcast(BF16).rearrange("p (q t) -> p q t", q=TB)

        s_in = [sem(f"stack{i}") for i in range(NB)]
        s_one, s_mask = sem("ones"), sem("mask")
        s_a, s_red, s_qk, s_exp, s_pv, s_norm, s_inv = (sem(n) for n in (
            "a", "reduced", "qk", "exp", "pv", "normalised", "inverse"))
        s_yc, s_yt = sem("y_copied"), sem("y_turned")
        s_mh, s_mt, s_mc, s_ms, s_ml = (sem(n) for n in ("m_parts", "m_turned", "m_copied", "m_stored", "m_loaded"))
        s_sp = sem("m_high")
        block = st.enter_context(nc.Block())
        UG = H // G

        def begins(u, g):
            return u == 0 and isinstance(g, int) and g == 0

        def unit_groups(eng, hh, group, between):
            g0, g1 = hh * (UG // 2), (hh + 1) * (UG // 2) - 1
            group(g0)
            between()
            if g1 > g0 + 1:
                with eng.Fori(1, g1 - g0) as i:
                    group(i + g0)
            group(g1, last=True)

        NIN = 2 * sum(len(c) for c in hs.chunks) + 1

        @block.sync
        def _(sp):
            def load(u):
                i = u % NB
                if u >= NB:
                    sp.wait_ge(s_pv, 2 * H * (u - NB + 1) + 2)
                for c, pairs in enumerate(hs.chunks):
                    for j, (qp, kp) in enumerate(pairs):
                        rows = slice(j * hd, (j + 1) * hd)
                        sp.dma_start(qS[i][c][rows], hs.q[u, qp].rearrange("(h d) t -> d h t", d=hd)
                                     ).then_inc(s_in[i], 16)
                        sp.dma_start(kS[i][c][rows], hs.k[u, kp].rearrange("(h d) t -> d h t", d=hd)
                                     ).then_inc(s_in[i], 16)
                sp.dma_start(vS[i][:, :, 0:KH * V], hs.v[u]).then_inc(s_in[i], 16)

            def max_rows(u, hh):
                n = 2 * u + hh
                sp.wait_ge(s_mc, n + 1)
                sp.dma_start(hs.m[u, hh].rearrange("a h t -> (a h) t"), mrow[hh][:]).then_inc(s_ms, 16)
                sp.wait_ge(s_ms, 16 * (n + 1))
                sp.dma_start(qS[u % NB][0][ROWS:R0, hh * HH:(hh + 1) * HH, :], hs.m[u, hh]).then_inc(s_ml, 16)

            for u in range(NB):
                load(u)
            for u in range(U):
                max_rows(u, 0)
                max_rows(u, 1)
                if u + NB - 1 < U and u >= 1:
                    load(u + NB - 1)

        @block.gpsimd
        def _(pool):
            for i in range(NB):
                pool.memset(kS[i][0][ROWS:R0], 1.0).then_inc(s_one, 1)
                pool.wait_ge(s_one, 2 * i + 1)
                pool.memset(vS[i][:, :, KH * V:], 1.0).then_inc(s_one, 1)
                pool.wait_ge(s_one, 2 * i + 2)
            pool.wait_ge(s_one, 2 * NB)
            if hs.causal:
                pool.memset(maskA[:], 0.0).then_inc(s_mask, 1)
                pool.memset(maskB[:], 0.0).then_inc(s_mask, 1)
                pool.wait_ge(s_mask, 2)
                pool.affine_select(out=maskA[:], in_=maskA[:], compare_op=ALU.is_ge, fill=-1e30, base=0,
                                   pattern=[[-1, P]], channel_multiplier=1).then_inc(s_mask, 1)
                pool.affine_select(out=maskB[:], in_=maskB[:], compare_op=ALU.is_ge, fill=-1e30, base=0,
                                   pattern=[[1, P]], channel_multiplier=-1).then_inc(s_mask, 1)

        @block.tensor
        def _(pe):
            def logits(out, lhs, rhs, cols, mask, diag, rows0):
                for c in range(NCH):
                    k = rows0 if c == 0 else ROWS
                    pe_last = pe.matmul(out[:, cols], lhs(c, k), rhs(c, k), start=(c == 0),
                                        stop=(c == NCH - 1 and not hs.causal))
                if hs.causal:
                    pe_last = pe.matmul(out[:, diag], identb[:], mask[:], start=False, stop=True)
                return pe_last

            turned = [0]

            def A(u, h, half):
                i, kh = u % NB, h if KH > 1 else 0
                if turned[0]:
                    pe.wait_ge(s_mc, turned[0])
                if half == 0:
                    pe.wait_ge(s_in[i], 16 * NIN * (u // NB + 1))
                for j in range(2):
                    qt = 2 * half + j
                    n4 = (u * H + h) * TB + qt
                    n = (qt + 1) * P if hs.causal else L
                    pe.wait_ge(s_red, n4 + 1)
                    logits(ps_a[:, j, :],
                           lambda c, k: qS[i][c][0:k, bass.ds(h, 1), qt * P:(qt + 1) * P].rearrange("p o t -> p (o t)"),
                           lambda c, k: kS[i][c][0:k, bass.ds(kh, 1), 0:n].rearrange("p o t -> p (o t)"),
                           slice(0, n), maskA, slice(qt * P, (qt + 1) * P), ROWS).then_inc(s_a, 1)

            def QK(u, h, pair):
                m2, i = (u * H + h) * 2 + pair, u % NB
                pe.wait_ge(s_exp, m2 + 1)
                for j in range(2):
                    kt = 2 * pair + j
                    q0 = kt * P if hs.causal else 0
                    kh = h if KH > 1 else 0
                    m = logits(ps_s[pair][:, j, :],
                               lambda c, k: kS[i][c][0:k, bass.ds(kh, 1), kt * P:(kt + 1) * P].rearrange("p o t -> p (o t)"),
                               lambda c, k: qS[i][c][0:k, bass.ds(h, 1), q0:L].rearrange("p o t -> p (o t)"),
                               slice(q0, L), maskB, slice(kt * P, (kt + 1) * P), R0)
                m.then_inc(s_qk, 1)

            def PV(u, h, pair, e):
                n, i = u * H + h, u % NB
                pe.wait_ge(s_exp, 2 * n + pair + 3)
                for j in range(2):
                    kt = 2 * pair + j
                    q0 = kt * P if hs.causal else 0
                    c = h * V if KH > 1 else 0
                    m = pe.matmul(ps_v[e * VP:(e + 1) * VP, q0:], vS[i][:, kt, c:c + VP], prob[pair][:, j, q0:],
                                  start=(kt == 0), stop=True, skip_group_check=True)
                m.then_inc(s_pv, 1)

            def turn_group(g):
                pe.wait_ge(s_yc, g + 1)
                pe.wait_ge(s_norm, g + 1)
                for q in range(TB):
                    m = pe.transpose(ps_y[:, q, :], yT[:, q * P:(q + 1) * P], ident[:])
                m.then_inc(s_yt, 1)

            def group(u, g, last=False):
                a, b, h = u + 1 < U, u >= 0, g * G
                for e in range(G):
                    ends = last and e == G - 1
                    un, hn = (u, h + e + 1) if not ends or h < HH else (u + 1, 0)
                    ahead = b and un < U
                    if ahead:
                        if ends:
                            pe.wait_ge(s_ml, 16 * (2 * un + hn // HH + 1))
                        QK(un, hn, 0)
                    if a:
                        A(u + 1, h + e, 0)
                    if b:
                        if e == 0 and not begins(u, g):
                            turn_group(u * UG + g - 1)
                        PV(u, h + e, 0, e)
                    if ahead:
                        QK(un, hn, 1)
                    if a:
                        A(u + 1, h + e, 1)
                    if b:
                        PV(u, h + e, 1, e)

            def turn_max(n, reduced):
                pe.wait_ge(s_mh, n + 1)
                pe.wait_ge(s_red, reduced)
                for qt in range(TB):
                    m = pe.transpose(ps_m[:, qt, :], mh[n % 2][:, qt].rearrange("p a h -> p (a h)"), identb[:])
                m.then_inc(s_mt, 1)

            pe.sem_inc(s_pv, 2)
            pe.sem_inc(s_yt, 1)
            pe.wait_ge(s_one, 2 * NB)
            if hs.causal:
                pe.wait_ge(s_mask, 4)
            for u in range(-1, U):
                if u == 0:
                    pe.wait_ge(s_ml, 16)
                    QK(0, 0, 0)
                    QK(0, 0, 1)
                for hh in range(2):
                    def between():
                        n = 2 * u + 1 + hh
                        if 0 <= n < 2 * U:
                            turn_max(n, TB * HH * (n + 1) + 2 + (TB * G if u + 1 < U else 0))
                            turned[0] = n + 1

                    unit_groups(pe, hh, lambda g, last=False: group(u, g, last), between)
            turn_group(U * UG - 1)

        @block.scalar
        def _(act):
            def exp(u, h, pair):
                m2 = (u * H + h) * 2 + pair
                act.wait_ge(s_qk, m2 + 1)
                act.wait_ge(s_pv, m2 + 1)
                if hs.causal:
                    for j in range(2):
                        q0 = (2 * pair + j) * P
                        last = act.activation(prob[pair][:, j, q0:], ps_s[pair][:, j, q0:], ACT.Exp, scale=hs.scale)
                else:
                    last = act.activation(prob[pair][:], ps_s[pair][:], ACT.Exp, scale=hs.scale)
                last.then_inc(s_exp, 1)

            def copy_group(g):
                act.wait_ge(s_pv, 2 * (g + 1) * G + 2)
                act.wait_ge(s_yt, g + 1)
                act.copy(yT[:], ps_v[:]).then_inc(s_yc, 1)

            def group(u, g):
                for e in range(G):
                    exp(u, g * G + e, 0)
                    if e == 0 and not begins(u, g):
                        copy_group(u * UG + g - 1)
                    exp(u, g * G + e, 1)

            def copy_max(n):
                act.wait_ge(s_mt, n + 1)
                if n >= 2:
                    act.wait_ge(s_ms, 16 * (n - 1))
                act.copy(mrow[n % 2][:], ps_m.rearrange("p q t -> p (q t)")).then_inc(s_mc, 1)

            act.sem_inc(s_exp, 2)
            for u in range(-1, U):
                for hh in range(2):
                    def between():
                        n = 2 * u + 1 + hh
                        if 0 <= n < 2 * U:
                            copy_max(n)

                    if u >= 0:
                        unit_groups(act, hh, lambda g, last=False: group(u, g), between)
                    else:
                        between()
            copy_group(U * UG - 1)

        @block.vector
        def _(dve):
            dve.sem_inc(s_red, 2)
            dve.sem_inc(s_norm, 1)

            def red(u, h, half):
                for j in range(2):
                    qt = 2 * half + j
                    n = (qt + 1) * P if hs.causal else L
                    dve.wait_ge(s_a, (u * H + h) * TB + qt + 1)
                    dve.tensor_reduce(mx[u % 2][:, qt, bass.ds(h, 1)], ps_a[:, j, 0:n], AX.X, ALU.max,
                                      negate=True).then_inc(s_red, 1)

            def norm(u, ug):
                g = u * UG + ug
                dve.wait_ge(s_yt, g + 2)
                dve.reciprocal(inv[:], heads_y[:, :, :, hd]).then_inc(s_inv, 1)
                dve.wait_ge(s_inv, (2 if add else 1) * g + 1)
                cols = bass.ds(ug * G * hd + (u % UB) * H * hd, G * hd)
                out = dst[:, u // UB * TB:(u // UB + 1) * TB, cols].rearrange("p q (g d) -> p q g d", g=G)
                f = inv[:].rearrange("p q (g o) -> p q g o", o=1).broadcast_to([P, TB, G, hd])
                if add:
                    dve.tensor_tensor(y[:], heads_y[:, :, :, 0:hd], f, ALU.mult).then_inc(s_inv, 1)
                    dve.wait_ge(s_inv, 2 * g + 2)
                    dve.tensor_tensor(out, out, y[:], ALU.add).then_inc(s_norm, 1)
                else:
                    dve.tensor_tensor(out, heads_y[:, :, :, 0:hd], f, ALU.mult).then_inc(s_norm, 1)

            def group(u, g):
                for e in range(G):
                    if u + 1 < U:
                        red(u + 1, g * G + e, 0)
                    if u >= 0 and e == 0:
                        if not isinstance(g, int) or g > 0:
                            norm(u, g - 1)
                        elif u:
                            norm(u - 1, UG - 1)
                    if u + 1 < U:
                        red(u + 1, g * G + e, 1)

            def split_max(n):
                u, hh = n // 2, n % 2
                m = mx[u % 2][:, :, hh * HH:(hh + 1) * HH]
                dve.wait_ge(s_red, TB * HH * (n + 1) + 2)
                if n >= 2:
                    dve.wait_ge(s_mt, n - 1)
                dve.tensor_copy(mh[n % 2][:, :, 0, :], m).then_inc(s_sp, 1)
                dve.wait_ge(s_sp, n + 1)
                dve.tensor_tensor(mh[n % 2][:, :, 1, :], m, mh[n % 2][:, :, 0, :], ALU.subtract).then_inc(s_mh, 1)

            for u in range(-1, U):
                for hh in range(2):
                    unit_groups(dve, hh, lambda g, last=False: group(u, g), lambda: None)
                    if u + 1 < U:
                        split_max(2 * u + 2 + hh)
            norm(U - 1, UG - 1)


def rope_tables(chip, name, pos, freq, cosT, sinT):
    nc, ident = chip.nc, chip.ident
    PI = float(np.pi)
    C1 = 6.28125
    C2 = 2 * PI - C1
    with ExitStack() as st:
        def sb(n, shape, dt=F32):
            return chip.sb(f"{name}_{n}", shape, dt, st)

        def sem(n):
            return chip.sem(f"{name}_{n}")

        A = pos.shape[2]
        prow, posT, fr = sb("pos", [P, NT, A]), sb("posT", [A, B, L]), sb("freq", [A, P])
        norm = Norm(chip, name + "_norm", st)
        ang, turns = sb("angle", [P, B, L]), sb("turns", [P, B, L])
        ps = chip.ps(name + "_ps", [P, B, L], F32, st)
        s_ld, s_t, s_pc, s_a, s_ac, s_c, s_r = (sem(n) for n in ("ld", "t", "pos", "angle", "ac", "chain", "reduced"))
        s_sin = sem("sin")
        block = st.enter_context(nc.Block())

        @block.sync
        def _(sp):
            sp.dma_start(prow[:], pos.rearrange("b (t p) a -> p (b t) a", p=P)).then_inc(s_ld, 16)
            sp.dma_start(fr[:], freq).then_inc(s_ld, 16)

        @block.tensor
        def _(pe):
            pe.wait_ge(s_ld, 32)
            for t in range(NT):
                m = pe.transpose(ps[0:A, t // TB, t % TB * P:(t % TB + 1) * P], prow[:, t, :], ident[:])
            m.then_inc(s_t, 1)
            pe.wait_ge(s_pc, 1)
            for b in range(B):
                m = pe.matmul(ps[:, b, :], fr[:], posT[:, b, :], start=True, stop=True)
            m.then_inc(s_a, 1)

        @block.scalar
        def _(act):
            act.wait_ge(s_t, 1)
            act.copy(posT[:], ps[0:A]).then_inc(s_pc, 1)
            norm.root(act)
            norm.odd_rows(act)
            for i, out in enumerate((sinT, cosT)):
                act.wait_ge(s_r, i + 1)
                act.activation(out[:], ang[:], ACT.Sin).then_inc(s_sin, 1)

        @block.vector
        def _(dve):
            ch = Chain(dve, s_c)
            norm.moments(dve)
            dve.wait_ge(s_a, 1)
            for i in range(2):
                if i:
                    norm.inverse(dve)
                    norm.even_rows(dve)
                    dve.wait_ge(s_sin, 1)
                ch.step(dve.tensor_scalar(ang[:], ps[:], i * PI / 2, None, ALU.add))
                ch.step(dve.tensor_scalar(turns[:], ang[:], 1 / (2 * PI), MAGIC, ALU.mult, ALU.add))
                ch.step(dve.tensor_scalar(turns[:], turns[:], -MAGIC, None, ALU.add))
                ch.step(dve.scalar_tensor_tensor(out=ang[:], in0=turns[:], scalar=-C1, in1=ang[:],
                                                 op0=ALU.mult, op1=ALU.add))
                ch.step(dve.scalar_tensor_tensor(out=ang[:], in0=turns[:], scalar=-C2, in1=ang[:],
                                                 op0=ALU.mult, op1=ALU.add))
                dve.tensor_scalar(ang[:], ang[:], 3.1415925, -3.1415925, ALU.min, ALU.max).then_inc(s_r, 1)


def stage_attention(chip, name, hs, pos, freq, wq, wkv, wout, bout):
    nc, X, XN, ctxT, ident = chip.nc, chip.X, chip.XN, chip.ctxT, chip.ident
    V = hs.hd + 1
    NH = D // hs.hd
    with ExitStack() as st:
        def sb(n, shape, dt=F32, c=st):
            return chip.sb(f"{name}_{n}", shape, dt, c)

        def sem(n):
            return chip.sem(f"{name}_{n}")

        cosT, sinT = sb("cos", [P, B, L]), sb("sin", [P, B, L])
        rope_tables(chip, name + "_rope", pos, freq, cosT, sinT)
        xnT = sb("xnT", [P, KD, B * L])
        transpose_norm(chip, name + "_xnT", xnT)
        W = {"q": [sb(f"wq{i}", [P, KD, D]) for i in range(2)], "k": [sb(f"wk{i}", [P, KC, D]) for i in range(2)]}
        wv = sb("wv", [P, KC, D])
        ra = [sb(f"ra{i}", [P, L]) for i in range(2)]
        rb = [sb(f"rb{i}", [P, L]) for i in range(2)]
        parts = [sb(f"parts{i}", [P, 3, L], BF16) for i in range(2)]
        vrow = [sb(f"vrow{i}", [P, NH, V]) for i in range(2)]
        ps = chip.ps(name + "_ps", [P, 2, 2, 512], F32, st)
        ps_v = chip.ps(name + "_pv", [P, 2, 512], F32, st)
        s_w, s_sw, s_p, s_t1, s_t2, s_ro, s_p1, s_r1, s_p2, s_p3 = (sem(n) for n in (
            "w", "swapped", "product", "cosine", "sine", "turned", "part1", "rest1", "part2", "part3"))
        s_st = [sem(f"stored{i}") for i in range(2)]
        s_one, s_pv, s_vc = sem("ones"), sem("v"), sem("v_copied")
        s_vs = [sem(f"v_stored{i}") for i in range(2)]
        ITEMS = [(w, b, g) for b in range(B) for g in range(KD) for w in "qk"]
        block = st.enter_context(nc.Block())

        @block.sync
        def _(sp):
            sp.dma_start(W["q"][0][:], wq.rearrange("(k p) n -> p k n", p=P)).then_inc(s_w, 16)
            sp.dma_start(W["k"][0][:], wkv[:, 0:D].rearrange("(k p) n -> p k n", p=P)).then_inc(s_w, 16)
            sp.dma_start(wv[:], wkv[:, D:2 * D].rearrange("(k p) n -> p k n", p=P)).then_inc(s_w, 16)
            UB = hs.U // B
            for n, (w, b, g) in enumerate(ITEMS):
                sp.wait_ge(s_p3, n + 1)
                u, r = b * UB + g * UB // KD, g % (KD // UB) * P
                sp.dma_start((hs.q if w == "q" else hs.k)[u, :, r:r + P, :].rearrange("a p t -> p a t"),
                             parts[n % 2][:]).then_inc(s_st[n % 2], 16)
                if n % 2:
                    t = n // 2
                    sp.wait_ge(s_vc, t + 1)
                    for h in range(UB):
                        sp.dma_start(hs.v[t // TB * UB + h, :, t % TB, :],
                                     vrow[t % 2][:, h * hs.H:(h + 1) * hs.H, :].rearrange("p h d -> p (h d)")
                                     ).then_inc(s_vs[t % 2], 16)
            for i in range(2):
                sp.wait_ge(s_st[i], 16 * len(ITEMS) // 2)
                sp.wait_ge(s_vs[i], 16 * UB * NT // 2)

        @block.tensor
        def _(pe):
            pe.wait_ge(s_w, 48)
            pe.wait_ge(s_sw, 4)
            for n, (w, b, g) in enumerate(ITEMS):
                src, K = (xnT, KD) if w == "q" else (ctxT, KC)
                if n >= 2:
                    pe.wait_ge(s_t1, n - 1)
                    pe.wait_ge(s_t2, n - 1)
                for i in range(2):
                    for k in range(K):
                        m = pe.matmul(ps[:, n % 2, i, :], W[w][i][:, k, g * P:(g + 1) * P],
                                      src[:, k, b * L:(b + 1) * L], start=(k == 0), stop=(k == K - 1))
                m.then_inc(s_p, 1)
                if n % 2:
                    t = n // 2
                    if t >= 2:
                        pe.wait_ge(s_vc, t - 1)
                    for k in range(KC):
                        m = pe.matmul(ps_v[:, t % 2, :], ctxT[:, k, t * P:(t + 1) * P], wv[:, k, :],
                                      start=(k == 0), stop=(k == KC - 1))
                    m.then_inc(s_pv, 1)

        @block.vector
        def _(dve):
            dve.wait_ge(s_w, 48)
            for w in "qk":
                a, s = (x[:].rearrange("p k (n two) -> p k n two", two=2) for x in W[w])
                dve.tensor_scalar(s[:, :, :, 0], a[:, :, :, 1], -1.0, None, ALU.mult).then_inc(s_sw, 1)
                dve.tensor_copy(s[:, :, :, 1], a[:, :, :, 0]).then_inc(s_sw, 1)

            def last_part(n):
                dve.wait_ge(s_p2, n + 1)
                dve.tensor_tensor(parts[n % 2][:, 2, :], ra[n % 2][:], parts[n % 2][:, 1, :],
                                  ALU.subtract).then_inc(s_p3, 1)

            for n, (w, b, g) in enumerate(ITEMS):
                i = n % 2
                dve.wait_ge(s_p, n + 1)
                if n >= 2:
                    dve.wait_ge(s_p3, n - 1)
                    dve.wait_ge(s_r1, n - 1)
                dve.tensor_tensor(ra[i][:], ps[:, i, 0, :], cosT[:, b, :], ALU.mult).then_inc(s_t1, 1)
                dve.tensor_tensor(rb[i][:], ps[:, i, 1, :], sinT[:, b, :], ALU.mult).then_inc(s_t2, 1)
                if n:
                    last_part(n - 1)
            last_part(len(ITEMS) - 1)

        @block.gpsimd
        def _(pool):
            for i in range(2):
                pool.memset(vrow[i][:, :, hs.hd:V], 1.0).then_inc(s_one, 1)
            for n in range(len(ITEMS)):
                i = n % 2
                pool.wait_ge(s_t1, n + 1)
                pool.wait_ge(s_t2, n + 1)
                pool.tensor_tensor(rb[i][:], ra[i][:], rb[i][:], ALU.add).then_inc(s_ro, 1)
                pool.wait_ge(s_p1, n + 1)
                pool.tensor_tensor(ra[i][:], rb[i][:], parts[i][:, 0, :], ALU.subtract).then_inc(s_r1, 1)

        @block.scalar
        def _(act):
            act.wait_ge(s_one, 2)
            for n in range(len(ITEMS)):
                i = n % 2
                act.wait_ge(s_ro, n + 1)
                if n >= 2:
                    act.wait_ge(s_st[i], 16 * (n // 2))
                act.copy(parts[i][:, 0, :], rb[i][:]).then_inc(s_p1, 1)
                act.wait_ge(s_r1, n + 1)
                act.copy(parts[i][:, 1, :], ra[i][:]).then_inc(s_p2, 1)
                if n % 2:
                    t = n // 2
                    act.wait_ge(s_pv, t + 1)
                    if t >= 2:
                        act.wait_ge(s_vs[t % 2], 16 * (hs.U // B) * (t // 2))
                    act.copy(vrow[t % 2][:, :, 0:hs.hd],
                             ps_v[:, t % 2, :].rearrange("p (h d) -> p h d", d=hs.hd)).then_inc(s_vc, 1)

    attention_core(chip, name + "_core", hs, add=False)
    out_projection(chip, name + "_out", wout, bout)


def out_projection(chip, name, wout, bout):
    nc, X = chip.nc, chip.X
    with ExitStack() as st:
        aT = chip.sb(name + "_aT", [P, KD, B * L], F32, st)
        transpose_norm(chip, name + "_aT", aT)
        w, bias = chip.sb(name + "_w", [P, KD, D], F32, st), chip.sb(name + "_bias", [P, D], F32, st)
        ps = chip.ps(name + "_ps", [P, 4, 512], F32, st)
        s_w, s_o, s_b, s_f = (chip.sem(f"{name}_{n}") for n in ("w", "product", "biased", "folded"))
        block = st.enter_context(nc.Block())

        @block.sync
        def _(sp):
            sp.dma_start(w[:], wout.rearrange("(k p) n -> p k n", p=P)).then_inc(s_w, 16)
            sp.dma_start(bias[:], bout.rearrange("(o n) -> o n", o=1).broadcast_to([P, D])).then_inc(s_w, 16)

        @block.tensor
        def _(pe):
            pe.wait_ge(s_w, 32)
            for t in range(NT):
                if t >= 4:
                    pe.wait_ge(s_f, t - 3)
                for k in range(KD):
                    m = pe.matmul(ps[:, t % 4, :], aT[:, k, t * P:(t + 1) * P], w[:, k, :],
                                  start=(k == 0), stop=(k == KD - 1))
                m.then_inc(s_o, 1)

        @block.gpsimd
        def _(pool):
            pool.wait_ge(s_w, 32)
            for t in range(NT):
                pool.tensor_tensor(X[:, t, :], X[:, t, :], bias[:], ALU.add).then_inc(s_b, 1)

        @block.vector
        def _(dve):
            for t in range(NT):
                dve.wait_ge(s_b, t + 1)
                dve.wait_ge(s_o, t + 1)
                dve.tensor_tensor(X[:, t, :], X[:, t, :], ps[:, t % 4, :], ALU.add).then_inc(s_f, 1)


def stage_routed_attention(chip, name, hs, w_gate, w_qkv):
    nc, X, XN, ident = chip.nc, chip.X, chip.XN, chip.ident
    NH, hd = w_gate.shape[0], hs.hd
    V = hd + 1
    with ExitStack() as st:
        def sb(n, shape, dt=F32):
            return chip.sb(f"{name}_{n}", shape, dt, st)

        def sem(n):
            return chip.sem(f"{name}_{n}")

        wT, gT = sb("wT", [P, KD, 3 * D]), sb("gT", [P, KD, NH])
        with ExitStack() as s2:
            norm = Norm(chip, name + "_norm", s2)
            wr = chip.sb(name + "_w_rows", [P, 3 * KD, D], F32, s2)
            gr = chip.sb(name + "_g_rows", [NH, D], F32, s2)
            ps = chip.ps(name + "_wps", [P, 4, 512], F32, s2)
            s_w, s_t, s_c = sem("w"), sem("wt"), sem("wc")
            block = s2.enter_context(nc.Block())

            @block.sync
            def _(sp):
                sp.dma_start(wr[:], w_qkv.rearrange("(r p) k -> p r k", p=P)).then_inc(s_w, 16)
                sp.dma_start(gr[:], w_gate).then_inc(s_w, 16)

            @block.tensor
            def _(pe):
                pe.wait_ge(s_w, 32)
                for r in range(3 * KD):
                    if r >= 4:
                        pe.wait_ge(s_c, r - 3)
                    for k in range(KD):
                        m = pe.transpose(ps[:, r % 4, k * P:(k + 1) * P], wr[:, r, k * P:(k + 1) * P], ident[:])
                    m.then_inc(s_t, 1)
                pe.wait_ge(s_c, 3 * KD - 3)
                for k in range(KD):
                    m = pe.transpose(ps[:, 0, k * NH:(k + 1) * NH], gr[:, k * P:(k + 1) * P], ident[0:NH, 0:NH])
                m.then_inc(s_t, 1)

            @block.vector
            def _(dve):
                norm.moments(dve)
                norm.inverse(dve)
                norm.even_rows(dve)

            @block.scalar
            def _(act):
                norm.root(act)
                norm.odd_rows(act)
                for r in range(3 * KD):
                    act.wait_ge(s_t, r + 1)
                    act.copy(wT[:, :, r * P:(r + 1) * P],
                             ps[:, r % 4, :].rearrange("p (k n) -> p k n", k=KD)).then_inc(s_c, 1)
                act.wait_ge(s_t, 3 * KD + 1)
                act.copy(gT[:].rearrange("p k n -> p (k n)"), ps[:, 0, 0:KD * NH]).then_inc(s_c, 1)

        xnT = sb("xnT", [P, KD, B * L])
        transpose_norm(chip, name + "_xnT", xnT)

        gate = sb("gate", [P, NT, NH])
        top, tot, inv = sb("top", [P, NT]), sb("tot", [P, NT]), sb("inv", [P, NT])
        pick, pickv = sb("pick", [P, NT, NH]), sb("pick_value", [P, NT, NH])
        rank, best = sb("rank", [P, 1, NH]), sb("best", [P, NT])
        sel = [sb(f"sel{i}", [P, 2, NH, hd]) for i in range(2)]
        kv = [sb(f"kv{i}", [P, 2, V]) for i in range(2)]
        rest = [sb(f"rest{i}", [P, L]) for i in range(2)]
        parts = [sb(f"parts{i}", [P, 3, L], BF16) for i in range(2)]
        ps_q, ps_kv = chip.ps(name + "_pq", [P, 2, 512], F32, st), chip.ps(name + "_pkv", [P, 2, 2, 512], F32, st)
        ps_g, ps_k = chip.ps(name + "_pg", [P, NT, NH], F32, st), chip.ps(name + "_pk", [hd, 512], F32, st)
        s_g, s_ch, s_top, s_e = sem("g"), sem("chain"), sem("gtop"), sem("gexp")
        s_rank, s_kv, s_sel, s_kvr, s_kt = (sem(n) for n in ("rank", "kv", "selected", "kv_reduced", "key_turned"))
        s_p, s_p1, s_r1, s_p2, s_p3 = (sem(n) for n in (
            "product", "part1", "rest1", "part2", "part3"))
        s_st, s_vs = ([sem(f"{n}{i}") for i in range(2)] for n in ("stored", "v_stored"))
        ITEMS = [(b, g) for b in range(B) for g in range(KD + 1)]
        block = st.enter_context(nc.Block())

        @block.tensor
        def _(pe):
            for t in range(NT):
                for k in range(KD):
                    m = pe.matmul(ps_g[:, t, :], xnT[:, k, t * P:(t + 1) * P], gT[:, k, :],
                                  start=(t == 0 and k == 0), stop=True, skip_group_check=True)
            m.then_inc(s_g, 1)
            for b in range(B):
                for g in range(KD + 1):
                    n = b * (KD + 1) + g
                    if g < KD:
                        if n >= 2:
                            pe.wait_ge(s_r1, n - 1)
                        for k in range(KD):
                            m = pe.matmul(ps_q[:, n % 2, :], wT[:, k, g * P:(g + 1) * P],
                                          xnT[:, k, b * L:(b + 1) * L], start=(k == 0), stop=(k == KD - 1))
                        m.then_inc(s_p, 1)
                        t = b * TB + g
                        if t >= 2:
                            pe.wait_ge(s_sel, 2 * (t - 1))
                        for i in range(2):
                            for k in range(KD):
                                m = pe.matmul(ps_kv[:, t % 2, i, :], xnT[:, k, t * P:(t + 1) * P],
                                              wT[:, k, (i + 1) * D:(i + 2) * D], start=(k == 0), stop=(k == KD - 1))
                        m.then_inc(s_kv, 1)
                        if g:
                            turn = t - 1
                            pe.wait_ge(s_kvr, turn + 1)
                            if g == 1 and b:
                                pe.wait_ge(s_r1, n - 1)
                            pe.transpose(ps_k[:, turn % TB * P:(turn % TB + 1) * P], kv[turn % 2][:, 0, 0:hd],
                                         ident[:]).then_inc(s_kt, 1)
                    else:
                        turn = b * TB + TB - 1
                        pe.wait_ge(s_kvr, turn + 1)
                        pe.transpose(ps_k[:, (TB - 1) * P:], kv[turn % 2][:, 0, 0:hd], ident[:]).then_inc(s_kt, 1)

        @block.gpsimd
        def _(pool):
            pool.iota(rank[:, 0, :], [[-1, NH]], base=NH, channel_multiplier=0,
                      allow_small_or_imprecise_dtypes=True).then_inc(s_rank, 1)
            for i in range(2):
                pool.memset(kv[i][:, 1, hd:V], 1.0).then_inc(s_rank, 1)

        @block.vector
        def _(dve):
            ch = Chain(dve, s_ch)
            wide = [P, NT, NH]

            def over(x):
                return x[:].rearrange("p (t o) -> p t o", o=1).broadcast_to(wide)

            dve.wait_ge(s_g, 1)
            dve.wait_ge(s_rank, 3)
            ch.step(dve.tensor_reduce(top[:], ps_g[:], AX.X, ALU.max))
            dve.tensor_tensor(gate[:], ps_g[:], over(top), ALU.subtract).then_inc(s_top, 1)
            dve.wait_ge(s_e, 1)
            ch.step(dve.tensor_reduce(tot[:], gate[:], AX.X, ALU.add))
            ch.step(dve.reciprocal(inv[:], tot[:]))
            ch.step(dve.tensor_tensor(gate[:], gate[:], over(inv), ALU.mult))
            ch.step(dve.tensor_reduce(top[:], gate[:], AX.X, ALU.max))
            ch.step(dve.tensor_tensor(pick[:], gate[:], over(top), ALU.is_equal))
            rk = rank[:].broadcast_to(wide)
            ch.step(dve.tensor_tensor(pickv[:], pick[:], rk, ALU.mult))
            ch.step(dve.tensor_reduce(best[:], pickv[:], AX.X, ALU.max))
            ch.step(dve.tensor_tensor(pick[:], rk, over(best), ALU.is_equal))
            ch.step(dve.tensor_tensor(pickv[:], pick[:], over(top), ALU.mult))

            def select(t):
                i = t % 2
                dve.wait_ge(s_kv, t + 1)
                if t >= 2:
                    dve.wait_ge(s_kvr, t - 1)
                for j, p in enumerate((pick, pickv)):
                    w = p[:, t, :].rearrange("p (h o) -> p h o", o=1).broadcast_to([P, NH, hd])
                    dve.tensor_tensor(sel[i][:, j], ps_kv[:, i, j, :].rearrange("p (h d) -> p h d", h=NH), w,
                                      ALU.mult).then_inc(s_sel, 1)
                dve.wait_ge(s_sel, 2 * t + 2)
                if t >= 2:
                    dve.wait_ge(s_kt, t - 1)
                    dve.wait_ge(s_vs[i], 16 * (t // 2))
                dve.tensor_reduce(kv[i][:, :, 0:hd], sel[i][:].rearrange("p j h d -> p j d h"), AX.X,
                                  ALU.add).then_inc(s_kvr, 1)

            def split(n):
                i, (b, g) = n % 2, ITEMS[n]
                src, rows = (ps_q[:, i, :], P) if g < KD else (ps_k[:], hd)
                dve.wait_ge(s_p1, n + 1)
                if n >= 2:
                    dve.wait_ge(s_p3, n - 1)
                dve.tensor_tensor(rest[i][0:rows], src, parts[i][0:rows, 0, :], ALU.subtract).then_inc(s_r1, 1)
                dve.wait_ge(s_p2, n + 1)
                dve.tensor_tensor(parts[i][0:rows, 2, :], rest[i][0:rows], parts[i][0:rows, 1, :],
                                  ALU.subtract).then_inc(s_p3, 1)

            for n, (b, g) in enumerate(ITEMS):
                if g < KD:
                    select(b * TB + g)
                split(n)

        @block.scalar
        def _(act):
            act.wait_ge(s_top, 1)
            act.activation(gate[:], gate[:], ACT.Exp).then_inc(s_e, 1)
            for n, (b, g) in enumerate(ITEMS):
                i = n % 2
                if g < KD:
                    src, rows = ps_q[:, i, :], P
                    act.wait_ge(s_p, b * KD + g + 1)
                else:
                    src, rows = ps_k[:], hd
                    act.wait_ge(s_kt, (b + 1) * TB)
                if n >= 2:
                    act.wait_ge(s_st[i], 16 * (n // 2))
                act.copy(parts[i][0:rows, 0, :], src).then_inc(s_p1, 1)
                act.wait_ge(s_r1, n + 1)
                act.copy(parts[i][0:rows, 1, :], rest[i][0:rows]).then_inc(s_p2, 1)

        @block.sync
        def _(sp):
            for n, (b, g) in enumerate(ITEMS):
                i = n % 2
                if g < KD:
                    t = b * TB + g
                    sp.wait_ge(s_kvr, t + 1)
                    sp.dma_start(hs.v[b, :, g, :], kv[t % 2][:, 1, :]).then_inc(s_vs[t % 2], 16)
                    dst, rows = hs.q[b, :, g * P:(g + 1) * P, :], P
                else:
                    dst, rows = hs.k[b], hd
                sp.wait_ge(s_p3, n + 1)
                sp.dma_start(dst.rearrange("a p t -> p a t"), parts[i][0:rows]).then_inc(s_st[i], 16)
            for i in range(2):
                sp.wait_ge(s_st[i], 16 * len(ITEMS) // 2)
                sp.wait_ge(s_vs[i], 16 * NT // 2)

    attention_core(chip, name + "_core", hs, add=True)


def ternary_weights(chip, name, mats, wT, wscale, tanh_rule):
    nc = chip.nc
    STEPS = 10 if tanh_rule else 3
    COUNT = float(mats[0].shape[0] * mats[0].shape[1])
    with ExitStack() as st:
        def sb(n, shape, dt=F32):
            return chip.sb(f"{name}_{n}", shape, dt, st)

        def sem(n):
            return chip.sem(f"{name}_{n}")

        SLOTS = 6
        W = sb("w", [P, SLOTS, 2048])
        norm = Norm(chip, name + "_norm", st)
        neg = [sb(f"neg{i}", [P, 2048], BF16) for i in range(2)]
        tern = [sb(f"tern{i}", [P, 4, 512], BF16) for i in range(2)]
        part, ones = sb("part", [P, 3, 4]), sb("ones", [P, P])
        psum1, s, th = sb("sum1", [P, 3]), sb("s", [P, 3]), sb("th", [P, 3, 2])
        tmp, junk = sb("tmp", [P, 6]), sb("junk", [P, 2048], BF16)
        ps = chip.ps(name + "_ps", [P, 2, 2 * BANK], BF16, st)
        ps_s = chip.ps(name + "_sum", [P, 3, BANK], F32, st)
        s_w = [sem(f"w{i}") for i in range(SLOTS)]
        s_abs, s_one, s_p1, s_sum, s_ch = sem("abs"), sem("ones"), sem("part"), sem("sum"), sem("chain")
        s_ln, s_neg, s_tern, s_t, s_cp = sem("ln"), sem("negative"), sem("ternary"), sem("t"), sem("copied")
        block = st.enter_context(nc.Block())

        @block.sync
        def _(sp):
            for n in range(12):
                m, c, i = n // 4, n % 4, n % SLOTS
                w = mats[m]
                if n >= SLOTS:
                    sp.wait_ge(s_tern, n - SLOTS + 1)
                if m < 2:
                    sp.dma_start(W[:, i, :].rearrange("p (j k) -> p j k", j=4),
                                 w[c * 512:(c + 1) * 512, :].rearrange("(j p) k -> p j k", p=P)).then_inc(s_w[i], 16)
                else:
                    sp.dma_start(W[:, i, :], w[c * P:(c + 1) * P, :]).then_inc(s_w[i], 16)

        @block.tensor
        def _(pe):
            pe.wait_ge(s_one, 1)

            def total(m):
                pe.wait_ge(s_p1, m + 1)
                pe.matmul(ps_s[:, m, 0:1], ones[:], psum1[:, m:m + 1], start=True, stop=True).then_inc(s_sum, 1)

            total(0)
            for m in range(3):
                for c in range(4):
                    pe.wait_ge(s_tern, 4 * m + c + 1)
                    for g in range(4):
                        n = 16 * m + 4 * c + g
                        if n >= 2:
                            pe.wait_ge(s_cp, n - 1)
                        for j in range(4):
                            src = tern[c % 2][:, j, g * P:(g + 1) * P] if m < 2 else \
                                tern[c % 2][:, g, j * P:(j + 1) * P]
                            t = pe.transpose(ps[:, n % 2, j * P:(j + 1) * P], src, chip.identb[:])
                        t.then_inc(s_t, 1)
                if m < 2:
                    total(m + 1)

        @block.scalar
        def _(act):
            def total(n):
                act.wait_ge(s_w[n % SLOTS], 16 * (n // SLOTS + 1))
                if n:
                    act.wait_ge(s_abs, n)
                act.activation(junk[:], W[:, n % SLOTS, :], ACT.Abs,
                               accum_out=part[:, n // 4, n % 4:n % 4 + 1]).then_inc(s_abs, 1)

            def log(m):
                act.wait_ge(s_ch, STEPS * m + 7)
                act.activation(tmp[:, 3:4], tmp[:, 1:2], ACT.Ln).then_inc(s_ln, 1)

            for c in range(4):
                total(c)
            norm.root(act)
            if tanh_rule:
                log(0)
            for m in range(3):
                for c in range(4):
                    for g in range(4):
                        n = 16 * m + 4 * c + g
                        act.wait_ge(s_t, n + 1)
                        if m < 2:
                            dst = wT[m][:, g, c * 512:(c + 1) * 512].rearrange("p (j k) -> p j k", j=4)
                        else:
                            dst = wT[m][:, 4 * g:4 * g + 4, c * P:(c + 1) * P]
                        act.copy(dst, ps[:, n % 2, 0:512].rearrange("p (j k) -> p j k", j=4)).then_inc(s_cp, 1)
                    if m < 2:
                        total(4 * m + c + 4)
                if m == 0:
                    norm.odd_rows(act)
                if m < 2 and tanh_rule:
                    log(m + 1)

        @block.vector
        def _(dve):
            ch = Chain(dve, s_ch)
            dve.memset(ones[:], 1.0).then_inc(s_one, 1)
            norm.moments(dve)
            for m in range(3):
                a, b = th[:, m, 0:1], th[:, m, 1:2]
                one = slice(m, m + 1)
                dve.wait_ge(s_abs, 4 * m + 4)
                dve.tensor_reduce(psum1[:, one], part[:, m, :], AX.X, ALU.add).then_inc(s_p1, 1)
                dve.wait_ge(s_sum, m + 1)
                if tanh_rule:
                    ch.step(dve.tensor_scalar(s[:, one], ps_s[:, m, 0:1], 1.0 / COUNT, None, ALU.mult))
                    ch.step(dve.tensor_scalar(a, s[:, one], 1e-8, float(np.arctanh(0.5)), ALU.add, ALU.mult))
                    ch.step(dve.tensor_scalar(b, a, -1.0, None, ALU.mult))
                    ch.step(dve.tensor_scalar(tmp[:, 0:1], s[:, one], -1.0, 1.0, ALU.mult, ALU.add))
                    ch.step(dve.reciprocal(tmp[:, 2:3], tmp[:, 0:1]))
                    ch.step(dve.scalar_tensor_tensor(out=tmp[:, 0:1], in0=s[:, one], scalar=2.0,
                                                     in1=tmp[:, 2:3], op0=ALU.mult, op1=ALU.mult))
                    ch.step(dve.tensor_scalar(tmp[:, 1:2], tmp[:, 0:1], 1.0, None, ALU.add))
                    ch.step(dve.tensor_scalar(tmp[:, 2:3], tmp[:, 1:2], -1.0, 2.0 ** -24, ALU.add, ALU.max))
                    ch.step(dve.reciprocal(tmp[:, 4:5], tmp[:, 2:3]))
                    dve.wait_ge(s_ln, m + 1)
                    ch.step(dve.scalar_tensor_tensor(out=tmp[:, 5:6], in0=tmp[:, 3:4], scalar=0.5,
                                                     in1=tmp[:, 0:1], op0=ALU.mult, op1=ALU.mult))
                    dve.tensor_tensor(wscale[:, one], tmp[:, 5:6], tmp[:, 4:5], ALU.mult)
                else:
                    ch.step(dve.tensor_scalar(wscale[:, one], ps_s[:, m, 0:1], 1.0 / COUNT, 1e-5,
                                              ALU.mult, ALU.add))
                    ch.step(dve.tensor_scalar(a, wscale[:, one], 0.5, None, ALU.mult))
                    ch.step(dve.tensor_scalar(b, wscale[:, one], -0.5, None, ALU.mult))
                for c in range(4):
                    n = 4 * m + c
                    if n >= 2:
                        dve.wait_ge(s_t, 4 * (n - 1))
                    dve.tensor_scalar(neg[c % 2][:], W[:, n % SLOTS, :], b, None, ALU.is_lt).then_inc(s_neg, 1)
                    dve.wait_ge(s_neg, n + 1)
                    dve.scalar_tensor_tensor(out=tern[c % 2][:].rearrange("p j k -> p (j k)"), in0=W[:, n % SLOTS, :],
                                             scalar=a, in1=neg[c % 2][:], op0=ALU.is_gt,
                                             op1=ALU.subtract).then_inc(s_tern, 1)
                    if n == 1:
                        norm.inverse(dve)
                    if n == 4:
                        norm.even_rows(dve)


def quantised_input(chip, name, gains, wscale, xqT, gsc):
    nc, XN = chip.nc, chip.XN
    NX = len(xqT)
    with ExitStack() as st:
        def sb(n, shape, dt=F32):
            return chip.sb(f"{name}_{n}", shape, dt, st)

        def sem(n):
            return chip.sem(f"{name}_{n}")

        m, q, c = sb("max", [P, NX, NT]), sb("q", [P, NX, NT]), sb("c", [P, NX, NT])
        ss, root, rroot = sb("ss", [P, NT]), sb("root", [P, NT]), sb("rroot", [P, NT])
        xg = [sb(f"xg{i}", [P, D]) for i in range(NX)]
        r1 = [sb(f"r{i}", [P, D]) for i in range(2)]
        xq = [sb(f"xq{i}", [P, D], BF16) for i in range(2)]
        junk, eps = sb("junk", [P, D]), sb("eps", [P, 1])
        g = [sb(f"g{j}", [P, D]) for j in range(NX)] if gains else None
        ps = chip.ps(name + "_ps", [P, 4, 2 * BANK], BF16, st)
        s_g, s_eps, s_ss, s_rt, s_xg = sem("g"), sem("eps"), sem("squares"), sem("root"), sem("xg")
        s_m, s_c, s_r, s_xq, s_t, s_cp = sem("max"), sem("chain"), sem("r"), sem("xq"), sem("t"), sem("copied")
        block = st.enter_context(nc.Block())

        @block.sync
        def _(sp):
            if gains:
                for j in range(NX):
                    sp.dma_start(g[j][:], gains[j].rearrange("(o n) -> o n", o=1).broadcast_to([P, D])
                                 ).then_inc(s_g, 16)
                sp.wait_ge(s_g, 32)

        @block.gpsimd
        def _(pool):
            if gains:
                pool.wait_ge(s_g, 32)
                for t in range(NT):
                    for j in range(NX):
                        if t:
                            pool.wait_ge(s_m, (t - 1) * NX + j + 1)
                        pool.tensor_tensor(xg[j][:], XN[:, t, :], g[j][:], ALU.mult).then_inc(s_xg, 1)

        @block.scalar
        def _(act):
            if gains:
                for t in range(NT):
                    if t:
                        act.wait_ge(s_ss, t)
                    act.activation(junk[:], XN[:, t, :], ACT.Square, accum_out=ss[:, t:t + 1]).then_inc(s_ss, 1)
                act.wait_ge(s_eps, 1)
                act.wait_ge(s_ss, NT)
                act.activation(root[:], ss[:], ACT.Sqrt, scale=1.0 / D, bias=eps[:]).then_inc(s_rt, 1)
            for t in range(NT):
                for j in range(NX):
                    n = t * NX + j
                    act.wait_ge(s_t, n + 1)
                    act.copy(xqT[j][:, t], ps[:, n % 4, 0:D].rearrange("p (k t) -> p k t", k=KD)).then_inc(s_cp, 1)

        @block.tensor
        def _(pe):
            for n in range(NT * NX):
                pe.wait_ge(s_xq, n + 1)
                if n >= 4:
                    pe.wait_ge(s_cp, n - 3)
                for k in range(KD):
                    i = pe.transpose(ps[:, n % 4, k * P:(k + 1) * P], xq[n % 2][:, k * P:(k + 1) * P],
                                     chip.identb[:])
                i.then_inc(s_t, 1)

        @block.vector
        def _(dve):
            ch = Chain(dve, s_c)
            ch.did(dve.memset(gsc[:, :, NT:NT + 1], 0.0))
            if gains:
                dve.memset(eps[:], 1e-8).then_inc(s_eps, 1)
                dve.wait_ge(s_g, 32)
                for t in range(NT):
                    for j in range(NX):
                        dve.wait_ge(s_xg, t * NX + j + 1)
                        dve.tensor_reduce(m[:, j, t:t + 1], xg[j][:], AX.X, ALU.max,
                                          apply_absolute_value=True).then_inc(s_m, 1)
                dve.wait_ge(s_m, NT * NX)
                dve.wait_ge(s_rt, 1)
                ch.step(dve.reciprocal(rroot[:], root[:]))
                for j in range(NX):
                    ch.step(dve.scalar_tensor_tensor(out=c[:, j], in0=root[:], scalar=1e-4, in1=m[:, j],
                                                     op0=ALU.mult, op1=ALU.max))
                ch.step(dve.tensor_scalar(c[:], c[:], 1.0 / 127, None, ALU.mult))
                ch.step(dve.reciprocal(q[:], c[:]))
                for j in range(NX):
                    ch.step(dve.scalar_tensor_tensor(out=gsc[:, j, 0:NT], in0=c[:, j], scalar=wscale[:, j:j + 1],
                                                     in1=rroot[:], op0=ALU.mult, op1=ALU.mult))
            else:
                ch.step(dve.tensor_reduce(m[:, 0], XN[:], AX.X, ALU.max, apply_absolute_value=True))
                ch.step(dve.tensor_scalar(c[:], m[:], 1e-5, 1.0 / 127, ALU.max, ALU.mult))
                ch.step(dve.reciprocal(q[:], c[:]))
                for j in range(2):
                    ch.step(dve.tensor_scalar(gsc[:, j, 0:NT], c[:, 0], wscale[:, j:j + 1], None, ALU.mult))
            for n in range(NT * NX):
                t, j, i = n // NX, n % NX, n % 2
                if n >= 2:
                    dve.wait_ge(s_xq, n - 1)
                if gains:
                    dve.scalar_tensor_tensor(out=r1[i][:], in0=XN[:, t, :], scalar=q[:, j, t:t + 1], in1=g[j][:],
                                             op0=ALU.mult, op1=ALU.mult).then_inc(s_r, 1)
                else:
                    dve.tensor_scalar(r1[i][:], XN[:, t, :], q[:, j, t:t + 1], None, ALU.mult).then_inc(s_r, 1)
                dve.wait_ge(s_r, n + 1)
                if n >= 2:
                    dve.wait_ge(s_t, n - 1)
                dve.tensor_scalar(xq[i][:], r1[i][:], MAGIC, -MAGIC, ALU.add, ALU.add).then_inc(s_xq, 1)


def stage_bitffn(chip, name, mats, gains=None):
    nc, X, XN = chip.nc, chip.X, chip.XN
    F = mats[0].shape[0]
    NC = F // 512
    NJ = F // P
    NX = 2 if gains else 1
    with ExitStack() as st0:
        wT = [chip.sb(f"{name}_wT{m}", [P, KD, F] if m < 2 else [P, NJ, D], BF16, st0) for m in range(3)]
        wscale = chip.sb(name + "_wscale", [P, 3], F32, st0)
        ternary_weights(chip, name + "_w", mats, wT, wscale, gains is not None)
        st = st0.enter_context(ExitStack())

        def sb(n, shape, dt=F32):
            return chip.sb(f"{name}_{n}", shape, dt, st)

        def sem(n):
            return chip.sem(f"{name}_{n}")

        xqT = [sb(f"xqT{j}", [P, NT, KD, P], BF16) for j in range(NX)]
        gsc = sb("gate_up_scale", [P, 2, NT + 1])
        quantised_input(chip, name + "_x", gains, wscale, xqT, gsc)

        gsel = [sb(f"gate_up_scale{i}", [P, 2]) for i in range(2)]
        sig = [sb(f"act{i}", [P, 512]) for i in range(2)]
        h = [XN[:, i * NC:(i + 1) * NC, :].rearrange("p c n -> p (c n)") for i in range(2)]
        r1 = XN[:, 2 * NC:3 * NC, :].rearrange("p c n -> p (c n)")
        hq = [sb(f"hq{i}", [P, F], BF16) for i in range(2)]
        hqT = [sb(f"hqT{i}", [P, NJ, P], BF16) for i in range(2)]
        sm = [sb(f"small{i}", [P, 8]) for i in range(2)]
        dsc = [sb(f"down_scale{i}", [P, 1]) for i in range(2)]
        if gains:
            g3 = XN[:, 3 * NC:4 * NC, :].rearrange("p c n -> p (c n)")
            hg = [sb(f"h_gained{i}", [P, F])[:] for i in range(2)]
            eps = sb("eps", [P, 1])
        ps_g, ps_u = chip.ps(name + "_g", [P, 2, 512], F32, st), chip.ps(name + "_u", [P, 2, 512], F32, st)
        ps_h = chip.ps(name + "_hT", [P, NJ, P], BF16, st)
        ps_d = chip.ps(name + "_d", [P, 512], F32, st)

        s_g, s_u, s_sig, s_h = sem("gate"), sem("up"), sem("act"), sem("h")
        s_hg, s_ss, s_rt, s_c, s_q = sem("h_gained"), sem("squares"), sem("root"), sem("chain"), sem("quantised")
        s_ht, s_hc, s_d, s_f = sem("hT"), sem("hT_copied"), sem("down"), sem("folded")
        s_g3, s_ep, s_gs = sem("g3"), sem("eps"), sem("scales")
        block = st.enter_context(nc.Block())
        LAST = NT - 1

        @block.sync
        def _(sp):
            if gains:
                sp.dma_start(g3, gains[2].rearrange("(o n) -> o n", o=1).broadcast_to([P, F])).then_inc(s_g3, 16)
                sp.wait_ge(s_g3, 16)

        @block.tensor
        def _(pe):
            pe.sem_inc(s_ht, 2)
            pe.sem_inc(s_d, 2)

            def gate_up(t):
                for c in range(NC):
                    n = t * NC + c
                    pe.wait_ge(s_sig, n + 1)
                    for m, (bank, sem_, j) in enumerate(((ps_g, s_g, 0), (ps_u, s_u, NX - 1))):
                        if m:
                            pe.wait_ge(s_h, n + 1)
                        for k in range(KD):
                            i = pe.matmul(bank[:, c % 2, :], xqT[j][:, bass.ds(t, 1), k, :].rearrange(
                                "p o t -> p (o t)"), wT[m][:, k, c * 512:(c + 1) * 512],
                                start=(k == 0), stop=(k == KD - 1))
                        i.then_inc(sem_, 1)

            def turn_h(t, p):
                pe.wait_ge(s_q, t + 3)
                pe.wait_ge(s_hc, t + 1)
                for j in range(NJ):
                    i = pe.transpose(ps_h[:, j, :], hq[p][:, j * P:(j + 1) * P], chip.identb[:])
                i.then_inc(s_ht, 1)

            def down(t, p):
                pe.wait_ge(s_hc, t + 2)
                pe.wait_ge(s_f, t + 2)
                for j in range(NJ):
                    i = pe.matmul(ps_d[:], hqT[p][:, j, :], wT[2][:, j, :], start=(j == 0), stop=(j == NJ - 1))
                i.then_inc(s_d, 1)

            gate_up(0)
            gate_up(1)
            turn_h(0, 0)
            with pe.Fori(0, LAST // 2) as i:
                t = i * 2 + 1
                for p in range(2):
                    gate_up(t + p + 1)
                    turn_h(t + p, 1 - p)
                    down(t + p - 1, p)
            turn_h(LAST, 1)
            down(LAST - 1, 0)
            down(LAST, 1)

        @block.scalar
        def _(act):
            act.sem_inc(s_sig, 2)
            act.sem_inc(s_hc, 1)

            def gate(t, c, p):
                n = t * NC + c
                act.wait_ge(s_gs, t + 1)
                act.wait_ge(s_g, n + 1)
                act.wait_ge(s_h, n + 1)
                act.activation(sig[c % 2][:], ps_g[:, c % 2, :], ACT.Silu if gains else ACT.Sigmoid,
                               scale=gsel[p][:, 0:1]).then_inc(s_sig, 1)

            def root(t, p):
                if gains:
                    act.wait_ge(s_h, t * NC + NC + 2)
                    act.wait_ge(s_q, t + 1)
                    act.wait_ge(s_ht, t + 1)
                    act.wait_ge(s_ss, t + 1)
                    act.activation(hq[p][:], h[p], ACT.Square, accum_out=sm[p][:, 0:1]).then_inc(s_ss, 1)
                    act.wait_ge(s_ss, t + 2)
                    act.activation(sm[p][:, 1:2], sm[p][:, 0:1], ACT.Sqrt, scale=1.0 / F,
                                   bias=eps[:]).then_inc(s_rt, 1)

            def copy_h(t, p):
                act.wait_ge(s_ht, t + 3)
                act.wait_ge(s_d, t + 1)
                act.copy(hqT[p][:], ps_h[:]).then_inc(s_hc, 1)

            if gains:
                act.wait_ge(s_ep, 1)
                act.sem_inc(s_ss, 1)
            for c in range(NC):
                gate(0, c, 0)
            root(0, 0)
            for c in range(NC):
                gate(1, c, 1)
            copy_h(0, 0)
            root(1, 1)
            with act.Fori(0, LAST // 2) as i:
                t = i * 2 + 1
                for p in range(2):
                    for c in range(NC):
                        gate(t + p + 1, c, p)
                    copy_h(t + p, 1 - p)
                    root(t + p + 1, p)
            copy_h(LAST, 1)

        @block.gpsimd
        def _(pool):
            if gains:
                def gained(t, p):
                    pool.wait_ge(s_g3, 16)
                    pool.wait_ge(s_q, t + 1)
                    for c in range(NC):
                        cols = slice(c * 512, (c + 1) * 512)
                        pool.wait_ge(s_h, t * NC + c + 3)
                        pool.tensor_tensor(hg[p][:, cols], h[p][:, cols], g3[:, cols], ALU.mult).then_inc(s_hg, 1)

                with pool.Fori(0, NT // 2) as i:
                    for p in range(2):
                        gained(i * 2 + p, p)

        @block.vector
        def _(dve):
            dve.sem_inc(s_h, 2)
            dve.sem_inc(s_q, 2)
            dve.sem_inc(s_f, 2)
            if gains:
                dve.memset(eps[:], 1e-8).then_inc(s_ep, 1)
            ch = Chain(dve, s_c)
            PER = 7 if gains else 5

            def pick(t, p):
                dve.tensor_copy(gsel[p][:].rearrange("q (j o) -> q j o", o=1),
                                gsc[:, :, bass.ds(t, 1)]).then_inc(s_gs, 1)

            def chunk(t, p, c):
                n = t * NC + c
                dve.wait_ge(s_u, n + 1)
                dve.wait_ge(s_sig, n + 3)
                if c == 0:
                    dve.wait_ge(s_gs, t + 1)
                    dve.wait_ge(s_q, t + 1)
                dve.scalar_tensor_tensor(out=h[p][:, c * 512:(c + 1) * 512], in0=ps_u[:, c % 2, :],
                                         scalar=gsel[p][:, 1:2], in1=sig[c % 2][:],
                                         op0=ALU.mult, op1=ALU.mult).then_inc(s_h, 1)

            def quantise(t, p, part):
                v = sm[p]
                if part == 0:
                    ch.base, ch.n = t * PER, 0
                    dve.wait_ge(s_h, t * NC + NC + 2)
                    if gains:
                        dve.wait_ge(s_hg, t * NC + NC)
                    ch.step(dve.tensor_reduce(v[:, 2:3], hg[p] if gains else h[p], AX.X, ALU.max, apply_absolute_value=True))
                elif part == 1:
                    dve.wait_ge(s_f, t + 1)
                    if gains:
                        dve.wait_ge(s_rt, t + 1)
                        ch.step(dve.scalar_tensor_tensor(out=v[:, 3:4], in0=v[:, 1:2], scalar=1e-4,
                                                         in1=v[:, 2:3], op0=ALU.mult, op1=ALU.max))
                        ch.did(dve.tensor_scalar(v[:, 4:5], v[:, 3:4], 1.0 / 127, None, ALU.mult))
                        ch.did(dve.reciprocal(v[:, 6:7], v[:, 1:2]))
                        ch.settle()
                        ch.did(dve.reciprocal(v[:, 5:6], v[:, 4:5]))
                        ch.did(dve.scalar_tensor_tensor(out=dsc[p][:], in0=v[:, 4:5], scalar=wscale[:, 2:3],
                                                        in1=v[:, 6:7], op0=ALU.mult, op1=ALU.mult))
                    else:
                        ch.step(dve.tensor_scalar(v[:, 4:5], v[:, 2:3], 1e-5, 1.0 / 127, ALU.max, ALU.mult))
                        ch.did(dve.reciprocal(v[:, 5:6], v[:, 4:5]))
                        ch.did(dve.tensor_tensor(dsc[p][:], v[:, 4:5], wscale[:, 2:3], ALU.mult))
                    ch.settle()
                    ch.did(dve.tensor_scalar(r1, hg[p] if gains else h[p], v[:, 5:6], MAGIC, ALU.mult, ALU.add))
                    assert ch.n == PER
                else:
                    ch.settle()
                    dve.wait_ge(s_ht, t + 1)
                    dve.tensor_scalar(hq[p][:], r1, -MAGIC, 127.0, ALU.add, ALU.min).then_inc(s_q, 1)

            def fold(t, p):
                dve.wait_ge(s_d, t + 3)
                x = X[:, bass.ds(t, 1), :].rearrange("p o d -> p (o d)")
                dve.scalar_tensor_tensor(out=x, in0=ps_d[:], scalar=dsc[p][:], in1=x,
                                         op0=ALU.mult, op1=ALU.add).then_inc(s_f, 1)

            def tile(t, p, last=False, first=False):
                for c in range(NC):
                    if c < 3:
                        quantise(t, p, c)
                    if not last:
                        chunk(t + 1, 1 - p, c)
                if not first:
                    fold(t - 1, 1 - p)
                if not last:
                    pick(t + 2, p)

            pick(0, 0)
            pick(1, 1)
            for c in range(NC):
                chunk(0, 0, c)
            tile(0, 0, first=True)
            with dve.Fori(0, LAST // 2) as i:
                t = i * 2 + 1
                for p in range(2):
                    tile(t + p, 1 - p)
            tile(LAST, 1, last=True)
            fold(LAST, 1)


ONE_PASS = [[(0, 0), (0, 1), (0, 2), (1, 0), (1, 1), (2, 0)]]
TWO_PASSES = [[(0, 0), (0, 1), (0, 2)], [(1, 0), (1, 1), (2, 0)]]


def mamba_args(a, layer):
    names = ("in_proj_w", "conv_w", "conv_b", "x_proj_w", "dt_proj_w", "dt_proj_b", "A_log", "D")
    got = [a[f"{layer}_xattn_{n}"] for n in names]
    if len(got[1].shape) == 3:
        got[1] = got[1].rearrange("e o t -> e (o t)")
    return got


def build(nc, a, out):
    with ExitStack() as ctx:
        chip = Chip(nc, ctx)
        bc = nc.dram_tensor("bc_rows", (B, 32, L), F32).ap()
        chip.run(stage_start, a["x"], a["ctx_1024"])

        chip.run(stage_mamba, "m0", bc, *mamba_args(a, "L0"))

        chip.run(stage_norm, "n1")
        names = ("gate_W_packed", "gate_scales", "up_W_packed", "up_scales", "down_W_packed", "down_scales")
        chip.run(stage_ffn4, "f0", *[a["L0_ffn_" + n] for n in names])

        heads = Heads(nc, "a1", D // 32, 16, ONE_PASS, False)
        names = ("Wq", "Wkv", "Wout", "bout")
        chip.run(stage_attention, "a1", heads, a["fside_BxSx2_0"], a["freq"], *[a["L1_xattn_" + n] for n in names])

        chip.run(stage_bitffn, "f1", [a["L1_ffn_w_" + n] for n in ("gate", "up", "down")])

        chip.run(stage_norm, "n4")
        chip.run(stage_mix, "a2", *[a["L2_xattn_" + n] for n in ("Wq", "bq", "Wk", "bk")])

        chip.run(stage_bitffn, "f2", [a["L2_ffn_w" + n] for n in "123"], [a["L2_ffn_g" + n] for n in "123"])

        chip.run(stage_mamba, "m3", bc, *mamba_args(a, "L3"))

        heads = Heads(nc, "f3", D // 16, 1, TWO_PASSES, True)
        chip.run(stage_routed_attention, "f3", heads, a["L3_ffn_W_gate"], a["L3_ffn_W_qkv"])

        chip.run(stage_end, out)

_INS = ['x',
        'ctx_1024',
        'fside_BxSx2_0',
        'L0_xattn_in_proj_w',
        'L0_xattn_conv_w',
        'L0_xattn_conv_b',
        'L0_xattn_x_proj_w',
        'L0_xattn_dt_proj_w',
        'L0_xattn_dt_proj_b',
        'L0_xattn_A_log',
        'L0_xattn_D',
        'L0_ffn_gate_W_packed',
        'L0_ffn_gate_scales',
        'L0_ffn_up_W_packed',
        'L0_ffn_up_scales',
        'L0_ffn_down_W_packed',
        'L0_ffn_down_scales',
        'L1_xattn_Wq',
        'L1_xattn_Wkv',
        'L1_xattn_Wout',
        'L1_xattn_bout',
        'L1_ffn_w_gate',
        'L1_ffn_w_up',
        'L1_ffn_w_down',
        'L2_xattn_Wq',
        'L2_xattn_bq',
        'L2_xattn_Wk',
        'L2_xattn_bk',
        'L2_ffn_w1',
        'L2_ffn_g1',
        'L2_ffn_w2',
        'L2_ffn_g2',
        'L2_ffn_w3',
        'L2_ffn_g3',
        'L3_xattn_in_proj_w',
        'L3_xattn_conv_w',
        'L3_xattn_conv_b',
        'L3_xattn_x_proj_w',
        'L3_xattn_dt_proj_w',
        'L3_xattn_dt_proj_b',
        'L3_xattn_A_log',
        'L3_xattn_D',
        'L3_ffn_W_gate',
        'L3_ffn_W_qkv']


def kernel(**inputs):
    import numpy as _np
    import concourse.bacc as _bacc
    from concourse import mybir as _mybir
    from concourse.bass_utils import run_bass_kernel_spmd as _run

    nc = _bacc.Bacc("TRN2", target_bir_lowering=False, num_devices=1)
    arrays, args = {}, {}
    for name in _INS:
        a = _np.ascontiguousarray(inputs[name])
        arrays[f"in_{name}_dram"] = a
        args[name] = nc.dram_tensor(f"in_{name}_dram", a.shape, _mybir.dt.from_np(a.dtype), kind="ExternalInput").ap()
    half = 4
    freq = _np.zeros((2, 128), _np.float32)
    rates = _np.float32(10000.0) ** (-_np.arange(half, dtype=_np.float32) / _np.float32(half))
    for p in range(128):
        freq[p % 16 // 8, p] = rates[p % 8 // 2]
    arrays["in_freq_dram"] = freq
    args["freq"] = nc.dram_tensor("in_freq_dram", freq.shape, _mybir.dt.float32, kind="ExternalInput").ap()
    out = nc.dram_tensor("out_0_dram", (B, L, D), _mybir.dt.float32, kind="ExternalOutput").ap()
    build(nc, args, out)
    r = _run(nc, [arrays], core_ids=[0])
    return r.results[0]["out_0_dram"]
```
